# Optimizing a Trainium2 kernel written in Bass

```python
import numpy as np
import jax
import jax.numpy as jnp

def _softmax(x, axis=-1):
    return jax.nn.softmax(x, axis=axis)

def _gelu(x):
    return jax.nn.gelu(x, approximate=True)

def _silu(x):
    return jax.nn.silu(x)

def _sigmoid(x):
    return jax.nn.sigmoid(x)

def _layernorm(x, axis=-1, eps=1e-05):
    m = jnp.mean(x, axis=axis, keepdims=True)
    v = jnp.var(x, axis=axis, keepdims=True)
    return (x - m) / jnp.sqrt(v + eps)

def _scatter_add(tgt, idx, src, axis=0):
    return tgt.at[idx].add(src)

def _segment_sum(src, seg, n):
    return jax.ops.segment_sum(src, seg, n)
kernel_name = 'mk_adaln_d4_jaxref_r8_fc131c'

def setup_inputs(seed: int=0):
    np.random.seed(seed)
    _w = jnp.asarray

    def _L0_attn_setup():
        import jax, jax.numpy as jnp
        import numpy as np
        B, S, D = (2, 256, 128)
        H, DH = (16, 64)
        SCALE = DH ** (-0.5)
        key = jax.random.key(seed)
        ks = jax.random.split(key, 5)

        def w(k, shape):
            return jax.random.normal(k, shape, dtype=jnp.float32) * 0.02
        return {'x': jax.random.normal(ks[0], (B, S, D), dtype=jnp.float32), 'Wq': w(ks[1], (D, H * DH)), 'Wk': w(ks[2], (D, H * DH)), 'Wv': w(ks[3], (D, H * DH)), 'Wo': w(ks[4], (H * DH, D)), 'bo': jnp.zeros((D,), dtype=jnp.float32)}
    _L0_attn_in = _L0_attn_setup()

    def _L0_ffn_setup():
        import jax, jax.numpy as jnp
        import numpy as np
        NUM_EXPERTS = 8
        TOP_K = 2
        key = jax.random.key(seed)
        ks = jax.random.split(key, 4)
        B, S, D, F = (4, 256, 128, 512)
        E = NUM_EXPERTS
        x = jax.random.normal(ks[0], (B, S, D), dtype=jnp.float32)
        gate_w = jax.random.normal(ks[1], (D, E), dtype=jnp.float32) * 0.02
        gate_b = jnp.zeros((E,), dtype=jnp.float32)
        W1 = jax.random.normal(ks[2], (E, D, F), dtype=jnp.float32) * 0.02
        b1 = jnp.zeros((E, F), dtype=jnp.float32)
        W2 = jax.random.normal(ks[3], (E, F, D), dtype=jnp.float32) * 0.02
        b2 = jnp.zeros((E, D), dtype=jnp.float32)
        return {'x': x, 'gate_w': gate_w, 'gate_b': gate_b, 'W1': W1, 'b1': b1, 'W2': W2, 'b2': b2}
    _L0_ffn_in = _L0_ffn_setup()
    _L0_c = _w((lambda *s: np.random.randn(*s).astype(np.float32) * 0.05)(4, 128))
    _L0_wmod = _w((lambda *s: np.random.randn(*s).astype(np.float32) * 0.05)(128, 6 * 128) * 128 ** (-0.5))

    def _L1_attn_setup():
        import jax, jax.numpy as jnp
        import numpy as np
        import math
        D_MODEL = 128
        N_HEADS = 16
        LATENT = 32
        key = jax.random.key(seed)
        ks = jax.random.split(key, 9)
        B, T, C, L = (2, 256, D_MODEL, LATENT)
        s = 0.02
        return {'x': jax.random.normal(ks[0], (B, T, C), dtype=jnp.float32), 'Wq': jax.random.normal(ks[1], (C, C), dtype=jnp.float32) * s, 'bq': jnp.zeros((C,), dtype=jnp.float32), 'Wkd': jax.random.normal(ks[2], (C, 2 * L), dtype=jnp.float32) * s, 'bkd': jnp.zeros((2 * L,), dtype=jnp.float32), 'Wku': jax.random.normal(ks[3], (L, 2 * C), dtype=jnp.float32) * s, 'bku': jnp.zeros((2 * C,), dtype=jnp.float32), 'Wo': jax.random.normal(ks[4], (C, C), dtype=jnp.float32) * s, 'bo': jnp.zeros((C,), dtype=jnp.float32)}
    _L1_attn_in = _L1_attn_setup()

    def _L1_ffn_setup():
        import jax, jax.numpy as jnp
        import numpy as np
        E = 8
        H = 128
        F = 448
        JITTER_EPS = 0.01

        def _route(scores):
            vals, idx = jax.lax.top_k(scores, 2)
            neg_inf = -jnp.inf
            t1 = vals[:, 0:1]
            factor1 = jnp.maximum(jnp.abs(scores), t1)
            mask1 = (t1 - scores) / factor1 > 2 * JITTER_EPS
            p1 = jax.nn.softmax(jnp.where(mask1, neg_inf, scores), axis=-1)
            mult1 = jnp.take_along_axis(p1, idx[:, 0:1], axis=-1)
            t2 = vals[:, 1:2]
            factor2 = jnp.maximum(jnp.abs(scores), t2)
            mask2 = (t2 - scores) / factor2 > 2 * JITTER_EPS
            onehot0 = jax.nn.one_hot(idx[:, 0], scores.shape[-1], dtype=bool)
            scores2 = jnp.where(onehot0, neg_inf, scores)
            p2 = jax.nn.softmax(jnp.where(mask2, neg_inf, scores2), axis=-1)
            mult2 = jnp.take_along_axis(p2, idx[:, 1:2], axis=-1)
            return (jnp.concatenate([mult1, mult2], axis=-1), idx)
        key = jax.random.key(seed)
        ks = jax.random.split(key, 5)
        hidden_states = jax.random.normal(ks[0], (2, 128, H), jnp.float32)
        gate_w = jax.random.normal(ks[1], (E, H), jnp.float32) * 0.02
        w1 = jax.random.normal(ks[2], (E, F, H), jnp.float32) * 0.02
        w2 = jax.random.normal(ks[3], (E, H, F), jnp.float32) * 0.02
        w3 = jax.random.normal(ks[4], (E, F, H), jnp.float32) * 0.02
        return {'hidden_states': hidden_states, 'gate_w': gate_w, 'w1': w1, 'w2': w2, 'w3': w3}
    _L1_ffn_in = _L1_ffn_setup()
    _L1_c = _w((lambda *s: np.random.randn(*s).astype(np.float32) * 0.05)(4, 128))
    _L1_wmod = _w((lambda *s: np.random.randn(*s).astype(np.float32) * 0.05)(128, 6 * 128) * 128 ** (-0.5))

    def _L2_attn_setup():
        import jax, jax.numpy as jnp
        import numpy as np
        EPS = 1e-08

        def _gated_scan(dt, ut):
            a = 1.0 - dt
            b = dt * ut

            def combine(c1, c2):
                a1, b1 = c1
                a2, b2 = c2
                return (a2 * a1, a2 * b1 + b2)
            _, h = jax.lax.associative_scan(combine, (a, b), axis=1)
            return h
        key = jax.random.key(seed)
        ks = jax.random.split(key, 6)
        B, L, D, S = (4, 1024, 128, 64)
        sc = lambda fan_in: 1.0 / np.sqrt(fan_in)
        return {'x': jax.random.normal(ks[0], (B, L, D), dtype=jnp.float32), 'norm_w': jnp.ones((D,), dtype=jnp.float32), 'W_in': jax.random.normal(ks[1], (D, 3 * S), dtype=jnp.float32) * sc(D), 'b_in': jnp.zeros((3 * S,), dtype=jnp.float32), 'W_x': jax.random.normal(ks[2], (S, S), dtype=jnp.float32) * sc(S), 'b_x': jnp.zeros((S,), dtype=jnp.float32), 'W_dt': jax.random.normal(ks[3], (S, S), dtype=jnp.float32) * sc(S), 'b_dt': jnp.zeros((S,), dtype=jnp.float32), 'W_out': jax.random.normal(ks[4], (S, D), dtype=jnp.float32) * sc(S), 'b_out': jnp.zeros((D,), dtype=jnp.float32)}
    _L2_attn_in = _L2_attn_setup()

    def _L2_ffn_setup():
        import jax, jax.numpy as jnp
        import numpy as np
        S, B, D = (128, 2, 128)
        E, TOPK = (15, 3)
        F = 128
        FS = 256

        def _uinit(k, shape, out_dim):
            std = out_dim ** (-0.5)
            return jax.random.uniform(k, shape, jnp.float32, -std, std)
        key = jax.random.key(seed)
        ks = jax.random.split(key, 10)
        return {'x': jax.random.normal(ks[0], (S, B, D), jnp.float32), 'gate_w': jax.random.normal(ks[1], (E, D), jnp.float32) * D ** (-0.5), 'fc1_w': _uinit(ks[2], (E, 2 * F, D), 2 * F), 'fc1_b': _uinit(ks[3], (E, 2 * F), 2 * F), 'geglu_mult': jnp.ones((E, F), jnp.float32), 'fc2_w': _uinit(ks[4], (E, D, F), D), 'fc2_b': _uinit(ks[5], (E, D), D), 's_fc1_w': _uinit(ks[6], (2 * FS, D), 2 * FS), 's_fc1_b': _uinit(ks[7], (2 * FS,), 2 * FS), 's_geglu_mult': jnp.ones((FS,), jnp.float32), 's_fc2_w': _uinit(ks[8], (D, FS), D), 's_fc2_b': _uinit(ks[9], (D,), D)}
    _L2_ffn_in = _L2_ffn_setup()
    _L2_c = _w((lambda *s: np.random.randn(*s).astype(np.float32) * 0.05)(4, 128))
    _L2_wmod = _w((lambda *s: np.random.randn(*s).astype(np.float32) * 0.05)(128, 6 * 128) * 128 ** (-0.5))

    def _L3_attn_setup():
        import jax, jax.numpy as jnp
        import numpy as np
        B, T, E = (4, 256, 128)
        H, D = (16, 64)
        key = jax.random.key(seed)
        ks = jax.random.split(key, 6)
        s = 0.02
        return {'x': jax.random.normal(ks[0], (B, T, E), dtype=jnp.float32), 'Wq': jax.random.normal(ks[1], (E, H * D), dtype=jnp.float32) * s, 'Wk': jax.random.normal(ks[2], (E, H * D), dtype=jnp.float32) * s, 'Wv': jax.random.normal(ks[3], (E, H * D), dtype=jnp.float32) * s, 'Wo': jax.random.normal(ks[4], (H * D, E), dtype=jnp.float32) * s, 'bo': jax.random.normal(ks[5], (E,), dtype=jnp.float32) * s}
    _L3_attn_in = _L3_attn_setup()

    def _L3_ffn_setup():
        import jax, jax.numpy as jnp
        import numpy as np
        H = 128
        I = 64
        E = 64
        K = 2
        EPS = 1e-06
        CAP = 128

        def _rmsnorm(x, w, eps=EPS):
            v = jnp.mean(x.astype(jnp.float32) ** 2, axis=-1, keepdims=True)
            return (x.astype(jnp.float32) * jax.lax.rsqrt(v + eps)).astype(x.dtype) * w
        key = jax.random.key(seed)
        ks = jax.random.split(key, 8)
        B, S = (2, 512)
        s_h = 1.0 / np.sqrt(H)
        s_i = 1.0 / np.sqrt(I)
        return {'hidden_states': jax.random.normal(ks[0], (B, S, H), jnp.float32), 'rms_w': jnp.ones((H,), jnp.float32), 'gate_w': jax.random.normal(ks[1], (E, H), jnp.float32) * s_h, 'w13': jax.random.normal(ks[2], (E, H, 2 * I), jnp.float32) * s_h, 'w2': jax.random.normal(ks[3], (E, I, H), jnp.float32) * s_i, 'sw_gate': jax.random.normal(ks[4], (H, I), jnp.float32) * s_h, 'sw_up': jax.random.normal(ks[5], (H, I), jnp.float32) * s_h, 'sw_down': jax.random.normal(ks[6], (I, H), jnp.float32) * s_i}
    _L3_ffn_in = _L3_ffn_setup()
    _L3_c = _w((lambda *s: np.random.randn(*s).astype(np.float32) * 0.05)(4, 128))
    _L3_wmod = _w((lambda *s: np.random.randn(*s).astype(np.float32) * 0.05)(128, 6 * 128) * 128 ** (-0.5))
    _d = {'L0_attn_x': _L0_attn_in['x'], 'L0_attn_Wq': _L0_attn_in['Wq'], 'L0_attn_Wk': _L0_attn_in['Wk'], 'L0_attn_Wv': _L0_attn_in['Wv'], 'L0_attn_Wo': _L0_attn_in['Wo'], 'L0_attn_bo': _L0_attn_in['bo'], 'L0_ffn_gate_w': _L0_ffn_in['gate_w'], 'L0_ffn_gate_b': _L0_ffn_in['gate_b'], 'L0_ffn_W1': _L0_ffn_in['W1'], 'L0_ffn_b1': _L0_ffn_in['b1'], 'L0_ffn_W2': _L0_ffn_in['W2'], 'L0_ffn_b2': _L0_ffn_in['b2'], 'L0_c': _L0_c, 'L0_wmod': _L0_wmod, 'L1_attn_Wq': _L1_attn_in['Wq'], 'L1_attn_bq': _L1_attn_in['bq'], 'L1_attn_Wkd': _L1_attn_in['Wkd'], 'L1_attn_bkd': _L1_attn_in['bkd'], 'L1_attn_Wku': _L1_attn_in['Wku'], 'L1_attn_bku': _L1_attn_in['bku'], 'L1_attn_Wo': _L1_attn_in['Wo'], 'L1_attn_bo': _L1_attn_in['bo'], 'L1_ffn_gate_w': _L1_ffn_in['gate_w'], 'L1_ffn_w1': _L1_ffn_in['w1'], 'L1_ffn_w2': _L1_ffn_in['w2'], 'L1_ffn_w3': _L1_ffn_in['w3'], 'L1_c': _L1_c, 'L1_wmod': _L1_wmod, 'L2_attn_norm_w': _L2_attn_in['norm_w'], 'L2_attn_W_in': _L2_attn_in['W_in'], 'L2_attn_b_in': _L2_attn_in['b_in'], 'L2_attn_W_x': _L2_attn_in['W_x'], 'L2_attn_b_x': _L2_attn_in['b_x'], 'L2_attn_W_dt': _L2_attn_in['W_dt'], 'L2_attn_b_dt': _L2_attn_in['b_dt'], 'L2_attn_W_out': _L2_attn_in['W_out'], 'L2_attn_b_out': _L2_attn_in['b_out'], 'L2_ffn_gate_w': _L2_ffn_in['gate_w'], 'L2_ffn_fc1_w': _L2_ffn_in['fc1_w'], 'L2_ffn_fc1_b': _L2_ffn_in['fc1_b'], 'L2_ffn_geglu_mult': _L2_ffn_in['geglu_mult'], 'L2_ffn_fc2_w': _L2_ffn_in['fc2_w'], 'L2_ffn_fc2_b': _L2_ffn_in['fc2_b'], 'L2_ffn_s_fc1_w': _L2_ffn_in['s_fc1_w'], 'L2_ffn_s_fc1_b': _L2_ffn_in['s_fc1_b'], 'L2_ffn_s_geglu_mult': _L2_ffn_in['s_geglu_mult'], 'L2_ffn_s_fc2_w': _L2_ffn_in['s_fc2_w'], 'L2_ffn_s_fc2_b': _L2_ffn_in['s_fc2_b'], 'L2_c': _L2_c, 'L2_wmod': _L2_wmod, 'L3_attn_Wq': _L3_attn_in['Wq'], 'L3_attn_Wk': _L3_attn_in['Wk'], 'L3_attn_Wv': _L3_attn_in['Wv'], 'L3_attn_Wo': _L3_attn_in['Wo'], 'L3_attn_bo': _L3_attn_in['bo'], 'L3_ffn_rms_w': _L3_ffn_in['rms_w'], 'L3_ffn_gate_w': _L3_ffn_in['gate_w'], 'L3_ffn_w13': _L3_ffn_in['w13'], 'L3_ffn_w2': _L3_ffn_in['w2'], 'L3_ffn_sw_gate': _L3_ffn_in['sw_gate'], 'L3_ffn_sw_up': _L3_ffn_in['sw_up'], 'L3_ffn_sw_down': _L3_ffn_in['sw_down'], 'L3_c': _L3_c, 'L3_wmod': _L3_wmod}
    _x0 = _d['L0_attn_x']
    _d['L0_attn_x'] = jax.random.normal(jax.random.fold_in(jax.random.key(seed), 1), (4, 512, 128), dtype=_x0.dtype)
    del _x0
    return _d

def reference(L0_attn_x, L0_attn_Wq, L0_attn_Wk, L0_attn_Wv, L0_attn_Wo, L0_attn_bo, L0_ffn_gate_w, L0_ffn_gate_b, L0_ffn_W1, L0_ffn_b1, L0_ffn_W2, L0_ffn_b2, L0_c, L0_wmod, L1_attn_Wq, L1_attn_bq, L1_attn_Wkd, L1_attn_bkd, L1_attn_Wku, L1_attn_bku, L1_attn_Wo, L1_attn_bo, L1_ffn_gate_w, L1_ffn_w1, L1_ffn_w2, L1_ffn_w3, L1_c, L1_wmod, L2_attn_norm_w, L2_attn_W_in, L2_attn_b_in, L2_attn_W_x, L2_attn_b_x, L2_attn_W_dt, L2_attn_b_dt, L2_attn_W_out, L2_attn_b_out, L2_ffn_gate_w, L2_ffn_fc1_w, L2_ffn_fc1_b, L2_ffn_geglu_mult, L2_ffn_fc2_w, L2_ffn_fc2_b, L2_ffn_s_fc1_w, L2_ffn_s_fc1_b, L2_ffn_s_geglu_mult, L2_ffn_s_fc2_w, L2_ffn_s_fc2_b, L2_c, L2_wmod, L3_attn_Wq, L3_attn_Wk, L3_attn_Wv, L3_attn_Wo, L3_attn_bo, L3_ffn_rms_w, L3_ffn_gate_w, L3_ffn_w13, L3_ffn_w2, L3_ffn_sw_gate, L3_ffn_sw_up, L3_ffn_sw_down, L3_c, L3_wmod):

    def _L0_attn_ref(x, Wq, Wk, Wv, Wo, bo):
        import jax, jax.numpy as jnp
        import numpy as np
        B, S, D = (2, 256, 128)
        H, DH = (16, 64)
        SCALE = DH ** (-0.5)
        b, s, _ = x.shape
        q = (x @ Wq).reshape(b, s, H, DH)
        k = (x @ Wk).reshape(b, s, H, DH)
        v = (x @ Wv).reshape(b, s, H, DH)
        scores = jnp.einsum('bqhd,bkhd->bhqk', q, k) * SCALE
        attn = jax.nn.softmax(scores, axis=-1)
        out = jnp.einsum('bhqk,bkhd->bqhd', attn, v).reshape(b, s, H * DH)
        return out @ Wo + bo

    def _L0_ffn_ref(x, gate_w, gate_b, W1, b1, W2, b2):
        import jax, jax.numpy as jnp
        import numpy as np
        NUM_EXPERTS = 8
        TOP_K = 2
        B, S, D = x.shape
        xf = x.reshape(-1, D)
        gate_logits = xf @ gate_w + gate_b
        top_vals, top_idx = jax.lax.top_k(gate_logits, TOP_K)
        top_w = jax.nn.softmax(top_vals, axis=-1)
        dense_w = jnp.sum(jax.nn.one_hot(top_idx, NUM_EXPERTS, dtype=top_w.dtype) * top_w[..., None], axis=1)

        def body(acc, params):
            W1e, b1e, W2e, b2e, we = params
            h = jax.nn.silu(xf @ W1e + b1e)
            y = h @ W2e + b2e
            return (acc + we[:, None] * y, None)
        out0 = jnp.zeros_like(xf)
        out, _ = jax.lax.scan(body, out0, (W1, b1, W2, b2, dense_w.T))
        return out.reshape(B, S, D)

    def _L1_attn_ref(x, Wq, bq, Wkd, bkd, Wku, bku, Wo, bo):
        import jax, jax.numpy as jnp
        import numpy as np
        import math
        D_MODEL = 128
        N_HEADS = 16
        LATENT = 32
        B, T, C = x.shape
        H = N_HEADS
        D = C // H
        L = LATENT
        q = (x @ Wq + bq).reshape(B, T, H, D)
        kv_latent = jax.nn.gelu(x @ Wkd + bkd, approximate=False)
        lat = kv_latent[..., :L] + kv_latent[..., L:]
        kv = lat @ Wku + bku
        k = kv[..., :C].reshape(B, T, H, D)
        v = kv[..., C:].reshape(B, T, H, D)
        scale = 1.0 / math.sqrt(D)
        attn = jnp.einsum('bqhd,bkhd->bhqk', q, k) * scale
        causal = jnp.tril(jnp.ones((T, T), dtype=bool))
        attn = jnp.where(causal, attn, -jnp.inf)
        attn = jax.nn.softmax(attn, axis=-1)
        out = jnp.einsum('bhqk,bkhd->bqhd', attn, v).reshape(B, T, C)
        return out @ Wo + bo

    def _L1_ffn_ref(hidden_states, gate_w, w1, w2, w3):
        import jax, jax.numpy as jnp
        import numpy as np
        E = 8
        H = 128
        F = 448
        JITTER_EPS = 0.01

        def _route(scores):
            vals, idx = jax.lax.top_k(scores, 2)
            neg_inf = -jnp.inf
            t1 = vals[:, 0:1]
            factor1 = jnp.maximum(jnp.abs(scores), t1)
            mask1 = (t1 - scores) / factor1 > 2 * JITTER_EPS
            p1 = jax.nn.softmax(jnp.where(mask1, neg_inf, scores), axis=-1)
            mult1 = jnp.take_along_axis(p1, idx[:, 0:1], axis=-1)
            t2 = vals[:, 1:2]
            factor2 = jnp.maximum(jnp.abs(scores), t2)
            mask2 = (t2 - scores) / factor2 > 2 * JITTER_EPS
            onehot0 = jax.nn.one_hot(idx[:, 0], scores.shape[-1], dtype=bool)
            scores2 = jnp.where(onehot0, neg_inf, scores)
            p2 = jax.nn.softmax(jnp.where(mask2, neg_inf, scores2), axis=-1)
            mult2 = jnp.take_along_axis(p2, idx[:, 1:2], axis=-1)
            return (jnp.concatenate([mult1, mult2], axis=-1), idx)
        B, S, Hd = hidden_states.shape
        x = hidden_states.reshape(-1, Hd)
        scores = x @ gate_w.T
        mult, idx = _route(scores)
        g = (jax.nn.one_hot(idx, E, dtype=x.dtype) * mult[..., None]).sum(axis=1)
        h1 = jnp.einsum('th,efh->tef', x, w1)
        h3 = jnp.einsum('th,efh->tef', x, w3)
        inter = jax.nn.silu(h1) * h3 * g[:, :, None]
        y = jnp.einsum('tef,ehf->th', inter, w2)
        return y.reshape(B, S, Hd)

    def _L2_attn_ref(x, norm_w, W_in, b_in, W_x, b_x, W_dt, b_dt, W_out, b_out):
        import jax, jax.numpy as jnp
        import numpy as np
        EPS = 1e-08

        def _gated_scan(dt, ut):
            a = 1.0 - dt
            b = dt * ut

            def combine(c1, c2):
                a1, b1 = c1
                a2, b2 = c2
                return (a2 * a1, a2 * b1 + b2)
            _, h = jax.lax.associative_scan(combine, (a, b), axis=1)
            return h
        residual = x
        xn = x * jax.lax.rsqrt(jnp.mean(x * x, axis=-1, keepdims=True) + EPS) * norm_w
        p = jnp.einsum('bld,df->blf', xn, W_in) + b_in
        u, z, g = jnp.split(p, 3, axis=-1)
        ut = jnp.tanh(jnp.einsum('bls,st->blt', u, W_x) + b_x)
        dt = jax.nn.sigmoid(jnp.einsum('bls,st->blt', z, W_dt) + b_dt)
        h = _gated_scan(dt, ut)
        y = h * jax.nn.sigmoid(g)
        out = jnp.einsum('bls,sd->bld', y, W_out) + b_out
        return residual + out

    def _L2_ffn_ref(x, gate_w, fc1_w, fc1_b, geglu_mult, fc2_w, fc2_b, s_fc1_w, s_fc1_b, s_geglu_mult, s_fc2_w, s_fc2_b):
        import jax, jax.numpy as jnp
        import numpy as np
        S, B, D = (128, 2, 128)
        E, TOPK = (15, 3)
        F = 128
        FS = 256

        def _uinit(k, shape, out_dim):
            std = out_dim ** (-0.5)
            return jax.random.uniform(k, shape, jnp.float32, -std, std)
        s, b, d = x.shape
        xt = x.reshape(-1, d)
        T = xt.shape[0]
        logits = xt @ gate_w.T
        scores = jax.nn.softmax(logits, axis=-1)
        topk_w, topk_idx = jax.lax.top_k(scores, TOPK)
        topk_w = topk_w / (jnp.sum(topk_w, axis=-1, keepdims=True) + 1e-20)
        comb = jnp.zeros((T, E), xt.dtype).at[jnp.arange(T)[:, None], topk_idx].add(topk_w)
        h = jnp.einsum('td,efd->etf', xt, fc1_w) + fc1_b[:, None, :]
        xh, g = (h[..., :F], h[..., F:])
        a = jax.nn.gelu(g, approximate=False) * xh * geglu_mult[:, None, :]
        yexp = jnp.einsum('etf,edf->etd', a, fc2_w) + fc2_b[:, None, :]
        y = jnp.einsum('etd,te->td', yexp, comb)
        hs = xt @ s_fc1_w.T + s_fc1_b
        xs, gs = (hs[..., :FS], hs[..., FS:])
        as_ = jax.nn.gelu(gs, approximate=False) * xs * s_geglu_mult
        ys = as_ @ s_fc2_w.T + s_fc2_b
        return (y + ys).reshape(s, b, d)

    def _L3_attn_ref(x, Wq, Wk, Wv, Wo, bo):
        import jax, jax.numpy as jnp
        import numpy as np
        B, T, E = (4, 256, 128)
        H, D = (16, 64)
        b, t, _ = x.shape
        q = (x @ Wq).reshape(b, t, H, D).transpose(0, 2, 1, 3)
        k = (x @ Wk).reshape(b, t, H, D).transpose(0, 2, 1, 3)
        v = (x @ Wv).reshape(b, t, H, D).transpose(0, 2, 1, 3)
        scores = jnp.einsum('bhqd,bhkd->bhqk', q, k)
        causal = jnp.tril(jnp.ones((t, t), dtype=bool))
        scores = jnp.where(causal, scores, -jnp.inf)
        attn = jax.nn.softmax(scores / np.sqrt(D).astype(np.float32), axis=-1)
        ctx = jnp.einsum('bhqk,bhkd->bhqd', attn, v)
        ctx = ctx.transpose(0, 2, 1, 3).reshape(b, t, H * D)
        return ctx @ Wo + bo

    def _L3_ffn_ref(hidden_states, rms_w, gate_w, w13, w2, sw_gate, sw_up, sw_down):
        import jax, jax.numpy as jnp
        import numpy as np
        H = 128
        I = 64
        E = 64
        K = 2
        EPS = 1e-06
        CAP = 128

        def _rmsnorm(x, w, eps=EPS):
            v = jnp.mean(x.astype(jnp.float32) ** 2, axis=-1, keepdims=True)
            return (x.astype(jnp.float32) * jax.lax.rsqrt(v + eps)).astype(x.dtype) * w
        B, S, Hh = hidden_states.shape
        residual = hidden_states
        x = _rmsnorm(hidden_states, rms_w).reshape(-1, Hh)
        T = x.shape[0]
        logits = x.astype(jnp.float32) @ gate_w.astype(jnp.float32).T
        probs = jax.nn.softmax(logits, axis=-1)
        topk_w, topk_ids = jax.lax.top_k(probs, K)
        topk_w = (topk_w / jnp.sum(topk_w, axis=-1, keepdims=True)).astype(x.dtype)
        flat_e = topk_ids.reshape(-1)
        order = jnp.argsort(flat_e)
        se = flat_e[order]
        tok = order // K
        counts = jax.ops.segment_sum(jnp.ones_like(se, jnp.int32), se, num_segments=E)
        starts = jnp.cumsum(counts) - counts
        pos = jnp.arange(se.shape[0]) - starts[se]
        pos_c = jnp.minimum(pos, CAP)
        buf = jnp.zeros((E, CAP + 1, Hh), x.dtype).at[se, pos_c].set(x[tok])
        xb = buf[:, :CAP]
        gu = jnp.einsum('ech,ehf->ecf', xb, w13)
        g, u = jnp.split(gu, 2, axis=-1)
        hact = jax.nn.silu(g) * u
        yb = jnp.einsum('eci,eih->ech', hact, w2)
        yb = jnp.concatenate([yb, jnp.zeros((E, 1, Hh), yb.dtype)], axis=1)
        y_slot = yb[se, pos_c]
        w_slot = topk_w.reshape(-1)[order]
        moe_out = jnp.zeros((T, Hh), x.dtype).at[tok].add(w_slot[:, None] * y_slot)
        shared = jax.nn.silu(x @ sw_gate) * (x @ sw_up) @ sw_down
        out = (moe_out + shared).reshape(B, S, Hh) + residual
        return out
    x = L0_attn_x
    mod = (_silu(L0_c) @ L0_wmod).reshape(L0_c.shape[0], 6, 1, -1)
    sa, ca, ga, sb, cb, gb = (mod[:, 0], mod[:, 1], mod[:, 2], mod[:, 3], mod[:, 4], mod[:, 5])
    ga = (2 * (ga >= 0) - 1) * jnp.maximum(jnp.abs(ga), 0.25)
    gb = (2 * (gb >= 0) - 1) * jnp.maximum(jnp.abs(gb), 0.25)
    h = _layernorm(x, axis=-1) * (1 + ca) + sa
    x = x + ga * _L0_attn_ref(h, L0_attn_Wq, L0_attn_Wk, L0_attn_Wv, L0_attn_Wo, L0_attn_bo)
    h = _layernorm(x, axis=-1) * (1 + cb) + sb
    x = x + gb * _L0_ffn_ref(h, L0_ffn_gate_w, L0_ffn_gate_b, L0_ffn_W1, L0_ffn_b1, L0_ffn_W2, L0_ffn_b2)
    mod = (_silu(L1_c) @ L1_wmod).reshape(L1_c.shape[0], 6, 1, -1)
    sa, ca, ga, sb, cb, gb = (mod[:, 0], mod[:, 1], mod[:, 2], mod[:, 3], mod[:, 4], mod[:, 5])
    ga = (2 * (ga >= 0) - 1) * jnp.maximum(jnp.abs(ga), 0.25)
    gb = (2 * (gb >= 0) - 1) * jnp.maximum(jnp.abs(gb), 0.25)
    h = _layernorm(x, axis=-1) * (1 + ca) + sa
    x = x + ga * _L1_attn_ref(h, L1_attn_Wq, L1_attn_bq, L1_attn_Wkd, L1_attn_bkd, L1_attn_Wku, L1_attn_bku, L1_attn_Wo, L1_attn_bo)
    h = _layernorm(x, axis=-1) * (1 + cb) + sb
    x = x + gb * _L1_ffn_ref(h, L1_ffn_gate_w, L1_ffn_w1, L1_ffn_w2, L1_ffn_w3)
    mod = (_silu(L2_c) @ L2_wmod).reshape(L2_c.shape[0], 6, 1, -1)
    sa, ca, ga, sb, cb, gb = (mod[:, 0], mod[:, 1], mod[:, 2], mod[:, 3], mod[:, 4], mod[:, 5])
    ga = (2 * (ga >= 0) - 1) * jnp.maximum(jnp.abs(ga), 0.25)
    gb = (2 * (gb >= 0) - 1) * jnp.maximum(jnp.abs(gb), 0.25)
    h = _layernorm(x, axis=-1) * (1 + ca) + sa
    x = x + ga * _L2_attn_ref(h, L2_attn_norm_w, L2_attn_W_in, L2_attn_b_in, L2_attn_W_x, L2_attn_b_x, L2_attn_W_dt, L2_attn_b_dt, L2_attn_W_out, L2_attn_b_out)
    h = _layernorm(x, axis=-1) * (1 + cb) + sb
    x = x + gb * _L2_ffn_ref(h, L2_ffn_gate_w, L2_ffn_fc1_w, L2_ffn_fc1_b, L2_ffn_geglu_mult, L2_ffn_fc2_w, L2_ffn_fc2_b, L2_ffn_s_fc1_w, L2_ffn_s_fc1_b, L2_ffn_s_geglu_mult, L2_ffn_s_fc2_w, L2_ffn_s_fc2_b)
    mod = (_silu(L3_c) @ L3_wmod).reshape(L3_c.shape[0], 6, 1, -1)
    sa, ca, ga, sb, cb, gb = (mod[:, 0], mod[:, 1], mod[:, 2], mod[:, 3], mod[:, 4], mod[:, 5])
    ga = (2 * (ga >= 0) - 1) * jnp.maximum(jnp.abs(ga), 0.25)
    gb = (2 * (gb >= 0) - 1) * jnp.maximum(jnp.abs(gb), 0.25)
    h = _layernorm(x, axis=-1) * (1 + ca) + sa
    x = x + ga * _L3_attn_ref(h, L3_attn_Wq, L3_attn_Wk, L3_attn_Wv, L3_attn_Wo, L3_attn_bo)
    h = _layernorm(x, axis=-1) * (1 + cb) + sb
    x = x + gb * _L3_ffn_ref(h, L3_ffn_rms_w, L3_ffn_gate_w, L3_ffn_w13, L3_ffn_w2, L3_ffn_sw_gate, L3_ffn_sw_up, L3_ffn_sw_down)
    return x

_drawn_inputs = setup_inputs


def setup_inputs(seed=0):
    import zlib

    import numpy as np

    out = dict(_drawn_inputs(seed))
    spreads = {'L0_attn_bo': (0.0, 0.1),
     'L0_ffn_gate_b': (0.0, 0.386),
     'L0_ffn_b1': (0.0, 0.8),
     'L0_ffn_b2': (0.0, 0.333),
     'L1_attn_bq': (0.0, 0.8),
     'L1_attn_bkd': (0.0, 0.8),
     'L1_attn_bku': (0.0, 0.785),
     'L1_attn_bo': (0.0, 0.1),
     'L2_attn_norm_w': (1.0, 0.6),
     'L2_attn_b_in': (0.0, 0.74),
     'L2_attn_b_x': (0.0, 0.598),
     'L2_attn_b_dt': (0.0, 2.0),
     'L2_attn_b_out': (0.0, 0.321),
     'L2_ffn_geglu_mult': (1.0, 0.6),
     'L2_ffn_s_geglu_mult': (1.0, 0.6),
     'L3_ffn_rms_w': (1.0, 0.6)}
    factors = {'L0_attn_Wq': 8.0,
     'L0_attn_Wk': 8.0,
     'L0_attn_Wv': 8.0,
     'L0_attn_Wo': 8.0,
     'L0_ffn_W1': 4.195,
     'L0_ffn_W2': 4.066,
     'L1_attn_Wq': 8.0,
     'L1_attn_Wkd': 8.0,
     'L1_attn_Wku': 8.0,
     'L1_attn_Wo': 6.123,
     'L1_ffn_gate_w': 7.596,
     'L1_ffn_w1': 7.236,
     'L1_ffn_w2': 7.565,
     'L1_ffn_w3': 6.696,
     'L2_ffn_gate_w': 3.872,
     'L2_ffn_fc1_w': 4.485,
     'L2_ffn_fc1_b': 8.0,
     'L2_ffn_fc2_w': 4.897,
     'L2_ffn_fc2_b': 13.73,
     'L2_ffn_s_fc1_w': 4.296,
     'L2_ffn_s_fc1_b': 8.0,
     'L2_ffn_s_fc2_w': 4.336,
     'L2_ffn_s_fc2_b': 10.145,
     'L3_attn_Wq': 8.0,
     'L3_attn_Wk': 8.0,
     'L3_attn_Wv': 8.0,
     'L3_attn_Wo': 7.546,
     'L3_attn_bo': 31.298}
    for name, (base, spread) in spreads.items():
        noise = np.random.default_rng([zlib.crc32(name.encode()), seed]).standard_normal(out[name].shape)
        drawn = base * np.exp(spread * noise) if base else spread * noise
        out[name] = jnp.asarray(drawn.astype(out[name].dtype))
    for name, factor in factors.items():
        out[name] = (out[name] * factor).astype(out[name].dtype)
    return out
```

```python
from contextlib import ExitStack

import concourse.bass as bass
from concourse import mybir
import numpy as np

ALU = mybir.AluOpType
ACT = mybir.ActivationFunctionType
F32 = mybir.dt.float32
BF16 = mybir.dt.bfloat16
I32 = mybir.dt.int32
U32 = mybir.dt.uint32
AX_X = mybir.AxisListType.X

P = 128
B = 4
S = 512
Q = S // P
NT = B * Q
T = B * S
LAYERS = 4
HEADS = 16
L3_E, CAP = 64, 128
L3_SLOTS = L3_E * CAP
ZERO_FILLS = L3_SLOTS * P // (P * 1024)
NEG = -1.0e30


class Signal:

    def __init__(self, sem):
        self.sem = sem
        self.base = 0

    def __call__(self, n):
        return self.sem, self.base + n


class Core:

    def __init__(self, nc, ctx):
        self.nc = nc
        self.ctx = ctx
        self.signals = {}


def signal(core, name):
    if name not in core.signals:
        core.signals[name] = Signal(core.ctx.enter_context(core.nc.semaphore(name)))
    return core.signals[name]


def stage_ends(core, **totals):
    for name, total in totals.items():
        core.signals[name].base += total


def setup(core, x, ct, wmod):
    nc = core.nc
    sb = lambda name, shape, dt=F32: core.ctx.enter_context(nc.sbuf_tensor(name, shape, dt))
    core.x = sb("x_tok", [P, NT, P])
    core.h = sb("h_feat", [P, T])
    core.ident = sb("ident", [P, P])
    core.ident_bf = sb("ident_bf", [P, P], BF16)
    core.mask = sb("causal_mask", [P, P], BF16)
    core.ones = sb("ones", [P, P])
    core.shift = sb("shift", [P, LAYERS, 2, B])
    core.scale = sb("scale", [P, LAYERS, 2, B])
    core.gate = sb("gate", [P, LAYERS, 2, B, P])

    core.zeros = sb("zeros", [P, 1024])
    core.slots_in = nc.dram_tensor("slots_in", [L3_SLOTS, P], F32).ap()
    core.slots_out = nc.dram_tensor("slots_out", [L3_SLOTS, P], F32).ap()
    zeroed = signal(core, "slots_zeroed")
    loaded, consts, silu_c, step = (signal(core, n) for n in ("loaded", "consts", "silu_c", "dve_step"))
    mod_psum, mod_free = signal(core, "mod_psum"), signal(core, "mod_free")
    gate_psum, gate_abs = (signal(core, n) for n in ("gate_psum", "gate_abs"))
    with ExitStack() as ctx:
        tmp = lambda name, shape, dt=F32: ctx.enter_context(nc.sbuf_tensor(name, shape, dt))
        w_sb = tmp("wmod_sb", [P, LAYERS, 6, P])
        c_sb = tmp("c_sb", [P, LAYERS * B])
        sc = tmp("silu_c_sb", [P, LAYERS * B])
        sc_wide = tmp("silu_c_wide", [P, LAYERS * B, P])
        sign = tmp("gate_sign", [P, 2, B, P])
        mag = tmp("gate_mag", [P, 2, B, P])
        mod_ps = ctx.enter_context(nc.psum_tensor("mod_ps", [P, 4, LAYERS, B], F32))
        gate_ps = ctx.enter_context(nc.psum_tensor("gate_ps", [P, 2, 2, B, P], F32))
        with nc.Block() as block:

            @block.sync
            def _(sp):
                sp.dma_start(c_sb[:], ct).then_inc(loaded.sem, 16)
                sp.dma_start(w_sb[:], wmod).then_inc(loaded.sem, 16)
                sp.dma_start(core.x[:], x.rearrange("b (q p) d -> p (b q) d", p=P)).then_inc(loaded.sem, 16)
                sp.wait_ge(*consts(5))
                for k in range(ZERO_FILLS):
                    part = L3_SLOTS // ZERO_FILLS
                    sp.dma_start(core.slots_in[k * part:(k + 1) * part, :].rearrange("(p r) d -> p (r d)", p=P),
                                 core.zeros[:]).then_inc(zeroed.sem, 16)
                sp.wait_ge(*loaded(48))

            @block.gpsimd
            def _(pool):
                pool.memset(core.zeros[:], 0.0).then_inc(consts.sem, 1)
                for m in (core.ident, core.ident_bf, core.mask):
                    pool.memset(m[:], 0.0).then_inc(consts.sem, 1)
                pool.memset(core.ones[:], 1.0).then_inc(consts.sem, 1)
                pool.wait_ge(*consts(5))
                for m in (core.ident, core.ident_bf):
                    pool.affine_select(out=m[:], in_=m[:], compare_op=ALU.not_equal, fill=1.0, base=0,
                                       pattern=[[-1, P]], channel_multiplier=1).then_inc(consts.sem, 1)
                pool.affine_select(out=core.mask[:], in_=core.mask[:], compare_op=ALU.is_ge, fill=NEG, base=0,
                                   pattern=[[-1, P]], channel_multiplier=1).then_inc(consts.sem, 1)

            @block.scalar
            def _(act):
                act.wait_ge(*loaded(48))
                act.activation(sc[:], c_sb[:], ACT.Silu).then_inc(silu_c.sem, 1)

            @block.tensor
            def _(pe):
                pe.wait_ge(*step(1))
                pe.wait_ge(*loaded(48))
                for j, part in enumerate((0, 1, 3, 4)):
                    for l in range(LAYERS):
                        mm = pe.matmul(mod_ps[:, j, l, :], w_sb[:, l, part, :], sc[:, l * B:(l + 1) * B],
                                       start=True, stop=True)
                mm.then_inc(mod_psum.sem, 1)
                for l in range(LAYERS):
                    if l >= 2:
                        pe.wait_ge(*gate_abs(4 * (l - 2) + 3))
                    for k, part in enumerate((2, 5)):
                        for b in range(B):
                            mm = pe.matmul(gate_ps[:, l % 2, k, b, :], sc_wide[:, l * B + b, :],
                                           w_sb[:, l, part, :], start=True, stop=True)
                    mm.then_inc(gate_psum.sem, 1)

            @block.vector
            def _(dve):
                dve.wait_ge(*silu_c(1))
                dve.tensor_copy(sc_wide[:], sc[:].unsqueeze(2).broadcast_to([P, LAYERS * B, P])).then_inc(step.sem, 1)
                dve.wait_ge(*mod_psum(1))
                for half in range(2):
                    dve.tensor_copy(core.shift[:, :, half, :], mod_ps[:, 2 * half]).then_inc(mod_free.sem, 1)
                    dve.tensor_scalar(core.scale[:, :, half, :], mod_ps[:, 2 * half + 1], 1.0, None,
                                      ALU.add).then_inc(mod_free.sem, 1)
                for l in range(LAYERS):
                    dve.wait_ge(*gate_psum(l + 1))
                    flat = lambda a: a.rearrange("p k b d -> p (k b d)")
                    dve.tensor_scalar(sign[:], gate_ps[:, l % 2], 0.0, 2.0, ALU.is_ge, ALU.mult)\
                       .then_inc(gate_abs.sem, 1)
                    dve.wait_ge(*gate_abs(4 * l + 1))
                    dve.tensor_scalar(sign[:], sign[:], -1.0, None, ALU.add).then_inc(gate_abs.sem, 1)
                    dve.wait_ge(*gate_abs(4 * l + 2))
                    dve.tensor_tensor(mag[:], gate_ps[:, l % 2], sign[:], ALU.mult).then_inc(gate_abs.sem, 1)
                    dve.wait_ge(*gate_abs(4 * l + 3))
                    dve.scalar_tensor_tensor(flat(core.gate[:, l]), flat(mag[:]), 0.25, flat(sign[:]), ALU.max,
                                             ALU.mult).then_inc(gate_abs.sem, 1)
                    dve.wait_ge(*gate_abs(4 * l + 4))
    stage_ends(core, loaded=48, consts=8, silu_c=1, dve_step=1, mod_psum=1, mod_free=4, gate_psum=4, gate_abs=16)


def layer_norm(core, layer, half):
    nc = core.nc
    step, var, std, xn, tr, done = (signal(core, n) for n in
                                    ("dve_step", "ln_var", "ln_std", "ln_normed", "ln_transposed", "ln_h"))
    with ExitStack() as ctx:
        tmp = lambda name, shape, dt=F32: ctx.enter_context(nc.sbuf_tensor(f"{name}_{layer}{half}", shape, dt))
        st = tmp("ln_stats", [P, NT, 6])
        mv = tmp("ln_mv", [P, NT, 2])
        ve = tmp("ln_ve", [P, NT])
        sd = tmp("ln_sd", [P, NT])
        rs = tmp("ln_rs", [P, NT])
        xm = tmp("ln_xn", [P, NT, P])
        ps = ctx.enter_context(nc.psum_tensor(f"ln_ps_{layer}{half}", [P, 2, S], F32))
        with nc.Block() as block:

            @block.vector
            def _(dve):
                n = 0
                for b in range(B):
                    for t in range(Q * b, Q * b + Q):
                        dve.bn_stats(st[:, t, :], core.x[:, t, :]).then_inc(step.sem, 1)
                    n += Q
                    dve.wait_ge(*step(n))
                    for t in range(Q * b, Q * b + Q):
                        dve.bn_aggr(mv[:, t, :], st[:, t, :]).then_inc(step.sem, 1)
                    n += Q
                    dve.wait_ge(*step(n))
                    dve.tensor_scalar(ve[:, Q * b:Q * b + Q], mv[:, Q * b:Q * b + Q, 1], 1e-5, None, ALU.add)\
                       .then_inc(var.sem, 1)
                for b in range(B):
                    dve.wait_ge(*std(b + 1))
                    dve.reciprocal(rs[:, Q * b:Q * b + Q], sd[:, Q * b:Q * b + Q]).then_inc(step.sem, 1)
                    n += 1
                    dve.wait_ge(*step(n))
                    for t in range(Q * b, Q * b + Q):
                        last = dve.tensor_scalar(xm[:, t, :], core.x[:, t, :], mv[:, t, 0:1], rs[:, t:t + 1],
                                                 ALU.subtract, ALU.mult)
                    last.then_inc(xn.sem, 1)

            @block.scalar
            def _(act):
                for b in range(B):
                    act.wait_ge(*var(b + 1))
                    act.activation(sd[:, Q * b:Q * b + Q], ve[:, Q * b:Q * b + Q], ACT.Sqrt).then_inc(std.sem, 1)
                for b in range(B):
                    act.wait_ge(*tr(b + 1))
                    act.activation(core.h[:, b * S:(b + 1) * S], ps[:, b % 2, :], ACT.Identity,
                                   bias=core.shift[:, layer, half, b:b + 1],
                                   scale=core.scale[:, layer, half, b:b + 1]).then_inc(done.sem, 1)

            @block.tensor
            def _(pe):
                for b in range(B):
                    pe.wait_ge(*xn(b + 1))
                    if b >= 2:
                        pe.wait_ge(*done(b - 1))
                    for q in range(Q):
                        mm = pe.transpose(ps[:, b % 2, q * P:(q + 1) * P], xm[:, Q * b + q, :], core.ident[:])
                    mm.then_inc(tr.sem, 1)
    stage_ends(core, dve_step=8 * B + B, ln_var=B, ln_std=B, ln_normed=B, ln_transposed=B, ln_h=B)


def values(core, name, source, w, bias, width):
    nc = core.nc
    loaded, vps, va, vd = (signal(core, n) for n in ("loaded", "v_psum", "v_by_act", "v_by_dve"))
    v = core.v
    K = w.shape[0]
    per = max(1, 512 // width)
    parts = max(1, width // 512)
    jobs = [(t, c) for t in range(0, NT, per) for c in range(parts)]
    with ExitStack() as ctx:
        w_sb = ctx.enter_context(nc.sbuf_tensor(f"wv_{name}", [K, width], F32))
        b_sb = ctx.enter_context(nc.sbuf_tensor(f"bv_{name}", [1, width], F32))
        ps = ctx.enter_context(nc.psum_tensor(f"v_ps_{name}", [P, 4, 512], F32))
        cols = min(width, 512)

        def out_of(t, c):
            return v[:, t:t + per, c * cols:(c + 1) * cols]

        with nc.Block() as block:

            @block.sync
            def _(sp):
                sp.dma_start(w_sb[:], w).then_inc(loaded.sem, 16)
                if bias is not None:
                    sp.dma_start(b_sb[:], bias).then_inc(loaded.sem, 16)

            @block.tensor
            def _(pe):
                pe.wait_ge(*loaded(16 if bias is None else 32))
                for n, (t, c) in enumerate(jobs):
                    if n >= 4:
                        m = n - 4
                        pe.wait_ge(*(va if m % 2 else vd)(m // 2 + 1))
                    for k in range(per):
                        if bias is not None:
                            pe.matmul(ps[:, n % 4, k * cols:(k + 1) * cols], core.ones[0:1, :],
                                      b_sb[0:1, c * cols:(c + 1) * cols], start=True, stop=False)
                        mm = pe.matmul(ps[:, n % 4, k * cols:(k + 1) * cols], source[:, (t + k) * P:(t + k + 1) * P],
                                       w_sb[:, c * cols:(c + 1) * cols], start=bias is None, stop=True)
                    mm.then_inc(vps.sem, 1)

            @block.scalar
            def _(act):
                for n, (t, c) in enumerate(jobs):
                    if n % 2:
                        act.wait_ge(*vps(n + 1))
                        act.activation(out_of(t, c), ps[:, n % 4, :].rearrange("p (k c) -> p k c", k=per), ACT.Copy)\
                           .then_inc(va.sem, 1)

            @block.vector
            def _(dve):
                for n, (t, c) in enumerate(jobs):
                    if n % 2 == 0:
                        dve.wait_ge(*vps(n + 1))
                        dve.tensor_copy(out_of(t, c), ps[:, n % 4, :].rearrange("p (k c) -> p k c", k=per))\
                           .then_inc(vd.sem, 1)
    stage_ends(core, loaded=16 if bias is None else 32, v_psum=len(jobs), v_by_act=len(jobs) // 2,
             v_by_dve=len(jobs) // 2)


def attention(core, layer, groups, dv, causal, k_source, wq, wk, wo, bo, q_bias=None, k_bias=None, q_scale=1.0, k_scale=1.0):
    nc = core.nc
    hpg = HEADS // groups
    hr = P // hpg
    U = hpg * Q
    hv = hpg * dv
    KK = wk.shape[1]
    NG = B * groups
    LAG_T, LAG_V = 2, 3
    names = ("loaded", "out_scaled", "x_biased", "q_made", "k_made", "misc_full", "s_full", "neg_max",
             "probs", "t_full", "pt_dve", "pt_act", "o_full", "sums_inverse", "ctx_ready", "ctx_turned", "x_added", "q_cleared")
    (loaded, out_scaled, x_biased, q_made, k_made, misc_full, s_full, neg_max, probs, t_full, pt_dve, pt_act,
     o_full, sums_inverse, ctx_ready, ctx_turned, x_added, q_cleared) = (signal(core, n) for n in names)
    wslot = [signal(core, "weights_slot0"), signal(core, "weights_slot1")]
    act_copies = lambda u: u % 4 == 3

    def copied(g, u):
        by_act = (u + 1) // 4
        return pt_act(g * (U // 4) + by_act) if act_copies(u) else pt_dve(g * (U - U // 4) + u + 1 - by_act)

    with ExitStack() as ctx:
        tmp = lambda name, shape, dt=F32: ctx.enter_context(nc.sbuf_tensor(f"{name}_{layer}", shape, dt))
        psum = lambda name, shape: ctx.enter_context(nc.psum_tensor(f"{name}_{layer}", shape, F32))
        wq_s = tmp("wq_slot", [P, 2, P])
        wk_s = tmp("wk_slot", [KK, 2, P])
        qb_s = tmp("qb_slot", [P, groups]) if q_bias is not None else None
        kb_s = tmp("kb_slot", [P, groups]) if k_bias is not None else None
        wo_sb = tmp("wo_sb", [hv, groups, P])
        wog = tmp("wo_gated", [hv, B, groups, P])
        bo_sb = tmp("bo_sb", [P, P])
        bog = tmp("bo_gated", [P, B, P])
        q_sb = tmp("q_sb", [P, 2, hpg, S])
        k_sb = tmp("k_sb", [P, 2, S])
        prob = tmp("prob", [P, 4, S])
        pt = tmp("prob_t", [P, 4, S])
        nm = tmp("neg_max", [P, 4])
        sums = tmp("sums", [P, 2, U])
        inv = tmp("inv_sums", [P, 2, U])
        ctx_sb = tmp("ctx_sb", [P, 2, U * dv])
        ctx_t = tmp("ctx_t", [hv, S])
        s_ps = psum("s_ps", [P, 2, S])
        t_ps = psum("t_ps", [P, 2, S])
        o_ps = psum("o_ps", [P, 2, 4, P])
        misc = psum("misc_ps", [P, S])

        batch = lambda g: g // groups
        in_batch = lambda g: g % groups
        v_column = lambda g: in_batch(g) * hv if hv == P else 0
        keys = lambda u: (u // hpg + 1) * P if causal else S

        with nc.Block() as block:

            @block.sync
            def _(sp):
                sp.dma_start(wo_sb[:], wo.rearrange("g f n -> f g n")).then_inc(loaded.sem, 16)
                sp.dma_start(bo_sb[:], bo.broadcast_to([P, P])).then_inc(loaded.sem, 16)
                if q_bias is not None:
                    sp.dma_start(qb_s[:], q_bias).then_inc(loaded.sem, 16)
                    sp.dma_start(kb_s[:], k_bias).then_inc(loaded.sem, 16)

                def load(g, s):
                    sp.dma_start(wq_s[:, s, :], wq[in_batch(g), :, :]).then_inc(wslot[s].sem, 16)
                    sp.dma_start(wk_s[:, s, :], wk[in_batch(g), :, :]).then_inc(wslot[s].sem, 16)

                load(0, 0)
                load(1, 1)
                with sp.Fori(1, NG // 2) as i:
                    for s in range(2):
                        sp.wait_ge(*k_made(2 * (i - 1) + s + 1))
                        load(2 * i + s, s)

            @block.gpsimd
            def _(pool):
                pool.memset(q_sb[:], 0.0).then_inc(q_cleared.sem, 1)
                pool.wait_ge(*loaded(32 if q_bias is None else 64))
                for b in range(B):
                    pool.tensor_tensor(wog[:, b], wo_sb[:],
                                       core.gate[0:hv, layer, 0, b, :].unsqueeze(1).broadcast_to([hv, groups, P]),
                                       ALU.mult).then_inc(out_scaled.sem, 1)
                for b in range(B):
                    pool.tensor_tensor(bog[:, b], bo_sb[:], core.gate[:, layer, 0, b, :], ALU.mult)\
                        .then_inc(out_scaled.sem, 1)
                pool.wait_ge(*out_scaled(2 * B))
                for b in range(B):
                    xb = core.x[:, Q * b:Q * b + Q, :]
                    pool.tensor_tensor(xb, xb, bog[:, b, :].unsqueeze(1).broadcast_to([P, Q, P]), ALU.add)\
                        .then_inc(x_biased.sem, 1)

            @block.tensor
            def _(pe):
                def project_q(g, s):
                    pe.wait_ge(*wslot[s](32 * (g // 2) + 32))
                    if not isinstance(g, int) or g > 2:
                        pe.wait_ge(*x_added(g - 2))
                    elif g:
                        pe.wait_ge(*k_made(g))
                    pe.matmul(misc[:], wq_s[:, s, :], core.h[:, bass.ds(batch(g) * S, S)], start=True, stop=True)\
                      .then_inc(misc_full.sem, 1)

                def project_k(g, s):
                    pe.wait_ge(*q_made(g + 1))
                    pe.matmul(misc[:], wk_s[:, s, :], k_source[:, bass.ds(batch(g) * S, S)], start=True,
                              stop=True).then_inc(misc_full.sem, 1)

                def scores(g, s, u, first):
                    n = g * U + u
                    h, q = u % hpg, u // hpg
                    if u == 0:
                        pe.wait_ge(*k_made(g + 1))
                    if not (first and u < 2):
                        pe.wait_ge(*probs(n - 2 + 1))
                    mm = pe.matmul(s_ps[:, u % 2, 0:keys(u)], q_sb[:, s, h, q * P:(q + 1) * P],
                                   k_sb[:, s, 0:keys(u)], start=True, stop=True)
                    if causal:
                        mm = pe.matmul(s_ps[:, u % 2, q * P:(q + 1) * P], core.ident_bf[:], core.mask[:],
                                       start=False, stop=True, skip_group_check=True)
                    mm.then_inc(s_full.sem, 1)

                def turn(g, u, first):
                    n = g * U + u
                    pe.wait_ge(*probs(n + 1))
                    if not (first and u < 2):
                        pe.wait_ge(*copied(g, u - 2))
                    for c in range(keys(u) // P):
                        mm = pe.transpose(t_ps[:, u % 2, c * P:(c + 1) * P], prob[:, u % 4, c * P:(c + 1) * P],
                                          core.ident[:])
                    mm.then_inc(t_full.sem, 1)

                def times_v(g, u, first):
                    pe.wait_ge(*copied(g, u))
                    if u % 4 == 0 and not (first and u < 8):
                        pe.wait_ge(*ctx_ready(g * (U // 4) + u // 4 - 1))
                    last = keys(u) // P - 1
                    for c in range(last + 1):
                        mm = pe.matmul(o_ps[:, u // 4 % 2, u % 4, :], pt[:, u % 4, c * P:(c + 1) * P],
                                       core.v[:, batch(g) * Q + c, bass.ds(v_column(g), P)],
                                       start=c == 0, stop=c == last)
                    if u % 4 == 3:
                        mm.then_inc(o_full.sem, 1)

                def turn_ctx(g, s):
                    pe.wait_ge(*ctx_ready((g + 1) * (U // 4)))
                    for q in range(Q):
                        mm = pe.transpose(misc[0:hv, q * P:(q + 1) * P], ctx_sb[:, s, q * hv:(q + 1) * hv],
                                          core.ident[:])
                    mm.then_inc(misc_full.sem, 1)

                def project_out(g):
                    if isinstance(g, int) and g == 0:
                        pe.wait_ge(*out_scaled(2 * B))
                    pe.wait_ge(*ctx_turned(g + 1))
                    for q in range(Q):
                        mm = pe.matmul(misc[:, q * P:(q + 1) * P], ctx_t[:, q * P:(q + 1) * P],
                                       wog[:, batch(g), in_batch(g), :], start=True, stop=True)
                    mm.then_inc(misc_full.sem, 1)

                def window(g, s, first=False, last=False):
                    for u in range(U):
                        scores(g, s, u, first)
                        if u == 0 and not last:
                            project_q(g + 1, 1 - s)
                        if u == 1 and not last:
                            project_k(g + 1, 1 - s)
                        if u >= LAG_T:
                            turn(g, u - LAG_T, first)
                        elif not first:
                            turn(g - 1, u - LAG_T + U, False)
                        if u >= LAG_V:
                            times_v(g, u - LAG_V, first)
                        elif not first:
                            times_v(g - 1, u - LAG_V + U, False)
                        if u == 4 and not first:
                            if last:
                                pe.wait_ge(*x_added(g - 1))
                            else:
                                pe.wait_ge(*k_made(g + 2))
                            turn_ctx(g - 1, 1 - s)
                        if u == 6 and not first:
                            project_out(g - 1)

                project_q(0, 0)
                project_k(0, 0)
                window(0, 0, first=True)
                window(1, 1)
                with pe.Fori(1, NG // 2 - 1) as i:
                    window(2 * i, 0)
                    window(2 * i + 1, 1)
                window(NG - 2, 0)
                window(NG - 1, 1, last=True)
                for u in range(U - LAG_T, U + 1):
                    if u < U:
                        turn(NG - 1, u, False)
                    times_v(NG - 1, u - 1, False)
                pe.wait_ge(*x_added(NG - 1))
                turn_ctx(NG - 1, 1)
                project_out(NG - 1)

            @block.scalar
            def _(act):
                def make_q(g, s, use):
                    act.wait_ge(*misc_full(use))
                    for h in range(hpg):
                        r = slice(h * hr, h * hr + hr)
                        if qb_s is None:
                            last = act.mul(q_sb[r, s, h, :], misc[r, :], q_scale)
                        else:
                            last = act.activation(q_sb[r, s, h, :], misc[r, :], ACT.Identity, scale=q_scale,
                                                  bias=qb_s[r, bass.ds(in_batch(g), 1)])
                    last.then_inc(q_made.sem, 1)

                def make_k(g, s, use):
                    act.wait_ge(*misc_full(use))
                    if kb_s is None:
                        act.copy(k_sb[:, s, :], misc[:]).then_inc(k_made.sem, 1)
                    else:
                        act.activation(k_sb[:, s, :], misc[:], ACT.Identity, scale=k_scale,
                                       bias=kb_s[:, bass.ds(in_batch(g), 1)]).then_inc(k_made.sem, 1)

                def exps(g, s, u, first):
                    n = g * U + u
                    act.wait_ge(*neg_max(n + 1))
                    if not (first and u < 4):
                        act.wait_ge(*t_full(n - 4 + 1))
                    act.activation(prob[:, u % 4, 0:keys(u)], s_ps[:, u % 2, 0:keys(u)], ACT.Exp,
                                   bias=nm[:, u % 4:u % 4 + 1], accum_out=sums[:, s, u:u + 1]).then_inc(probs.sem, 1)

                def copy_turned(g, u):
                    if act_copies(u):
                        n = g * U + u
                        act.wait_ge(*t_full(n + 1))
                        act.copy(pt[:, u % 4, 0:keys(u)], t_ps[:, u % 2, 0:keys(u)]).then_inc(pt_act.sem, 1)

                def copy_ctx(g, use):
                    act.wait_ge(*misc_full(use))
                    act.copy(ctx_t[:], misc[0:hv, :]).then_inc(ctx_turned.sem, 1)

                def window(g, s, first=False, last=False):
                    for u in range(U):
                        exps(g, s, u, first)
                        if u == 0 and not last:
                            make_q(g + 1, 1 - s, 3 if first else 4 * g + 1)
                        if u == 1 and not last:
                            make_k(g + 1, 1 - s, 4 if first else 4 * g + 2)
                        if u >= LAG_T:
                            copy_turned(g, u - LAG_T)
                        elif not first:
                            copy_turned(g - 1, u - LAG_T + U)
                        if u == 5 and not first:
                            copy_ctx(g - 1, 4 * g + 1 if last else 4 * g + 3)

                if q_bias is not None:
                    act.wait_ge(*loaded(64))
                act.wait_ge(*q_cleared(1))
                make_q(0, 0, 1)
                make_k(0, 0, 2)
                window(0, 0, first=True)
                window(1, 1)
                with act.Fori(1, NG // 2 - 1) as i:
                    window(2 * i, 0)
                    window(2 * i + 1, 1)
                window(NG - 2, 0)
                window(NG - 1, 1, last=True)
                for u in range(U - LAG_T, U):
                    copy_turned(NG - 1, u)
                copy_ctx(NG - 1, 4 * NG - 1)

            @block.vector
            def _(dve):
                def maxima(g, u, first):
                    n = g * U + u
                    dve.wait_ge(*s_full(n + 1))
                    if not (first and u < 4):
                        dve.wait_ge(*probs(n - 4 + 1))
                    dve.tensor_reduce(nm[:, u % 4:u % 4 + 1], s_ps[:, u % 2, 0:keys(u)], AX_X, ALU.max,
                                      negate=True).then_inc(neg_max.sem, 1)

                def copy_turned(g, u):
                    if not act_copies(u):
                        n = g * U + u
                        dve.wait_ge(*t_full(n + 1))
                        dve.tensor_copy(pt[:, u % 4, 0:keys(u)], t_ps[:, u % 2, 0:keys(u)]).then_inc(pt_dve.sem, 1)

                def normalise(g, s, k):
                    n = g * (U // 4) + k
                    dve.wait_ge(*probs(g * U + 4 * k + 4))
                    dve.reciprocal(inv[:, s, 4 * k:4 * k + 4], sums[:, s, 4 * k:4 * k + 4]).then_inc(sums_inverse.sem, 1)
                    dve.wait_ge(*o_full(n + 1))
                    dve.wait_ge(*sums_inverse(n + 1))
                    for i in range(4 // hpg):
                        flat = o_ps[:, k % 2, i * hpg:(i + 1) * hpg, :].rearrange("p h c -> p (h c)")
                        at = 4 * k + i * hpg
                        own = [flat[:, bass.ds(h * P + h * dv + (0 if hv == P else in_batch(g) * hv), dv)]
                               for h in range(hpg)]
                        for h in range(hpg):
                            last = dve.tensor_scalar(ctx_sb[:, s, (at + h) * dv:(at + h + 1) * dv], own[h],
                                                     inv[:, s, at + h:at + h + 1], None, ALU.mult)
                    last.then_inc(ctx_ready.sem, 1)

                def add_to_x(g, use):
                    if isinstance(g, int) and g == 0:
                        dve.wait_ge(*x_biased(B))
                    dve.wait_ge(*misc_full(use))
                    xb = core.x[:, bass.ds(batch(g) * Q, Q), :]
                    dve.tensor_tensor(xb, xb, misc[:].rearrange("p (q d) -> p q d", q=Q), ALU.add)\
                       .then_inc(x_added.sem, 1)

                def window(g, s, first=False, last=False):
                    for u in range(U):
                        if u % 4 == 3 and u > 4:
                            normalise(g, s, (u - 7) // 4)
                        elif u == 3 and not first:
                            normalise(g - 1, 1 - s, U // 4 - 1)
                        maxima(g, u, first)
                        if u >= LAG_T:
                            copy_turned(g, u - LAG_T)
                        elif not first:
                            copy_turned(g - 1, u - LAG_T + U)
                        if u == 7 and not first:
                            add_to_x(g - 1, 4 * g + 2 if last else 4 * g + 4)

                window(0, 0, first=True)
                window(1, 1)
                with dve.Fori(1, NG // 2 - 1) as i:
                    window(2 * i, 0)
                    window(2 * i + 1, 1)
                window(NG - 2, 0)
                window(NG - 1, 1, last=True)
                for u in range(U - LAG_T, U):
                    copy_turned(NG - 1, u)
                normalise(NG - 1, 1, U // 4 - 1)
                add_to_x(NG - 1, 4 * NG)
    units = NG * U
    stage_ends(core, loaded=32 if q_bias is None else 64, weights_slot0=16 * NG, weights_slot1=16 * NG, out_scaled=2 * B, x_biased=B, q_made=NG, k_made=NG,
             misc_full=4 * NG, s_full=units, neg_max=units, probs=units, t_full=units, pt_dve=units - units // 4,
             pt_act=units // 4, o_full=units // 4, sums_inverse=units // 4, ctx_ready=units // 4, ctx_turned=NG, x_added=NG, q_cleared=1)


def route(core, layer, E, gate_w, gate_b, kind, source=None, chosen=None):
    nc = core.nc
    K = 3 if kind == "renormed" else 2
    loaded, full, step, to_exp, exped, iotas = (signal(core, n) for n in
                                                ("loaded", "logits_full", "dve_step", "to_exp", "exped", "iotas"))
    counts = {}
    with ExitStack() as ctx:
        tmp = lambda name, shape, dt=F32: ctx.enter_context(nc.sbuf_tensor(f"{name}_r{layer}", shape, dt))
        gw = tmp("gate_w", [P, E])
        gb = tmp("gate_b", [P, E])
        lg = tmp("logits", [P, NT, E])
        top = tmp("top", [P, NT, 8])
        idx = tmp("idx", [P, NT, 8], U32)
        iota_i = tmp("iota_i", [P, E], I32)
        iota = tmp("iota", [P, E])
        wide = [tmp(f"wide{n}", [P, NT, E]) for n in range(4)]
        if chosen is None:
            hot, ws, idx_f = tmp("hot", [P, K, NT, E]), tmp("ws", [P, K, NT]), tmp("idx_f", [P, NT, 8])
        else:
            hot, ws, idx_f = chosen
        thin = [tmp(f"thin{n}", [P, NT]) for n in range(4)]
        ps = ctx.enter_context(nc.psum_tensor(f"logits_ps{layer}", [P, NT, E], F32))
        g = core.g if chosen is None else None
        source = core.h if source is None else source
        over_e = lambda a: a.unsqueeze(2).broadcast_to([P, NT, E])
        val = lambda k: top[:, :, k]
        with nc.Block() as block:

            @block.sync
            def _(sp):
                sp.dma_start(gw[:], gate_w).then_inc(loaded.sem, 16)
                if gate_b is not None:
                    sp.dma_start(gb[:], gate_b.broadcast_to([P, E])).then_inc(loaded.sem, 16)

            @block.gpsimd
            def _(pool):
                pool.iota(iota_i[:], pattern=[[1, E]], base=0, channel_multiplier=0).then_inc(iotas.sem, 1)
                if kind == "renormed":
                    pool.memset(g[:, E:E + 2, :], 1.0).then_inc(iotas.sem, 1)

            @block.tensor
            def _(pe):
                pe.wait_ge(*loaded(16 if gate_b is None else 32))
                for t in range(NT):
                    mm = pe.matmul(ps[:, t, :], source[:, t * P:(t + 1) * P], gw[:], start=True, stop=True)
                mm.then_inc(full.sem, 1)

            @block.vector
            def _(dve):
                n = 0

                def link(ins):
                    nonlocal n
                    n += 1
                    ins.then_inc(step.sem, 1)
                    dve.wait_ge(*step(n))

                exps = 0

                def exp_of(out):
                    nonlocal exps
                    exps += 1
                    dve.wait_ge(*exped(exps))

                dve.wait_ge(*iotas(2 if kind == "renormed" else 1))
                link(dve.tensor_copy(iota[:], iota_i[:]))
                dve.wait_ge(*full(1))
                if gate_b is not None:
                    dve.wait_ge(*loaded(32))
                    link(dve.tensor_tensor(lg[:], ps[:], gb[:].unsqueeze(1).broadcast_to([P, NT, E]), ALU.add))
                else:
                    link(dve.tensor_copy(lg[:], ps[:]))
                for t in range(NT):
                    last = dve.max(out=top[:, t, :], in_=lg[:, t, :])
                link(last)
                for t in range(NT):
                    last = dve.max_index(out=idx[:, t, :], in_max=top[:, t, :], in_values=lg[:, t, :])
                link(last)
                link(dve.tensor_copy(idx_f[:], idx[:]))
                for k in range(K):
                    last = dve.tensor_tensor(hot[:, k], iota[:].unsqueeze(1).broadcast_to([P, NT, E]),
                                             over_e(idx_f[:, :, k]), ALU.is_equal)
                link(last)
                if kind == "softmax":
                    dve.tensor_tensor(thin[0][:], val(1), val(0), ALU.subtract).then_inc(to_exp.sem, 1)
                    exp_of(thin[1])
                    link(dve.tensor_scalar(thin[2][:], thin[1][:], 1.0, None, ALU.add))
                    link(dve.reciprocal(ws[:, 0], thin[2][:]))
                    link(dve.tensor_tensor(ws[:, 1], thin[1][:], ws[:, 0], ALU.mult))
                elif kind == "jitter":
                    link(dve.scalar_tensor_tensor(wide[3][:].rearrange("p t e -> p (t e)"),
                                                  lg[:].rearrange("p t e -> p (t e)"), -1.0,
                                                  lg[:].rearrange("p t e -> p (t e)"), ALU.mult, ALU.max))
                    for k in range(2):
                        link(dve.tensor_tensor(wide[0][:], over_e(val(k)), lg[:], ALU.subtract))
                        link(dve.tensor_tensor(wide[1][:], wide[3][:], over_e(val(k)), ALU.max))
                        link(dve.tensor_scalar(wide[1][:], wide[1][:], 0.02, None, ALU.mult))
                        link(dve.tensor_tensor(wide[1][:], wide[0][:], wide[1][:], ALU.is_le))
                        if k == 1:
                            link(dve.tensor_tensor(wide[2][:], wide[1][:], hot[:, 0], ALU.mult))
                            link(dve.tensor_tensor(wide[1][:], wide[1][:], wide[2][:], ALU.subtract))
                        dve.tensor_scalar(wide[0][:], wide[0][:], 0.0, None, ALU.max).then_inc(to_exp.sem, 1)
                        exp_of(wide[2])
                        link(dve.tensor_tensor(wide[2][:], wide[2][:], wide[1][:], ALU.mult))
                        link(dve.tensor_reduce(thin[0][:], wide[2][:], AX_X, ALU.add))
                        link(dve.reciprocal(ws[:, k], thin[0][:]))
                else:
                    dve.tensor_tensor(wide[0][:], lg[:], over_e(val(0)), ALU.subtract).then_inc(to_exp.sem, 1)
                    exp_of(wide[2])
                    link(dve.tensor_reduce(thin[0][:], wide[2][:], AX_X, ALU.add))
                    link(dve.reciprocal(thin[0][:], thin[0][:]))
                    for k in range(K):
                        link(dve.tensor_tensor(wide[0][:], wide[2][:], hot[:, k], ALU.mult))
                        link(dve.tensor_reduce(ws[:, k], wide[0][:], AX_X, ALU.add))
                        link(dve.tensor_tensor(ws[:, k], ws[:, k], thin[0][:], ALU.mult))
                    link(dve.tensor_tensor(thin[1][:], ws[:, 0], ws[:, 1], ALU.add))
                    link(dve.tensor_tensor(thin[1][:], thin[1][:], ws[:, 2], ALU.add))
                    link(dve.tensor_scalar(thin[1][:], thin[1][:], 1e-20, None, ALU.add))
                    link(dve.reciprocal(thin[1][:], thin[1][:]))
                    for k in range(K):
                        last = dve.tensor_tensor(ws[:, k], ws[:, k], thin[1][:], ALU.mult)
                    link(last)
                if chosen is None:
                    for k in range(K):
                        last = dve.tensor_tensor(wide[k][:], hot[:, k], over_e(ws[:, k]), ALU.mult)
                    link(last)
                    if K == 3:
                        link(dve.tensor_tensor(wide[1][:], wide[1][:], wide[2][:], ALU.add))
                    link(dve.tensor_tensor(g[:, 0:E, :].rearrange("p e t -> p t e"), wide[0][:], wide[1][:],
                                           ALU.add))
                counts.update(step=n, exps=exps)

            @block.scalar
            def _(act):
                src, dst, sign = {"softmax": (thin[0], thin[1], 1.0), "jitter": (wide[0], wide[2], -1.0),
                                  "renormed": (wide[0], wide[2], 1.0)}[kind]
                for k in range(counts["exps"]):
                    act.wait_ge(*to_exp(k + 1))
                    act.activation(dst[:], src[:], ACT.Exp, scale=sign).then_inc(exped.sem, 1)
    stage_ends(core, loaded=16 if gate_b is None else 32, logits_full=1, dve_step=counts["step"], to_exp=counts["exps"],
             exped=counts["exps"], iotas=2 if kind == "renormed" else 1)


def mixed_biases(core, layer, E, b2):
    nc = core.nc
    loaded, turned, g_copied, mixed, acc_set = (signal(core, n) for n in
                                                ("loaded", "g_turned", "g_copied", "bias_mixed", "acc_set"))
    with ExitStack() as ctx:
        b2_sb = ctx.enter_context(nc.sbuf_tensor(f"b2_{layer}", [E, P], F32))
        g_t = ctx.enter_context(nc.sbuf_tensor(f"g_t_{layer}", [E, T], F32))
        t_ps = ctx.enter_context(nc.psum_tensor(f"g_t_ps_{layer}", [P, B, S], F32))
        m_ps = ctx.enter_context(nc.psum_tensor(f"mix_ps_{layer}", [P, B, S], F32))
        with nc.Block() as block:

            @block.sync
            def _(sp):
                sp.dma_start(b2_sb[:], b2).then_inc(loaded.sem, 16)

            @block.tensor
            def _(pe):
                for b in range(B):
                    for q in range(Q):
                        mm = pe.transpose(t_ps[0:E, b, q * P:(q + 1) * P], core.g[:, 0:E, b * Q + q], core.ident[:])
                    mm.then_inc(turned.sem, 1)
                pe.wait_ge(*loaded(16))
                for b in range(B):
                    pe.wait_ge(*g_copied(b + 1))
                    for t in range(b * Q, b * Q + Q):
                        mm = pe.matmul(m_ps[:, b, (t % Q) * P:(t % Q + 1) * P], g_t[:, t * P:(t + 1) * P], b2_sb[:],
                                       start=True, stop=True)
                    mm.then_inc(mixed.sem, 1)

            @block.scalar
            def _(act):
                for b in range(B):
                    act.wait_ge(*turned(b + 1))
                    act.copy(g_t[:, b * S:(b + 1) * S], t_ps[0:E, b, :]).then_inc(g_copied.sem, 1)

            @block.vector
            def _(dve):
                for b in range(B):
                    dve.wait_ge(*mixed(b + 1))
                    dve.tensor_copy(core.acc[:, b * Q:(b + 1) * Q, :], m_ps[:, b, :].rearrange("p (q d) -> p q d", q=Q))\
                       .then_inc(acc_set.sem, 1)
    stage_ends(core, loaded=16, g_turned=B, g_copied=B, bias_mixed=B, acc_set=B)


def experts(core, layer, E, FR, FB, func, w1, w2, b1=None, mult=None, fresh=False):
    nc = core.nc
    parts = w1.shape[2] // (FB * FR)
    glu = parts == 2
    U = B * FB
    LAG = 2
    R = 2 if glu else 4
    (up_full, gated, a_made, y_full, y_added, w2_scaled, acc_zero) = (
        signal(core, n) for n in ("up_full", "gated", "a_made", "y_full", "y_added", "w2_scaled", "acc_zero"))
    final = signal(core, "dve_step")
    wslot = [signal(core, "weights_slot0"), signal(core, "weights_slot1")]
    loads = 2 + (b1 is not None) + (mult is not None)
    head = 1 if E % 2 else 2
    with ExitStack() as ctx:
        tmp = lambda name, shape, dt=F32: ctx.enter_context(nc.sbuf_tensor(f"{name}_e{layer}", shape, dt))
        w1_s = tmp("w1_slot", [P, 2, FB * parts * FR])
        w2_s = tmp("w2_slot", [FR, 2, FB * P])
        b1_s = tmp("b1_slot", [FR, 2, FB * parts])
        mu_s = tmp("mult_slot", [FR, 2, 1])
        w2_m = tmp("w2_scaled", [FR, 2, FB * P]) if mult is not None else w2_s
        gs = tmp("gated", [FR, 2, S])
        a_s = tmp("hidden", [FR, 4, S])
        up = ctx.enter_context(nc.psum_tensor(f"up_ps_{layer}", [P, R, parts, S], F32))
        y_ps = ctx.enter_context(nc.psum_tensor(f"y_ps_{layer}", [P, 2, S], F32))
        acc = core.acc

        def run(eng, window):
            for e in range(head):
                window(e, e % 2, first=e == 0)
            with eng.Fori(0, (E - head - 2) // 2) as i:
                window(2 * i + head, head % 2)
                window(2 * i + head + 1, 1 - head % 2)
            window(E - 2, E % 2)
            window(E - 1, 1 - E % 2, last=True)

        with nc.Block() as block:

            @block.sync
            def _(sp):
                def window(e, s, first=False, last=False):
                    if not isinstance(e, int) or e >= 2:
                        sp.wait_ge(*y_full(B * (e - 2) + B))
                    sp.dma_start(w1_s[:, s, :], w1[e, :, :]).then_inc(wslot[s].sem, 16)
                    sp.dma_start(w2_s[:, s, :], w2[e, :, :]).then_inc(wslot[s].sem, 16)
                    if b1 is not None:
                        sp.dma_start(b1_s[:, s, :], b1[e, :, :]).then_inc(wslot[s].sem, 16)
                    if mult is not None:
                        sp.dma_start(mu_s[:, s, :], mult[e, :, :]).then_inc(wslot[s].sem, 16)

                run(sp, window)

            @block.gpsimd
            def _(pool):
                if fresh:
                    pool.memset(acc[:], 0.0).then_inc(acc_zero.sem, 1)
                if mult is not None:
                    def window(e, s, first=False, last=False):
                        pool.wait_ge(*wslot[s](16 * loads * (e // 2 + 1)))
                        pool.tensor_tensor(w2_m[:, s, :], w2_s[:, s, :], mu_s[:, s, :].broadcast_to([FR, FB * P]),
                                           ALU.mult).then_inc(w2_scaled.sem, 1)
                    run(pool, window)

            @block.tensor
            def _(pe):
                def up_proj(e, s, u, first):
                    n = e * U + u
                    if u == 0:
                        pe.wait_ge(*wslot[s](16 * loads * (e // 2 + 1)))
                    if not (first and u < R):
                        pe.wait_ge(*a_made(n - R + 1))
                    c, f = divmod(u, FB)
                    for k in range(parts):
                        at = (f * parts + k) * FR
                        mm = pe.matmul(up[0:FR, u % R, k, :], w1_s[:, s, at:at + FR], core.h[:, c * S:(c + 1) * S],
                                       start=True, stop=True)
                    mm.then_inc(up_full.sem, 1)

                def down_proj(e, s, u, first):
                    n = e * U + u
                    c, f = divmod(u, FB)
                    pe.wait_ge(*a_made(n + 1))
                    if f == 0 and not (first and c < 2):
                        pe.wait_ge(*y_added(B * e + c - 1))
                    if u == 0 and mult is not None:
                        pe.wait_ge(*w2_scaled(e + 1))
                    for q in range(Q):
                        mm = pe.matmul(y_ps[:, c % 2, q * P:(q + 1) * P], a_s[:, u % 4, q * P:(q + 1) * P],
                                       w2_m[:, s, f * P:(f + 1) * P], start=f == 0 and q == 0,
                                       stop=f == FB - 1, skip_group_check=True)
                    if f == FB - 1:
                        mm.then_inc(y_full.sem, 1)

                def window(e, s, first=False, last=False):
                    for u in range(U):
                        up_proj(e, s, u, first)
                        if u >= LAG:
                            down_proj(e, s, u - LAG, first)
                        elif not first:
                            down_proj(e - 1, 1 - s, u - LAG + U, isinstance(e, int) and e == 1)
                    if last:
                        for u in range(U - LAG, U):
                            down_proj(e, s, u, False)

                run(pe, window)

            @block.scalar
            def _(act):
                def window(e, s, first=False, last=False):
                    for u in range(U):
                        n = e * U + u
                        f = u % FB
                        act.wait_ge(*up_full(n + 1))
                        if glu and not (first and u < 2):
                            act.wait_ge(*a_made(n - 2 + 1))
                        bias = b1_s[:, s, parts * f:parts * f + 1] if b1 is not None else 0.0
                        out = gs[:, u % 2, :] if glu else a_s[:, u % 4, :]
                        act.activation(out, up[0:FR, u % R, 0, :], func, bias=bias)\
                           .then_inc(gated.sem if glu else a_made.sem, 1)

                run(act, window)

            @block.vector
            def _(dve):
                def product(e, s, u):
                    f = u % FB
                    dve.wait_ge(*gated(e * U + u + 1))
                    out, lin = a_s[:, u % 4, :], up[0:FR, u % R, 1, :]
                    if b1 is None:
                        ins = dve.tensor_tensor(out, lin, gs[:, u % 2, :], ALU.mult)
                    else:
                        ins = dve.scalar_tensor_tensor(out, lin, b1_s[:, s, 2 * f + 1:2 * f + 2], gs[:, u % 2, :],
                                                       ALU.add, ALU.mult)
                    ins.then_inc(a_made.sem, 1)

                def add_y(e, c, first):
                    dve.wait_ge(*y_full(B * e + c + 1))
                    if first and c == 0 and fresh:
                        dve.wait_ge(*acc_zero(1))
                    if not first:
                        dve.wait_ge(*y_added(B * (e - 1) + c + 1))
                    for q in range(Q):
                        t = c * Q + q
                        last = dve.scalar_tensor_tensor(acc[:, t, :], y_ps[:, c % 2, q * P:(q + 1) * P],
                                                        core.g[:, e, t:t + 1], acc[:, t, :], ALU.mult, ALU.add)
                    last.then_inc(y_added.sem, 1)

                def window(e, s, first=False, last=False):
                    for u in range(U):
                        if glu:
                            product(e, s, u)
                        at = u - LAG - 1
                        if at >= 0:
                            if at % FB == FB - 1:
                                add_y(e, at // FB, first)
                        elif not first and (at + U) % FB == FB - 1:
                            add_y(e - 1, (at + U) // FB, isinstance(e, int) and e == 1)
                    if last:
                        for at in range(U - LAG - 1, U):
                            if at % FB == FB - 1:
                                add_y(e, at // FB, False)

                run(dve, window)
                dve.wait_ge(*y_added(B * E))
                for b in range(B):
                    xb, ab = core.x[:, Q * b:Q * b + Q, :], acc[:, Q * b:Q * b + Q, :]
                    dve.tensor_tensor(ab, ab, core.gate[:, layer, 1, b, :].unsqueeze(1).broadcast_to([P, Q, P]),
                                      ALU.mult).then_inc(final.sem, 1)
                for b in range(B):
                    xb, ab = core.x[:, Q * b:Q * b + Q, :], acc[:, Q * b:Q * b + Q, :]
                    dve.wait_ge(*final(b + 1))
                    dve.tensor_tensor(xb, xb, ab, ALU.add)
    stage_ends(core, up_full=E * U, a_made=E * U, y_full=E * B, y_added=E * B, dve_step=B, gated=E * U if glu else 0,
             w2_scaled=E if mult is not None else 0, acc_zero=1 if fresh else 0,
             weights_slot0=16 * loads * ((E + 1) // 2), weights_slot1=16 * loads * (E // 2))


def latents(core, wkd, bkd, out):
    nc = core.nc
    loaded, full, gelu, lat = (signal(core, n) for n in ("loaded", "lat_psum", "lat_gelu", "lat_made"))
    with ExitStack() as ctx:
        w = ctx.enter_context(nc.sbuf_tensor("wkd_sb", [P, 2, 32], F32))
        bb = ctx.enter_context(nc.sbuf_tensor("bkd_sb", [32, 2], F32))
        g = ctx.enter_context(nc.sbuf_tensor("lat_gelu_sb", [32, B, 2, S], F32))
        ps = ctx.enter_context(nc.psum_tensor("lat_ps", [32, B, 2, S], F32))
        with nc.Block() as block:

            @block.sync
            def _(sp):
                sp.dma_start(w[:], wkd.rearrange("a k n -> k a n")).then_inc(loaded.sem, 16)
                sp.dma_start(bb[:], bkd).then_inc(loaded.sem, 16)

            @block.tensor
            def _(pe):
                pe.wait_ge(*loaded(32))
                for b in range(B):
                    for a in range(2):
                        mm = pe.matmul(ps[:, b, a, :], w[:, a, :], core.h[:, b * S:(b + 1) * S], start=True, stop=True)
                    mm.then_inc(full.sem, 1)

            @block.scalar
            def _(act):
                for b in range(B):
                    act.wait_ge(*full(b + 1))
                    for a in range(2):
                        ins = act.activation(g[:, b, a, :], ps[:, b, a, :], ACT.Gelu, bias=bb[:, a:a + 1])
                    ins.then_inc(gelu.sem, 1)

            @block.vector
            def _(dve):
                for b in range(B):
                    dve.wait_ge(*gelu(b + 1))
                    dve.tensor_tensor(out[:, b * S:(b + 1) * S], g[:, b, 0, :], g[:, b, 1, :], ALU.add)\
                       .then_inc(lat.sem, 1)
    stage_ends(core, loaded=32, lat_psum=B, lat_gelu=B, lat_made=B)


def rms_norm(core, name, layer, half, eps, w, out_tok, out_feat):
    nc = core.nc
    names = ("loaded", "squared", "sq_summed", "rms_step", "rms_root", "h_turned", "h_scaled", "n_turned", "n_made")
    (loaded, squared, summed, step, root, h_turned, h_scaled, n_turned, n_made) = (signal(core, n) for n in names)
    with ExitStack() as ctx:
        tmp = lambda nm, shape, dt=F32: ctx.enter_context(nc.sbuf_tensor(f"{nm}_{name}", shape, dt))
        w_sb = tmp("rms_w", [P, 1])
        sq = tmp("rms_sq", [P, T])
        ms = tmp("rms_ms", [P, NT])
        sd = tmp("rms_sd", [P, NT])
        rs = tmp("rms_rs", [P, NT])
        hg = tmp("rms_hg", [P, 2, Q, P])
        s_ps = ctx.enter_context(nc.psum_tensor(f"rms_s_{name}", [P, NT], F32))
        h_ps = ctx.enter_context(nc.psum_tensor(f"rms_h_{name}", [P, 2, S], F32))
        n_ps = ctx.enter_context(nc.psum_tensor(f"rms_n_{name}", [P, 2, S], F32))
        with nc.Block() as block:

            @block.sync
            def _(sp):
                sp.dma_start(w_sb[:], w).then_inc(loaded.sem, 16)

            @block.scalar
            def _(act):
                act.wait_ge(*loaded(16))
                for b in range(B):
                    act.activation(sq[:, b * S:(b + 1) * S], core.h[:, b * S:(b + 1) * S], ACT.Square)\
                       .then_inc(squared.sem, 1)
                act.wait_ge(*step(1))
                act.activation(sd[:], ms[:], ACT.Sqrt).then_inc(root.sem, 1)
                for b in range(B):
                    act.wait_ge(*n_turned(b + 1))
                    act.activation(out_feat[:, b * S:(b + 1) * S], n_ps[:, b % 2, :], ACT.Copy, scale=w_sb[:, 0:1])\
                       .then_inc(n_made.sem, 1)

            def turn_back(pe, b):
                pe.wait_ge(*h_scaled(b + 1))
                if b >= 2:
                    pe.wait_ge(*n_made(b - 1))
                for q in range(Q):
                    mm = pe.transpose(n_ps[:, b % 2, q * P:(q + 1) * P], out_tok[:, b * Q + q, :], core.ident[:])
                mm.then_inc(n_turned.sem, 1)

            @block.tensor
            def _(pe):
                for b in range(B):
                    pe.wait_ge(*squared(b + 1))
                    for t in range(b * Q, b * Q + Q):
                        mm = pe.matmul(s_ps[:, t:t + 1], sq[:, t * P:(t + 1) * P], core.ones[:, 0:1], start=True,
                                       stop=True)
                mm.then_inc(summed.sem, 1)
                for b in range(B):
                    if b >= 2:
                        pe.wait_ge(*h_scaled(b - 1))
                    for q in range(Q):
                        t = b * Q + q
                        mm = pe.transpose(h_ps[:, b % 2, q * P:(q + 1) * P], core.h[:, t * P:(t + 1) * P], core.ident[:])
                    mm.then_inc(h_turned.sem, 1)
                    if b >= 1:
                        turn_back(pe, b - 1)
                turn_back(pe, B - 1)

            @block.vector
            def _(dve):
                dve.wait_ge(*summed(1))
                dve.tensor_scalar(ms[:], s_ps[:], 1.0 / P, eps, ALU.mult, ALU.add).then_inc(step.sem, 1)
                dve.wait_ge(*root(1))
                dve.reciprocal(rs[:], sd[:]).then_inc(step.sem, 1)
                dve.wait_ge(*step(2))
                for b in range(B):
                    dve.wait_ge(*h_turned(b + 1))
                    h3 = h_ps[:, b % 2, :].rearrange("p (q d) -> p q d", q=Q)
                    dve.tensor_tensor(hg[:, b % 2], h3, core.gate[:, layer, half, b, :].unsqueeze(1)
                                      .broadcast_to([P, Q, P]), ALU.mult).then_inc(step.sem, 1)
                    dve.tensor_tensor(out_tok[:, b * Q:b * Q + Q, :], h3,
                                      rs[:, b * Q:b * Q + Q].unsqueeze(2).broadcast_to([P, Q, P]), ALU.mult)\
                       .then_inc(h_scaled.sem, 1)
                    dve.wait_ge(*step(3 + b))
                    xb = core.x[:, b * Q:b * Q + Q, :]
                    dve.tensor_tensor(xb, xb, hg[:, b % 2], ALU.add)
    stage_ends(core, loaded=16, squared=B, sq_summed=1, rms_step=2 + B, rms_root=1, h_turned=B, h_scaled=B, n_turned=B,
             n_made=B)


def gated_scan(core, layer, xn, w_in, b_in, w_x, w_dt, b_xdt, w_out, b_out):
    nc = core.nc
    H = 64
    names = ("loaded", "p_full", "z_made", "u_made", "sg_made", "ud_full", "ut_made", "dt_made", "scan_step", "y_made",
             "out_full", "out_added")
    (loaded, p_full, z_made, u_made, sg_made, ud_full, ut_made, dt_made, step, y_made, out_full, out_added) = (
        signal(core, n) for n in names)
    with ExitStack() as ctx:
        tmp = lambda nm, shape, dt=F32: ctx.enter_context(nc.sbuf_tensor(f"gs_{nm}", shape, dt))
        win = tmp("w_in", [P, 3 * H])
        bin_ = tmp("b_in", [H, 3])
        wx, wdt = tmp("w_x", [H, H]), tmp("w_dt", [H, H])
        bx = tmp("b_xdt", [H, 2])
        wout = tmp("w_out", [H, P])
        bout = tmp("b_out", [1, P])
        u, z, sg, ut, dt, a, bb, h, y = (tmp(n, [H, 2, S]) for n in "u z sg ut dt a b h y".split())
        og = tmp("og", [P, 2, Q, P])
        p_ps = ctx.enter_context(nc.psum_tensor("gs_p", [H, 3, S], F32))
        ud_ps = ctx.enter_context(nc.psum_tensor("gs_ud", [H, 2, S], F32))
        o_ps = ctx.enter_context(nc.psum_tensor("gs_o", [P, 2, S], F32))
        with nc.Block() as block:

            @block.sync
            def _(sp):
                for dst, src in ((win, w_in), (bin_, b_in), (wx, w_x), (wdt, w_dt), (bx, b_xdt), (wout, w_out),
                                 (bout, b_out)):
                    sp.dma_start(dst[:], src).then_inc(loaded.sem, 16)

            @block.tensor
            def _(pe):
                def project_in(b):
                    if b:
                        pe.wait_ge(*u_made(b))
                        pe.wait_ge(*z_made(b))
                        pe.wait_ge(*sg_made(b))
                    for k in range(3):
                        mm = pe.matmul(p_ps[:, k, :], win[:, k * H:(k + 1) * H], xn[:, b * S:(b + 1) * S], start=True,
                                       stop=True)
                    mm.then_inc(p_full.sem, 1)

                pe.wait_ge(*loaded(16 * 7))
                project_in(0)
                for b in range(B):
                    pe.wait_ge(*u_made(b + 1))
                    pe.wait_ge(*z_made(b + 1))
                    if b:
                        pe.wait_ge(*ut_made(b))
                        pe.wait_ge(*dt_made(b))
                    pe.matmul(ud_ps[:, 0, :], wx[:], u[:, b % 2, :], start=True, stop=True)
                    pe.matmul(ud_ps[:, 1, :], wdt[:], z[:, b % 2, :], start=True, stop=True).then_inc(ud_full.sem, 1)
                    if b + 1 < B:
                        project_in(b + 1)
                    pe.wait_ge(*y_made(b + 1))
                    if b >= 2:
                        pe.wait_ge(*out_added(b - 1))
                    for q in range(Q):
                        at = slice(q * P, (q + 1) * P)
                        pe.matmul(o_ps[:, b % 2, at], core.ones[0:1, :], bout[:], start=True, stop=False)
                        mm = pe.matmul(o_ps[:, b % 2, at], y[:, b % 2, at], wout[:], start=False, stop=True)
                    mm.then_inc(out_full.sem, 1)

            @block.scalar
            def _(act):
                act.wait_ge(*loaded(16 * 7))
                for b in range(B):
                    act.wait_ge(*p_full(b + 1))
                    act.activation(u[:, b % 2, :], p_ps[:, 0, :], ACT.Identity, bias=bin_[:, 0:1]).then_inc(u_made.sem, 1)
                    if b >= 2:
                        act.wait_ge(*y_made(b - 1))
                    act.activation(sg[:, b % 2, :], p_ps[:, 2, :], ACT.Sigmoid, bias=bin_[:, 2:3])\
                       .then_inc(sg_made.sem, 1)
                    act.wait_ge(*ud_full(b + 1))
                    act.activation(ut[:, b % 2, :], ud_ps[:, 0, :], ACT.Tanh, bias=bx[:, 0:1]).then_inc(ut_made.sem, 1)
                    act.activation(dt[:, b % 2, :], ud_ps[:, 1, :], ACT.Sigmoid, bias=bx[:, 1:2])\
                       .then_inc(dt_made.sem, 1)

            @block.vector
            def _(dve):
                dve.wait_ge(*loaded(16 * 7))
                n = 0
                for b in range(B):
                    k = b % 2
                    dve.wait_ge(*p_full(b + 1))
                    dve.tensor_scalar(z[:, k, :], p_ps[:, 1, :], bin_[:, 1:2], None, ALU.add).then_inc(z_made.sem, 1)
                    dve.wait_ge(*ut_made(b + 1))
                    dve.wait_ge(*dt_made(b + 1))
                    dve.tensor_scalar(a[:, k, :], dt[:, k, :], -1.0, 1.0, ALU.mult, ALU.add).then_inc(step.sem, 1)
                    dve.tensor_tensor(bb[:, k, :], dt[:, k, :], ut[:, k, :], ALU.mult).then_inc(step.sem, 1)
                    dve.wait_ge(*step(n + 2))
                    dve.tensor_tensor_scan(h[:, k, :], a[:, k, :], bb[:, k, :], 0.0, ALU.mult, ALU.add)\
                       .then_inc(step.sem, 1)
                    dve.wait_ge(*step(n + 3))
                    dve.wait_ge(*sg_made(b + 1))
                    dve.tensor_tensor(y[:, k, :], h[:, k, :], sg[:, k, :], ALU.mult).then_inc(y_made.sem, 1)
                    dve.wait_ge(*out_full(b + 1))
                    dve.tensor_tensor(og[:, k], o_ps[:, k, :].rearrange("p (q d) -> p q d", q=Q),
                                      core.gate[:, layer, 0, b, :].unsqueeze(1).broadcast_to([P, Q, P]), ALU.mult)\
                       .then_inc(out_added.sem, 1)
                    dve.wait_ge(*out_added(b + 1))
                    xb = core.x[:, b * Q:b * Q + Q, :]
                    dve.tensor_tensor(xb, xb, og[:, k], ALU.add)
                    n += 3
    stage_ends(core, loaded=112, p_full=B, z_made=B, u_made=B, sg_made=B, ud_full=B, ut_made=B, dt_made=B, scan_step=3 * B,
             y_made=B, out_full=B, out_added=B)


def dispatch(core, hot, ws, idx_f, slot, tokens):
    nc = core.nc
    step, tri_set, m_set, r_set, pos_full, slot_set, scattered = (signal(core, n) for n in (
        "dve_step", "tri_set", "m_set", "r_set", "pos_full", "slot_set", "scattered"))
    zeroed = signal(core, "slots_zeroed")
    E = L3_E
    counts = {}
    with ExitStack() as ctx:
        tmp = lambda name, shape, dt=F32: ctx.enter_context(nc.sbuf_tensor(f"d_{name}", shape, dt))
        tri = tmp("tri", [P, P], BF16)
        ones = tmp("ones", [P, P], BF16)
        m = tmp("m", [P, NT, E], BF16)
        before = tmp("before", [P, NT, E], BF16)
        wide = tmp("wide", [P, NT, E])
        pos = tmp("pos", [P, 2, NT])
        over = tmp("over", [P, 2, NT])
        slot_f = tmp("slot_f", [P, 2, NT])
        ps = ctx.enter_context(nc.psum_tensor("pos_ps", [P, NT, E], F32))
        with nc.Block() as block:

            @block.gpsimd
            def _(pool):
                pool.memset(ones[:], 1.0).then_inc(tri_set.sem, 1)
                pool.wait_ge(*tri_set(1))
                pool.affine_select(out=tri[:], in_=ones[:], compare_op=ALU.is_gt, fill=0.0, base=0, pattern=[[1, P]],
                                   channel_multiplier=-1).then_inc(tri_set.sem, 1)
                pool.wait_ge(*zeroed(16 * ZERO_FILLS))
                pool.wait_ge(*slot_set(1))
                for k in range(2):
                    for t in range(NT):
                        pool.indirect_dma_start(out=core.slots_in,
                                                out_offset=bass.IndirectOffsetOnAxis(ap=slot[:, k, t:t + 1], axis=0),
                                                in_=tokens[:, t, :], in_offset=None, bounds_check=L3_SLOTS - 1,
                                                oob_is_err=False).then_inc(scattered.sem, 16)
                pool.wait_ge(*scattered(16 * 2 * NT))

            @block.tensor
            def _(pe):
                pe.wait_ge(*tri_set(2))
                pe.wait_ge(*m_set(1))
                pe.wait_ge(*r_set(NT))
                for t in range(NT):
                    pe.matmul(ps[:, t, :], tri[:], m[:, t, :], start=True, stop=False)
                    mm = pe.matmul(ps[:, t, :], ones[:], before[:, t, :], start=False, stop=True)
                mm.then_inc(pos_full.sem, 1)

            @block.vector
            def _(dve):
                n = 0

                def link(ins):
                    nonlocal n
                    n += 1
                    ins.then_inc(step.sem, 1)
                    dve.wait_ge(*step(n))

                dve.tensor_tensor(m[:], hot[:, 0], hot[:, 1], ALU.add).then_inc(m_set.sem, 1)
                dve.memset(before[:, 0, :], 0.0).then_inc(r_set.sem, 1)
                dve.wait_ge(*m_set(1))
                for t in range(1, NT):
                    dve.wait_ge(*r_set(t))
                    dve.tensor_tensor(before[:, t, :], before[:, t - 1, :], m[:, t - 1, :], ALU.add)\
                       .then_inc(r_set.sem, 1)
                dve.wait_ge(*pos_full(1))
                for k in range(2):
                    link(dve.tensor_tensor(wide[:], ps[:], hot[:, k], ALU.mult))
                    link(dve.tensor_reduce(pos[:, k, :], wide[:], AX_X, ALU.add))
                link(dve.tensor_scalar(over[:], pos[:], float(CAP), None, ALU.is_lt))
                link(dve.tensor_tensor(ws[:], ws[:], over[:], ALU.mult))
                for k in range(2):
                    last = dve.tensor_scalar(slot_f[:, k, :], idx_f[:, :, k], float(CAP), None, ALU.mult)
                link(last)
                link(dve.tensor_tensor(slot_f[:], slot_f[:], pos[:], ALU.add))
                link(dve.tensor_scalar(over[:], pos[:], float(CAP), float(4 * L3_SLOTS), ALU.is_ge, ALU.mult))
                link(dve.tensor_tensor(slot_f[:], slot_f[:], over[:], ALU.add))
                dve.tensor_copy(slot[:], slot_f[:]).then_inc(slot_set.sem, 1)
                counts.update(step=n)
    stage_ends(core, dve_step=counts["step"], tri_set=2, m_set=1, r_set=NT, pos_full=1, slot_set=1, scattered=32 * NT,
             slots_zeroed=16 * ZERO_FILLS)


def slot_experts(core, rms_w, w13, w2):
    nc = core.nc
    G = 4
    NW = L3_E // G
    RING = 4
    H = 64
    names = ("loaded", "xb_turned", "xt_made", "gu_full", "silu_made", "hh_made", "yb_full", "yb_copied")
    (loaded, xb_turned, xt_made, gu_full, silu_made, hh_made, yb_full, yb_copied) = (signal(core, n) for n in names)
    ring = [signal(core, f"ring_slot{k}") for k in range(RING)]
    stored = [signal(core, "stored_even"), signal(core, "stored_odd")]
    src = core.slots_in.rearrange("(w j p) d -> w p j d", j=G, p=P)
    dst = core.slots_out.rearrange("(w j p) d -> w p j d", j=G, p=P)
    w13_v = w13.rearrange("(w j) k n -> w k j n", j=G)
    w2_v = w2.rearrange("(w j) k n -> w k j n", j=G)
    with ExitStack() as ctx:
        tmp = lambda name, shape, dt=F32: ctx.enter_context(nc.sbuf_tensor(f"se_{name}", shape, dt))
        rw = tmp("rms_w", [P, 1])
        xb = tmp("xb", [P, RING, G, P])
        w13_s = tmp("w13", [P, RING, G, P])
        w2_s = tmp("w2", [H, RING, G, P])
        xt = tmp("xt", [P, 2, S])
        sg = tmp("sg", [H, 2, S])
        hh = tmp("hh", [H, 2, S])
        y = tmp("y", [P, 2, G, P])
        t_ps = ctx.enter_context(nc.psum_tensor("se_t", [P, 2, S], F32))
        gu_ps = ctx.enter_context(nc.psum_tensor("se_gu", [H, 2, 2, S], F32))
        y_ps = ctx.enter_context(nc.psum_tensor("se_y_ps", [P, 2, S], F32))

        def run(eng, window):
            for i in range(RING):
                window(i, i)
            with eng.Fori(1, NW // RING) as r:
                for k in range(RING):
                    window(r * RING + k, k)
            for i in range(NW, NW + 2):
                window(i, i % RING)

        new = lambda i: not isinstance(i, int) or i < NW
        old = lambda i, n: not isinstance(i, int) or i >= n
        with nc.Block() as block:

            @block.sync
            def _(sp):
                sp.dma_start(rw[:], rms_w).then_inc(loaded.sem, 16)

                def window(i, k):
                    if new(i):
                        if old(i, RING):
                            sp.wait_ge(*yb_full(i - RING + 1))
                        sp.dma_start(xb[:, k], src[i]).then_inc(ring[k].sem, 16)
                        sp.dma_start(w13_s[:, k], w13_v[i]).then_inc(ring[k].sem, 16)
                        sp.dma_start(w2_s[:, k], w2_v[i]).then_inc(ring[k].sem, 16)

                run(sp, window)

            @block.tensor
            def _(pe):
                def window(i, k):
                    if new(i):
                        pe.wait_ge(*ring[k](48 * (i // RING + 1)))
                        if old(i, 2):
                            pe.wait_ge(*xt_made(i - 1))
                        for j in range(G):
                            mm = pe.transpose(t_ps[:, k % 2, j * P:(j + 1) * P], xb[:, k, j, :], core.ident[:])
                        mm.then_inc(xb_turned.sem, 1)
                    if old(i, 1) and (not isinstance(i, int) or i - 1 < NW):
                        kk = (k - 1) % RING
                        pe.wait_ge(*xt_made(i))
                        if old(i, 3):
                            pe.wait_ge(*hh_made(i - 2))
                        for j in range(G):
                            at = slice(j * P, (j + 1) * P)
                            for part in range(2):
                                mm = pe.matmul(gu_ps[:, kk % 2, part, at], w13_s[:, kk, j, part * H:(part + 1) * H],
                                               xt[:, kk % 2, at], start=True, stop=True)
                        mm.then_inc(gu_full.sem, 1)
                    if old(i, 2):
                        kk = (k - 2) % RING
                        pe.wait_ge(*hh_made(i - 1))
                        if old(i, 4):
                            pe.wait_ge(*yb_copied(i - 3))
                        for j in range(G):
                            at = slice(j * P, (j + 1) * P)
                            mm = pe.matmul(y_ps[:, kk % 2, at], hh[:, kk % 2, at], w2_s[:, kk, j, :], start=True,
                                           stop=True)
                        mm.then_inc(yb_full.sem, 1)

                run(pe, window)

            @block.scalar
            def _(act):
                def window(i, k):
                    if new(i):
                        act.wait_ge(*xb_turned(i + 1))
                        if old(i, 2):
                            act.wait_ge(*gu_full(i - 1))
                        act.activation(xt[:, k % 2, :], t_ps[:, k % 2, :], ACT.Copy, scale=rw[:, 0:1])\
                           .then_inc(xt_made.sem, 1)
                    if old(i, 1) and (not isinstance(i, int) or i - 1 < NW):
                        kk = (k - 1) % RING
                        act.wait_ge(*gu_full(i))
                        act.activation(sg[:, kk % 2, :], gu_ps[:, kk % 2, 0, :], ACT.Silu).then_inc(silu_made.sem, 1)

                act.wait_ge(*loaded(16))
                run(act, window)

            @block.vector
            def _(dve):
                def window(i, k):
                    if old(i, 1) and (not isinstance(i, int) or i - 1 < NW):
                        kk = (k - 1) % RING
                        dve.wait_ge(*silu_made(i))
                        if old(i, 3):
                            dve.wait_ge(*yb_full(i - 2))
                        dve.tensor_tensor(hh[:, kk % 2, :], sg[:, kk % 2, :], gu_ps[:, kk % 2, 1, :], ALU.mult)\
                           .then_inc(hh_made.sem, 1)
                    if old(i, 2):
                        kk = (k - 2) % RING
                        dve.wait_ge(*yb_full(i - 1))
                        if old(i, 4):
                            dve.wait_ge(*stored[kk % 2](16 * ((i - 2) // 2)))
                        dve.tensor_copy(y[:, kk % 2], y_ps[:, kk % 2, :].rearrange("p (j d) -> p j d", j=G))\
                           .then_inc(yb_copied.sem, 1)

                run(dve, window)

            @block.gpsimd
            def _(pool):
                def window(i, k):
                    if old(i, 2):
                        kk = (k - 2) % RING
                        pool.wait_ge(*yb_copied(i - 1))
                        pool.dma_start(dst[i - 2], y[:, kk % 2]).then_inc(stored[kk % 2].sem, 16)

                run(pool, window)
                for s in stored:
                    pool.wait_ge(*s(16 * NW // 2))
    stage_ends(core, loaded=16, xb_turned=NW, xt_made=NW, gu_full=NW, silu_made=NW, hh_made=NW, yb_full=NW, yb_copied=NW,
             ring_slot0=12 * NW, ring_slot1=12 * NW, ring_slot2=12 * NW, ring_slot3=12 * NW,
             stored_even=8 * NW, stored_odd=8 * NW)


def combine(core, xn, ws, slot, w_gate, w_up, w_down):
    nc = core.nc
    H = 64
    names = ("loaded", "y_cleared", "gu_full", "silu_made", "hh_made", "shared_full", "mix_step")
    (loaded, cleared, gu_full, silu_made, hh_made, shared_full, step) = (signal(core, n) for n in names)
    gathered = [signal(core, f"gathered{b}") for b in range(B)]
    with ExitStack() as ctx:
        tmp = lambda name, shape, dt=F32: ctx.enter_context(nc.sbuf_tensor(f"cm_{name}", shape, dt))
        wg, wu = tmp("w_gate", [P, H]), tmp("w_up", [P, H])
        wd = tmp("w_down", [H, P])
        y = tmp("y", [P, 2, NT, P])
        sg, hh = tmp("sg", [H, 2, S]), tmp("hh", [H, 2, S])
        acc = tmp("acc", [P, NT, P])
        gu = ctx.enter_context(nc.psum_tensor("cm_gu", [H, 2, 2, S], F32))
        sh = ctx.enter_context(nc.psum_tensor("cm_sh", [P, B, S], F32))
        with nc.Block() as block:

            @block.sync
            def _(sp):
                for dst, src in ((wg, w_gate), (wu, w_up), (wd, w_down)):
                    sp.dma_start(dst[:], src).then_inc(loaded.sem, 16)

            @block.gpsimd
            def _(pool):
                pool.memset(y[:], 0.0).then_inc(cleared.sem, 1)
                pool.wait_ge(*cleared(1))
                for t in range(NT):
                    for k in range(2):
                        pool.indirect_dma_start(out=y[:, k, t, :], out_offset=None, in_=core.slots_out,
                                                in_offset=bass.IndirectOffsetOnAxis(ap=slot[:, k, t:t + 1], axis=0),
                                                bounds_check=L3_SLOTS - 1, oob_is_err=False)\
                            .then_inc(gathered[t // Q].sem, 16)

            @block.tensor
            def _(pe):
                def up(b):
                    if b >= 2:
                        pe.wait_ge(*hh_made(b - 1))
                    pe.matmul(gu[:, b % 2, 0, :], wg[:], xn[:, b * S:(b + 1) * S], start=True, stop=True)
                    pe.matmul(gu[:, b % 2, 1, :], wu[:], xn[:, b * S:(b + 1) * S], start=True, stop=True)\
                      .then_inc(gu_full.sem, 1)

                pe.wait_ge(*loaded(48))
                up(0)
                for b in range(B):
                    if b + 1 < B:
                        up(b + 1)
                    pe.wait_ge(*hh_made(b + 1))
                    for q in range(Q):
                        mm = pe.matmul(sh[:, b, q * P:(q + 1) * P], hh[:, b % 2, q * P:(q + 1) * P], wd[:], start=True,
                                       stop=True)
                    mm.then_inc(shared_full.sem, 1)

            @block.scalar
            def _(act):
                for b in range(B):
                    act.wait_ge(*gu_full(b + 1))
                    act.activation(sg[:, b % 2, :], gu[:, b % 2, 0, :], ACT.Silu).then_inc(silu_made.sem, 1)

            @block.vector
            def _(dve):
                for b in range(B):
                    dve.wait_ge(*silu_made(b + 1))
                    if b >= 2:
                        dve.wait_ge(*shared_full(b - 1))
                    dve.tensor_tensor(hh[:, b % 2, :], sg[:, b % 2, :], gu[:, b % 2, 1, :], ALU.mult)\
                       .then_inc(hh_made.sem, 1)
                n = 0
                for b in range(B):
                    dve.wait_ge(*shared_full(b + 1))
                    dve.wait_ge(*gathered[b](16 * 2 * Q))
                    for k in range(2):
                        for q in range(Q):
                            t = b * Q + q
                            base = sh[:, b, q * P:(q + 1) * P] if k == 0 else acc[:, t, :]
                            last = dve.scalar_tensor_tensor(acc[:, t, :], y[:, k, t, :], ws[:, k, t:t + 1], base, ALU.mult,
                                                            ALU.add)
                        last.then_inc(step.sem, 1)
                        n += 1
                        dve.wait_ge(*step(n))
                    ab, xb = acc[:, b * Q:b * Q + Q, :], core.x[:, b * Q:b * Q + Q, :]
                    dve.tensor_tensor(ab, ab, core.gate[:, 3, 1, b, :].unsqueeze(1).broadcast_to([P, Q, P]), ALU.mult)\
                       .then_inc(step.sem, 1)
                    n += 1
                    dve.wait_ge(*step(n))
                    dve.tensor_tensor(xb, xb, ab, ALU.add)
    stage_ends(core, loaded=48, y_cleared=1, gu_full=B, silu_made=B, hh_made=B, shared_full=B, mix_step=3 * B,
             **{f"gathered{b}": 32 * Q for b in range(B)})


INS = {
    "x": lambda a: a["L0_attn_x"],
    "ct": lambda a: np.concatenate([a[f"L{l}_c"] for l in range(LAYERS)], 0).T,
    "wmod": lambda a: np.stack([a[f"L{l}_wmod"].reshape(P, 6, P) for l in range(LAYERS)], 1),
    "l0_wq": lambda a: by_groups(a["L0_attn_Wq"], 8),
    "l0_wk": lambda a: by_groups(a["L0_attn_Wk"], 8),
    "l0_wv": lambda a: a["L0_attn_Wv"],
    "l0_wo": lambda a: a["L0_attn_Wo"].reshape(8, P, P),
    "l0_bo": lambda a: a["L0_attn_bo"].reshape(1, P),
    "l0_gw": lambda a: a["L0_ffn_gate_w"],
    "l0_gb": lambda a: a["L0_ffn_gate_b"].reshape(1, 8),
    "l0_w1": lambda a: a["L0_ffn_W1"],
    "l0_b1": lambda a: a["L0_ffn_b1"].reshape(8, 4, P).transpose(0, 2, 1),
    "l0_w2": lambda a: by_rows(a["L0_ffn_W2"], 4),
    "l0_b2": lambda a: a["L0_ffn_b2"],
    "l1_wq": lambda a: spread_heads(a["L1_attn_Wq"]),
    "l1_bq": lambda a: spread_heads(a["L1_attn_bq"].reshape(1, P))[:, 0, :].T,
    "l1_wkd": lambda a: a["L1_attn_Wkd"].reshape(P, 2, 32).transpose(1, 0, 2),
    "l1_bkd": lambda a: a["L1_attn_bkd"].reshape(2, 32).T,
    "l1_wku": lambda a: spread_heads(a["L1_attn_Wku"][:, :P]),
    "l1_bku": lambda a: spread_heads(a["L1_attn_bku"][:P].reshape(1, P))[:, 0, :].T,
    "l1_wv": lambda a: a["L1_attn_Wku"][:, P:],
    "l1_bv": lambda a: a["L1_attn_bku"][P:].reshape(1, P),
    "l1_wo": lambda a: a["L1_attn_Wo"].reshape(4, 32, P),
    "l1_bo": lambda a: a["L1_attn_bo"].reshape(1, P),
    "l1_gw": lambda a: a["L1_ffn_gate_w"].T,
    "l1_w1": lambda a: two_parts(a["L1_ffn_w1"], a["L1_ffn_w3"], 4),
    "l1_w2": lambda a: by_rows(a["L1_ffn_w2"].transpose(0, 2, 1), 4),
    "l2_nw": lambda a: a["L2_attn_norm_w"].reshape(P, 1),
    "l2_win": lambda a: a["L2_attn_W_in"],
    "l2_bin": lambda a: a["L2_attn_b_in"].reshape(3, 64).T,
    "l2_wx": lambda a: a["L2_attn_W_x"],
    "l2_wdt": lambda a: a["L2_attn_W_dt"],
    "l2_bxdt": lambda a: np.stack([a["L2_attn_b_x"], a["L2_attn_b_dt"]], 1),
    "l2_wout": lambda a: a["L2_attn_W_out"],
    "l2_bout": lambda a: a["L2_attn_b_out"].reshape(1, P),
    "l2_gw": lambda a: a["L2_ffn_gate_w"].T,
    "l2_w1": lambda a: two_parts(
        np.concatenate([a["L2_ffn_fc1_w"][:, P:], a["L2_ffn_s_fc1_w"][2 * P:].reshape(2, P, P)]),
        np.concatenate([a["L2_ffn_fc1_w"][:, :P], a["L2_ffn_s_fc1_w"][:2 * P].reshape(2, P, P)]), 1),
    "l2_b1": lambda a: np.stack([
        np.concatenate([a["L2_ffn_fc1_b"][:, P:], a["L2_ffn_s_fc1_b"][2 * P:].reshape(2, P)]),
        np.concatenate([a["L2_ffn_fc1_b"][:, :P], a["L2_ffn_s_fc1_b"][:2 * P].reshape(2, P)])], 2),
    "l2_mult": lambda a: np.concatenate([a["L2_ffn_geglu_mult"], a["L2_ffn_s_geglu_mult"].reshape(2, P)])[:, :, None],
    "l2_w2": lambda a: np.concatenate([a["L2_ffn_fc2_w"].transpose(0, 2, 1),
                                       a["L2_ffn_s_fc2_w"].T.reshape(2, P, P)]),
    "l2_b2": lambda a: np.concatenate([a["L2_ffn_fc2_b"], a["L2_ffn_s_fc2_b"].reshape(1, P),
                                       np.zeros((1, P), np.float32)]),
    "l3_wq": lambda a: by_groups(a["L3_attn_Wq"], 8),
    "l3_wk": lambda a: by_groups(a["L3_attn_Wk"], 8),
    "l3_wv": lambda a: a["L3_attn_Wv"],
    "l3_wo": lambda a: a["L3_attn_Wo"].reshape(8, P, P),
    "l3_bo": lambda a: a["L3_attn_bo"].reshape(1, P),
    "l3_rw": lambda a: a["L3_ffn_rms_w"].reshape(P, 1),
    "l3_gw": lambda a: a["L3_ffn_gate_w"].T,
    "l3_w13": lambda a: a["L3_ffn_w13"],
    "l3_w2": lambda a: a["L3_ffn_w2"],
    "l3_sg": lambda a: a["L3_ffn_sw_gate"],
    "l3_su": lambda a: a["L3_ffn_sw_up"],
    "l3_sd": lambda a: a["L3_ffn_sw_down"],
}


def by_groups(w, groups):
    return w.reshape(w.shape[0], groups, -1).transpose(1, 0, 2)


def by_rows(w, blocks):
    e, f, n = w.shape
    return w.reshape(e, blocks, f // blocks, n).transpose(0, 2, 1, 3).reshape(e, f // blocks, blocks * n)


def two_parts(first, second, blocks):
    e, f, k = first.shape
    both = np.stack([w.reshape(e, blocks, f // blocks, k) for w in (first, second)], 2)
    return both.transpose(0, 4, 1, 2, 3).reshape(e, k, 2 * f)


def spread_heads(w):
    k = w.shape[0]
    out = np.zeros((k, 4, 4, 32), np.float32)
    out[:, :, :, :8] = w.reshape(k, 4, 4, 8)
    return out.transpose(1, 0, 2, 3).reshape(4, k, P)


def build(nc, d, out, stages=None):
    on = lambda s: stages is None or s in stages
    with ExitStack() as ctx:
        core = Core(nc, ctx)
        setup(core, d["x"], d["ct"], d["wmod"])
        if on("a0"):
            layer_norm(core, 0, 0)
            with nc.sbuf_tensor("v0", [P, NT, HEADS * 64], F32) as core.v:
                values(core, "l0", core.h, d["l0_wv"], None, HEADS * 64)
                attention(core, 0, 8, 64, False, core.h, d["l0_wq"], d["l0_wk"], d["l0_wo"], d["l0_bo"],
                          q_scale=64 ** -0.5)
        if on("f0"):
            layer_norm(core, 0, 1)
            with nc.sbuf_tensor("g0", [P, 8, NT], F32) as core.g, nc.sbuf_tensor("acc0", [P, NT, P], F32) as core.acc:
                route(core, 0, 8, d["l0_gw"], d["l0_gb"], "softmax")
                mixed_biases(core, 0, 8, d["l0_b2"])
                experts(core, 0, 8, P, 4, ACT.Silu, d["l0_w1"], d["l0_w2"], b1=d["l0_b1"])
        if on("a1"):
            layer_norm(core, 1, 0)
            with nc.sbuf_tensor("v1", [P, NT, P], F32) as core.v, nc.sbuf_tensor("lat", [32, T], F32) as lat:
                latents(core, d["l1_wkd"], d["l1_bkd"], lat)
                values(core, "l1", lat, d["l1_wv"], d["l1_bv"], P)
                attention(core, 1, 4, 8, True, lat, d["l1_wq"], d["l1_wku"], d["l1_wo"], d["l1_bo"],
                          q_bias=d["l1_bq"], k_bias=d["l1_bku"], k_scale=8 ** -0.5)
        if on("f1"):
            layer_norm(core, 1, 1)
            with nc.sbuf_tensor("g1", [P, 8, NT], F32) as core.g, nc.sbuf_tensor("acc1", [P, NT, P], F32) as core.acc:
                route(core, 1, 8, d["l1_gw"], None, "jitter")
                experts(core, 1, 8, 112, 4, ACT.Silu, d["l1_w1"], d["l1_w2"], fresh=True)
        if on("a2"):
            layer_norm(core, 2, 0)
            with nc.sbuf_tensor("xn2", [P, T], F32) as xn, nc.sbuf_tensor("xnt2", [P, NT, P], F32) as xn_tok:
                rms_norm(core, "l2", 2, 0, 1e-8, d["l2_nw"], xn_tok, xn)
                gated_scan(core, 2, xn, d["l2_win"], d["l2_bin"], d["l2_wx"], d["l2_wdt"], d["l2_bxdt"], d["l2_wout"],
                           d["l2_bout"])
        if on("f2"):
            layer_norm(core, 2, 1)
            with nc.sbuf_tensor("g2", [P, 17, NT], F32) as core.g, nc.sbuf_tensor("acc2", [P, NT, P], F32) as core.acc:
                route(core, 2, 15, d["l2_gw"], None, "renormed")
                mixed_biases(core, 2, 17, d["l2_b2"])
                experts(core, 2, 17, P, 1, ACT.Gelu, d["l2_w1"], d["l2_w2"], b1=d["l2_b1"], mult=d["l2_mult"])
        if on("a3"):
            layer_norm(core, 3, 0)
            with nc.sbuf_tensor("v3", [P, NT, HEADS * 64], F32) as core.v:
                values(core, "l3", core.h, d["l3_wv"], None, HEADS * 64)
                attention(core, 3, 8, 64, True, core.h, d["l3_wq"], d["l3_wk"], d["l3_wo"], d["l3_bo"],
                          q_scale=64 ** -0.5)
        if on("f3"):
            layer_norm(core, 3, 1)
            with ExitStack() as half:
                sb = lambda name, shape, dt=F32: half.enter_context(nc.sbuf_tensor(name, shape, dt))
                xn, xn_tok = sb("xn3", [P, T]), sb("xnt3", [P, NT, P])
                hot, ws, idx_f = sb("hot3", [P, 2, NT, L3_E]), sb("ws3", [P, 2, NT]), sb("idx3", [P, NT, 8])
                slot = sb("slot3", [P, 2, NT], U32)
                rms_norm(core, "l3", 3, 1, 1e-6, d["l3_rw"], xn_tok, xn)
                route(core, 3, L3_E, d["l3_gw"], None, "softmax", source=xn, chosen=(hot, ws, idx_f))
                dispatch(core, hot, ws, idx_f, slot, xn_tok)
                slot_experts(core, d["l3_rw"], d["l3_w13"], d["l3_w2"])
                combine(core, xn, ws, slot, d["l3_sg"], d["l3_su"], d["l3_sd"])
        store(core, out)


def store(core, out):
    nc = core.nc
    stored = signal(core, "stored")
    with nc.Block() as block:

        @block.sync
        def _(sp):
            sp.dma_start(out.rearrange("b (q p) d -> p (b q) d", p=P), core.x[:]).then_inc(stored.sem, 16)
            sp.wait_ge(*stored(16))


def kernel(**inputs):
    import concourse.bacc as bacc
    from concourse.bass_utils import run_bass_kernel_spmd

    nc = bacc.Bacc("TRN2", target_bir_lowering=False, num_devices=1)
    arrays, d = {}, {}
    for name, layout in INS.items():
        arrays[name] = np.ascontiguousarray(layout(inputs))
        d[name] = nc.dram_tensor(name, arrays[name].shape, F32, kind="ExternalInput").ap()
    out = nc.dram_tensor("out", (B, S, P), F32, kind="ExternalOutput").ap()
    build(nc, d, out)
    r = run_bass_kernel_spmd(nc, [arrays], core_ids=[0])
    return r.results[0]["out"]
```

```python
from contextlib import ExitStack, contextmanager

import concourse.bass as bass
from concourse import mybir
import numpy as np

ALU = mybir.AluOpType
ACT = mybir.ActivationFunctionType
F32 = mybir.dt.float32
F32R = mybir.dt.float32r
BF16 = mybir.dt.bfloat16
I32 = mybir.dt.int32
U32 = mybir.dt.uint32
AX_X = mybir.AxisListType.X

P = 128
B = 4
S = 512
Q = S // P
NT = B * Q
T = B * S
LAYERS = 4
HEADS = 16
L3_E, CAP = 64, 128
L3_SLOTS = L3_E * CAP
ZERO_FILLS = L3_SLOTS * P // (P * 1024)
PV_COLS = 96
NEG = -1.0e30


class Signal:

    def __init__(self, sem):
        self.sem = sem
        self.base = 0

    def __call__(self, n):
        return self.sem, self.base + n


class Core:

    def __init__(self, nc, ctx):
        self.nc = nc
        self.ctx = ctx
        self.signals = {}


def signal(core, name):
    if name not in core.signals:
        core.signals[name] = Signal(core.ctx.enter_context(core.nc.semaphore(name)))
    return core.signals[name]


def stage_ends(core, **totals):
    for name, total in totals.items():
        core.signals[name].base += total


def setup(core, x, ct, wmod):
    nc = core.nc
    sb = lambda name, shape, dt=F32: core.ctx.enter_context(nc.sbuf_tensor(name, shape, dt))
    core.x = sb("x_tok", [P, NT, P])
    core.h = sb("h_feat", [P, T])
    core.ident = sb("ident", [P, P])
    core.ident_bf = sb("ident_bf", [P, P], BF16)
    core.mask = sb("causal_mask", [P, P], BF16)
    core.ones = sb("ones", [P, P])
    core.ones_r = sb("ones_r", [P, P], F32R)
    core.shift = sb("shift", [P, LAYERS, 2, B])
    core.scale = sb("scale", [P, LAYERS, 2, B])
    core.gate = sb("gate", [P, LAYERS, 2, B, P])

    core.g_rows = nc.dram_tensor("g_rows", [17, T], F32).ap()
    core.zeros = sb("zeros", [P, 1024])
    core.slots_in = nc.dram_tensor("slots_in", [L3_SLOTS, P], F32).ap()
    core.slots_out = nc.dram_tensor("slots_out", [L3_SLOTS, P], F32).ap()
    zeroed = signal(core, "slots_zeroed")
    loaded, consts, silu_c, step = (signal(core, n) for n in ("loaded", "consts", "silu_c", "dve_step"))
    mod_psum, mod_free = signal(core, "mod_psum"), signal(core, "mod_free")
    gate_psum, gate_abs = (signal(core, n) for n in ("gate_psum", "gate_abs"))
    with ExitStack() as ctx:
        tmp = lambda name, shape, dt=F32: ctx.enter_context(nc.sbuf_tensor(name, shape, dt))
        w_sb = tmp("wmod_sb", [P, LAYERS, 6, P])
        c_sb = tmp("c_sb", [P, LAYERS * B])
        sc = tmp("silu_c_sb", [P, LAYERS * B])
        sc_wide = tmp("silu_c_wide", [P, LAYERS * B, P])
        sign = tmp("gate_sign", [P, 2, B, P])
        mag = tmp("gate_mag", [P, 2, B, P])
        mod_ps = ctx.enter_context(nc.psum_tensor("mod_ps", [P, 4, LAYERS, B], F32))
        gate_ps = ctx.enter_context(nc.psum_tensor("gate_ps", [P, 2, 2, B, P], F32))
        with nc.Block() as block:

            @block.sync
            def _(sp):
                sp.dma_start(c_sb[:], ct).then_inc(loaded.sem, 16)
                sp.dma_start(w_sb[:], wmod).then_inc(loaded.sem, 16)
                sp.dma_start(core.x[:], x.rearrange("b (q p) d -> p (b q) d", p=P)).then_inc(loaded.sem, 16)
                sp.wait_ge(*consts(6))
                for k in range(ZERO_FILLS):
                    part = L3_SLOTS // ZERO_FILLS
                    sp.dma_start(core.slots_in[k * part:(k + 1) * part, :].rearrange("(p r) d -> p (r d)", p=P),
                                 core.zeros[:]).then_inc(zeroed.sem, 16)
                sp.wait_ge(*loaded(48))

            @block.gpsimd
            def _(pool):
                pool.memset(core.zeros[:], 0.0).then_inc(consts.sem, 1)
                for m in (core.ident, core.ident_bf, core.mask):
                    pool.memset(m[:], 0.0).then_inc(consts.sem, 1)
                for m in (core.ones[:], core.ones_r[:].bitcast(F32)):
                    pool.memset(m, 1.0).then_inc(consts.sem, 1)
                pool.wait_ge(*consts(6))
                for m in (core.ident, core.ident_bf):
                    pool.affine_select(out=m[:], in_=m[:], compare_op=ALU.not_equal, fill=1.0, base=0,
                                       pattern=[[-1, P]], channel_multiplier=1).then_inc(consts.sem, 1)
                pool.affine_select(out=core.mask[:], in_=core.mask[:], compare_op=ALU.is_ge, fill=NEG, base=0,
                                   pattern=[[-1, P]], channel_multiplier=1).then_inc(consts.sem, 1)

            @block.scalar
            def _(act):
                act.wait_ge(*loaded(48))
                act.activation(sc[:], c_sb[:], ACT.Silu).then_inc(silu_c.sem, 1)

            @block.tensor
            def _(pe):
                pe.wait_ge(*step(1))
                pe.wait_ge(*loaded(48))
                for j, part in enumerate((0, 1, 3, 4)):
                    for l in range(LAYERS):
                        mm = pe.matmul(mod_ps[:, j, l, :], w_sb[:, l, part, :], sc[:, l * B:(l + 1) * B],
                                       start=True, stop=True)
                mm.then_inc(mod_psum.sem, 1)
                for l in range(LAYERS):
                    if l >= 2:
                        pe.wait_ge(*gate_abs(4 * (l - 2) + 3))
                    for k, part in enumerate((2, 5)):
                        for b in range(B):
                            mm = pe.matmul(gate_ps[:, l % 2, k, b, :], sc_wide[:, l * B + b, :],
                                           w_sb[:, l, part, :], start=True, stop=True)
                    mm.then_inc(gate_psum.sem, 1)

            @block.vector
            def _(dve):
                dve.wait_ge(*silu_c(1))
                dve.tensor_copy(sc_wide[:], sc[:].unsqueeze(2).broadcast_to([P, LAYERS * B, P])).then_inc(step.sem, 1)
                dve.wait_ge(*mod_psum(1))
                for half in range(2):
                    dve.tensor_copy(core.shift[:, :, half, :], mod_ps[:, 2 * half]).then_inc(mod_free.sem, 1)
                    dve.tensor_scalar(core.scale[:, :, half, :], mod_ps[:, 2 * half + 1], 1.0, None,
                                      ALU.add).then_inc(mod_free.sem, 1)
                for l in range(LAYERS):
                    dve.wait_ge(*gate_psum(l + 1))
                    flat = lambda a: a.rearrange("p k b d -> p (k b d)")
                    dve.tensor_scalar(sign[:], gate_ps[:, l % 2], 0.0, 2.0, ALU.is_ge, ALU.mult)\
                       .then_inc(gate_abs.sem, 1)
                    dve.wait_ge(*gate_abs(4 * l + 1))
                    dve.tensor_scalar(sign[:], sign[:], -1.0, None, ALU.add).then_inc(gate_abs.sem, 1)
                    dve.wait_ge(*gate_abs(4 * l + 2))
                    dve.tensor_tensor(mag[:], gate_ps[:, l % 2], sign[:], ALU.mult).then_inc(gate_abs.sem, 1)
                    dve.wait_ge(*gate_abs(4 * l + 3))
                    dve.scalar_tensor_tensor(flat(core.gate[:, l]), flat(mag[:]), 0.25, flat(sign[:]), ALU.max,
                                             ALU.mult).then_inc(gate_abs.sem, 1)
                    dve.wait_ge(*gate_abs(4 * l + 4))
    stage_ends(core, loaded=48, consts=9, silu_c=1, dve_step=1, mod_psum=1, mod_free=4, gate_psum=4, gate_abs=16)


def layer_norm(core, layer, half):
    nc = core.nc
    step, var, std, xn, tr, done = (signal(core, n) for n in
                                    ("dve_step", "ln_var", "ln_std", "ln_normed", "ln_transposed", "ln_h"))
    with ExitStack() as ctx:
        tmp = lambda name, shape, dt=F32: ctx.enter_context(nc.sbuf_tensor(f"{name}_{layer}{half}", shape, dt))
        st = tmp("ln_stats", [P, NT, 6])
        mv = tmp("ln_mv", [P, NT, 2])
        ve = tmp("ln_ve", [P, NT])
        sd = tmp("ln_sd", [P, NT])
        rs = tmp("ln_rs", [P, NT])
        xm = tmp("ln_xn", [P, NT, P])
        ps = ctx.enter_context(nc.psum_tensor(f"ln_ps_{layer}{half}", [P, 2, S], F32))
        with nc.Block() as block:

            @block.vector
            def _(dve):
                n = 0
                for b in range(B):
                    for t in range(Q * b, Q * b + Q):
                        dve.bn_stats(st[:, t, :], core.x[:, t, :]).then_inc(step.sem, 1)
                    n += Q
                    dve.wait_ge(*step(n))
                    for t in range(Q * b, Q * b + Q):
                        dve.bn_aggr(mv[:, t, :], st[:, t, :]).then_inc(step.sem, 1)
                    n += Q
                    dve.wait_ge(*step(n))
                    dve.tensor_scalar(ve[:, Q * b:Q * b + Q], mv[:, Q * b:Q * b + Q, 1], 1e-5, None, ALU.add)\
                       .then_inc(var.sem, 1)
                for b in range(B):
                    dve.wait_ge(*std(b + 1))
                    dve.reciprocal(rs[:, Q * b:Q * b + Q], sd[:, Q * b:Q * b + Q]).then_inc(step.sem, 1)
                    n += 1
                    dve.wait_ge(*step(n))
                    for t in range(Q * b, Q * b + Q):
                        last = dve.tensor_scalar(xm[:, t, :], core.x[:, t, :], mv[:, t, 0:1], rs[:, t:t + 1],
                                                 ALU.subtract, ALU.mult)
                    last.then_inc(xn.sem, 1)

            @block.scalar
            def _(act):
                for b in range(B):
                    act.wait_ge(*var(b + 1))
                    act.activation(sd[:, Q * b:Q * b + Q], ve[:, Q * b:Q * b + Q], ACT.Sqrt).then_inc(std.sem, 1)
                for b in range(B):
                    act.wait_ge(*tr(b + 1))
                    act.activation(core.h[:, b * S:(b + 1) * S], ps[:, b % 2, :], ACT.Identity,
                                   bias=core.shift[:, layer, half, b:b + 1],
                                   scale=core.scale[:, layer, half, b:b + 1]).then_inc(done.sem, 1)

            @block.tensor
            def _(pe):
                for b in range(B):
                    pe.wait_ge(*xn(b + 1))
                    if b >= 2:
                        pe.wait_ge(*done(b - 1))
                    for q in range(Q):
                        mm = pe.transpose(ps[:, b % 2, q * P:(q + 1) * P], xm[:, Q * b + q, :], core.ident[:])
                    mm.then_inc(tr.sem, 1)
    stage_ends(core, dve_step=8 * B + B, ln_var=B, ln_std=B, ln_normed=B, ln_transposed=B, ln_h=B)


def v_width(dv):
    return HEADS * (dv + 1) + PV_COLS - (dv + 1)


def values(core, name, source, w, bias, width):
    nc = core.nc
    loaded, vps, va, vd, v_ones = (signal(core, n) for n in ("loaded", "v_psum", "v_by_act", "v_by_dve", "v_ones"))
    w_cleared = signal(core, "w_cleared")
    v = core.v
    dv = width // HEADS
    K = w.shape[0]
    per = max(1, 512 // width)
    parts = max(1, width // 512)
    jobs = [(t, c) for t in range(0, NT, per) for c in range(parts)]
    with ExitStack() as ctx:
        w_sb = ctx.enter_context(nc.sbuf_tensor(f"wv_{name}", [P, width], F32))
        ps = ctx.enter_context(nc.psum_tensor(f"v_ps_{name}", [P, 4, 512], F32))
        cols = min(width, 512)

        heads = cols // dv
        head_columns = lambda tiles, h, n: v[:, tiles, h * (dv + 1):(h + n) * (dv + 1)]\
            .rearrange("p t (h e) -> p t h e", e=dv + 1)

        def out_of(t, c):
            return head_columns(slice(t, t + per), c * heads, heads)[:, :, :, 0:dv]

        with nc.Block() as block:

            @block.gpsimd
            def _(pool):
                if bias is not None:
                    pool.memset(w_sb[:], 0.0).then_inc(w_cleared.sem, 1)
                pool.memset(head_columns(slice(0, NT), 0, HEADS)[:, :, :, dv], 1.0).then_inc(v_ones.sem, 1)
                pool.memset(v[:, :, HEADS * (dv + 1):], 0.0).then_inc(v_ones.sem, 1)

            @block.sync
            def _(sp):
                if bias is not None:
                    sp.wait_ge(*w_cleared(1))
                sp.dma_start(w_sb[0:K, :], w).then_inc(loaded.sem, 16)
                if bias is not None:
                    sp.dma_start(w_sb[K:K + 1, :], bias).then_inc(loaded.sem, 16)

            @block.tensor
            def _(pe):
                pe.wait_ge(*loaded(16 if bias is None else 32))
                for n, (t, c) in enumerate(jobs):
                    if n >= 4:
                        m = n - 4
                        pe.wait_ge(*(va if m % 2 else vd)(m // 2 + 1))
                    for k in range(per):
                        mm = pe.matmul(ps[:, n % 4, k * cols:(k + 1) * cols], source[:, (t + k) * P:(t + k + 1) * P],
                                       w_sb[:, c * cols:(c + 1) * cols], start=True, stop=True)
                    mm.then_inc(vps.sem, 1)

            @block.scalar
            def _(act):
                for n, (t, c) in enumerate(jobs):
                    if n % 2:
                        act.wait_ge(*vps(n + 1))
                        act.activation(out_of(t, c), ps[:, n % 4, :].rearrange("p (k h c) -> p k h c", k=per, c=dv), ACT.Copy)\
                           .then_inc(va.sem, 1)

            @block.vector
            def _(dve):
                for n, (t, c) in enumerate(jobs):
                    if n % 2 == 0:
                        dve.wait_ge(*vps(n + 1))
                        dve.tensor_copy(out_of(t, c), ps[:, n % 4, :].rearrange("p (k h c) -> p k h c", k=per, c=dv))\
                           .then_inc(vd.sem, 1)
    stage_ends(core, loaded=16 if bias is None else 32, v_psum=len(jobs), v_by_act=len(jobs) // 2,
             v_by_dve=len(jobs) // 2, v_ones=2,
             w_cleared=0 if bias is None else 1)


def attention(core, layer, groups, dv, causal, k_source, wq, wk, wo, bo, q_bias=None, k_bias=None, minus=None,
              q_scale=1.0, k_scale=1.0):
    nc = core.nc
    hpg = HEADS // groups
    Q_STEP = 4
    hv = hpg * dv
    split8 = minus is not None
    KK = wk.shape[1]
    NG = B * groups
    (loaded, out_scaled, x_biased, q_full, k_full, q_plain, k_plain, q_high, k_high, q_made, k_made, s_full,
     neg_max, diag_made, probs_full, probs, o_full, sums_inverse, ctx_ready, ctx_t_full, ctx_turned, y_full, x_added,
     q_cleared) = (signal(core, n) for n in (
         "loaded", "out_scaled", "x_biased", "q_full", "k_full", "q_plain", "k_plain", "q_high", "k_high", "q_made",
         "k_made", "s_full", "neg_max", "diag_made", "probs_full", "probs", "o_full", "sums_inverse", "ctx_ready",
         "ctx_t_full", "ctx_turned", "y_full", "x_added", "q_cleared"))
    wslot = [signal(core, "weights_slot0"), signal(core, "weights_slot1")]
    loads = 16 * (5 if split8 else 2)
    rows_cleared = signal(core, "rows_cleared")
    masked, k_low = signal(core, "masked"), signal(core, "k_low")
    clears = (KK < P) + 2 * (hv < P)

    with ExitStack() as ctx:
        tmp = lambda name, shape, dt=F32: ctx.enter_context(nc.sbuf_tensor(f"{name}_{layer}", shape, dt))
        psum = lambda name, shape: ctx.enter_context(nc.psum_tensor(f"{name}_{layer}", shape, F32))
        wq_s = tmp("wq_slot", [P, 2, P])
        wk_s = tmp("wk_slot", [P, 2, P])
        if split8:
            qb_s, kb_s = tmp("qb_slot", [P, groups]), tmp("kb_slot", [P, groups])
            minus_s = tmp("minus_low", [P, 2])
            q_f, k_f = tmp("q_plain", [P, S]), tmp("k_plain", [P, S])
            q_h, k_h = tmp("q_high", [P, S], F32R), tmp("k_high", [P, S], F32R)
        wo_sb = tmp("wo_sb", [hv, groups, P])
        wog = tmp("wo_gated", [P, B, groups, P])
        bo_sb = tmp("bo_sb", [P, P])
        bog = tmp("bo_gated", [P, B, P])
        q_st = tmp("q_parts", [P, 2, hpg, S], F32R)
        k_heads = 1 if split8 else hpg
        k_a = tmp("k_parts_a", [P, 2, k_heads, S], F32R)
        k_b = None if split8 else tmp("k_parts_b", [P, 2, k_heads, S], F32R)
        pt = tmp("probs_t", [P, 2, Q, S])
        nm = tmp("neg_max", [P, 2, Q])
        diag = tmp("max_diag", [P, 2, Q, P], F32R)
        inv = tmp("inv_sums", [P, 2, Q])
        tick = tmp("tick", [P, hpg * Q])
        ctx_sb = tmp("ctx_sb", [P, 2, Q, hpg, dv])
        ctx_t = tmp("ctx_t", [P, S])
        s_ps = psum("s_ps", [P, 2, S])
        p_ps = psum("p_ps", [P, 2, S])
        o_ps = psum("o_ps", [P, 2, Q, P])
        turn_ps = psum("turn_ps", [P, S])
        add_ps = psum("add_ps", [P, S])

        batch = lambda g: g // groups
        in_batch = lambda g: g % groups
        tile_of = lambda i: Q - 1 - i if split8 else i
        keys = lambda i: (i + 1) * P if causal else S
        seen_by = lambda i: slice(i * P if causal else 0, S)
        half = lambda h: slice(h % 2 * 64, h % 2 * 64 + 64)
        other = lambda h: half(h + 1)
        among_first = lambda g, h, n: isinstance(g, int) and g * hpg + h < n

        with nc.Block() as block:

            @block.sync
            def _(sp):
                sp.dma_start(wo_sb[:], wo.rearrange("g f n -> f g n")).then_inc(loaded.sem, 16)
                sp.dma_start(bo_sb[:], bo.broadcast_to([P, P])).then_inc(loaded.sem, 16)
                if split8:
                    sp.dma_start(qb_s[:], q_bias).then_inc(loaded.sem, 16)
                    sp.dma_start(kb_s[:], k_bias).then_inc(loaded.sem, 16)
                    sp.dma_start(minus_s[:], minus).then_inc(loaded.sem, 16)

                def load(g, s):
                    sp.dma_start(wq_s[:, s, :], wq[in_batch(g), :, :]).then_inc(wslot[s].sem, 16)
                    sp.dma_start(wk_s[0:KK, s, :], wk[in_batch(g), :, :]).then_inc(wslot[s].sem, 16)

                if KK < P:
                    sp.wait_ge(*rows_cleared(1))
                load(0, 0)
                load(1, 1)
                with sp.Fori(1, NG // 2) as i:
                    for s in range(2):
                        sp.wait_ge(*k_full(2 * (i - 1) + s + 1))
                        load(2 * i + s, s)

            @block.gpsimd
            def _(pool):
                if KK < P:
                    pool.memset(wk_s[:], 0.0).then_inc(rows_cleared.sem, 1)
                pool.memset(q_st[:].bitcast(F32), 0.0).then_inc(q_cleared.sem, 1)
                if hv < P:
                    pool.memset(ctx_t[:], 0.0).then_inc(rows_cleared.sem, 1)
                    pool.memset(wog[:], 0.0).then_inc(rows_cleared.sem, 1)
                    pool.wait_ge(*rows_cleared(clears))
                pool.wait_ge(*loaded(loads))
                for b in range(B):
                    pool.tensor_tensor(wog[0:hv, b], wo_sb[:],
                                       core.gate[0:hv, layer, 0, b, :].unsqueeze(1).broadcast_to([hv, groups, P]),
                                       ALU.mult).then_inc(out_scaled.sem, 1)
                for b in range(B):
                    pool.tensor_tensor(bog[:, b], bo_sb[:], core.gate[:, layer, 0, b, :], ALU.mult)\
                        .then_inc(out_scaled.sem, 1)
                pool.wait_ge(*out_scaled(2 * B))
                for b in range(B):
                    xb = core.x[:, Q * b:Q * b + Q, :]
                    pool.tensor_tensor(xb, xb, bog[:, b, :].unsqueeze(1).broadcast_to([P, Q, P]), ALU.add)\
                        .then_inc(x_biased.sem, 1)
                if causal:
                    def select(g, h, i):
                        n = (g * hpg + h) * Q + i
                        pool.wait_ge(*probs(n + 1))
                        own = pt[:, h % 2, i, i * P:(i + 1) * P]
                        pool.tensor_tensor(tick[:, h * Q + i:h * Q + i + 1], core.zeros[:, 0:1], core.zeros[:, 0:1], ALU.add)
                        pool.affine_select(out=own, in_=own, compare_op=ALU.is_ge, fill=0.0, base=0, pattern=[[1, P]],
                                           channel_multiplier=-1).then_inc(masked.sem, 1)

                    with pool.Fori(0, NG) as g:
                        for h in range(hpg):
                            for i in range(Q):
                                select(g, h, i)

            @block.tensor
            def _(pe):
                def project_q(g, s, turned):
                    pe.wait_ge(*wslot[s](32 * (g // 2) + 32))
                    if turned is not None:
                        pe.wait_ge(*turned)
                    pe.matmul(turn_ps[:], wq_s[:, s, :], core.h[:, bass.ds(batch(g) * S, S)], start=True,
                              stop=True).then_inc(q_full.sem, 1)

                def project_k(g, s, added):
                    if added is not None:
                        pe.wait_ge(*added)
                    pe.matmul(add_ps[:], wk_s[:, s, :], k_source[:, bass.ds(batch(g) * S, S)], start=True,
                              stop=True).then_inc(k_full.sem, 1)

                def scores(g, s, h, i):
                    n = (g * hpg + h) * Q + i
                    if i == 0:
                        pe.wait_ge(*q_made(g * hpg + h + 1))
                        pe.wait_ge(*(k_made(g + 1) if split8 else k_high(g * hpg + h + 1)))
                    if not (among_first(g, h, 1) and i < 2):
                        pe.wait_ge(*neg_max(n - 1))
                    q = tile_of(i)
                    mm = pe.matmul(s_ps[:, i % 2, 0:keys(q)], q_st[:, s, h, q * P:(q + 1) * P],
                                   k_a[:, s, h % k_heads, 0:keys(q)], start=True, stop=True)
                    if causal:
                        mm = pe.matmul(s_ps[:, i % 2, q * P:(q + 1) * P], core.ident_bf[:], core.mask[:],
                                       start=False, stop=True, skip_group_check=True)
                    mm.then_inc(s_full.sem, 1)

                def scores_t(g, s, h, i):
                    j = g * hpg + h
                    if not (among_first(g, h, 1) and i < 2):
                        pe.wait_ge(*probs(j * Q + i - 1))
                    if i == 0 and not split8:
                        pe.wait_ge(*k_made(j + 1))
                    into, seen = p_ps[:, i % 2, seen_by(i)], seen_by(i)
                    for m, k in enumerate((k_a,) if split8 else (k_a, k_b)):
                        pe.matmul(into, k[:, s, h % k_heads, i * P:(i + 1) * P], q_st[:, s, h, seen], start=m == 0,
                                  stop=False)
                    if i == 0:
                        pe.wait_ge(*diag_made((j + 1) * Q))
                    mm = pe.matmul(into, core.ones_r[:],
                                   diag[:, h % 2, seen.start // P:Q, :].rearrange("p q k -> p (q k)"), start=False,
                                   stop=True)
                    mm.then_inc(probs_full.sem, 1)

                def times_v(g, h, i):
                    j = g * hpg + h
                    pe.wait_ge(*(masked(j * Q + i + 1) if causal else probs((j + 1) * Q)))
                    if i == 0 and not among_first(g, h, 2):
                        pe.wait_ge(*ctx_ready(j - 1))
                    last = i if causal else Q - 1
                    for c in range(last + 1):
                        mm = pe.matmul(o_ps[:, h % 2, i, 0:PV_COLS], pt[:, h % 2, c, i * P:(i + 1) * P],
                                       core.v[:, batch(g) * Q + c,
                                              bass.ds((in_batch(g) * hpg + h) * (dv + 1), PV_COLS)],
                                       start=c == 0, stop=c == last)
                    if i == Q - 1:
                        mm.then_inc(o_full.sem, 1)

                def turn_ctx(g, s, left):
                    pe.wait_ge(*left)
                    pe.wait_ge(*ctx_ready((g + 1) * hpg))
                    for q in range(Q):
                        mm = pe.transpose(turn_ps[0:hv, q * P:(q + 1) * P],
                                          ctx_sb[:, s, q].rearrange("p h e -> p (h e)"), core.ident[:])
                    mm.then_inc(ctx_t_full.sem, 1)

                def project_out(g, left):
                    pe.wait_ge(*left)
                    pe.wait_ge(*ctx_turned(g + 1))
                    for q in range(Q):
                        mm = pe.matmul(add_ps[:, q * P:(q + 1) * P], ctx_t[:, q * P:(q + 1) * P],
                                       wog[:, batch(g), in_batch(g), :], start=True, stop=True)
                    mm.then_inc(y_full.sem, 1)

                def window(g, s, turned, added, first=False, out=True):
                    for h in range(hpg):
                        for i in range(Q):
                            scores(g, s, h, i)
                            if h >= 1:
                                scores_t(g, s, h - 1, i)
                            elif not first:
                                scores_t(g - 1, 1 - s, hpg - 1, i)
                            if h >= 2:
                                times_v(g, h - 2, i)
                            elif not first:
                                times_v(g - 1, hpg + h - 2, i)
                            step = h * Q + i
                            if step == 1 and out:
                                turn_ctx(g - 2, s, q_made((g + 1) * hpg))
                            if step == 3 and out:
                                project_out(g - 2, k_made(g + 1) if split8 else k_low((g + 1) * hpg))
                            if step == Q_STEP and turned is not None:
                                project_q(g + 1, 1 - s, turned)
                            if step == Q_STEP + 1 and added is not None:
                                project_k(g + 1, 1 - s, added)

                project_q(0, 0, None)
                project_k(0, 0, None)
                window(0, 0, q_made(hpg), k_made(k_heads), first=True, out=False)
                window(1, 1, q_made(2 * hpg), k_made(2 * k_heads), out=False)
                pe.wait_ge(*out_scaled(2 * B))
                with pe.Fori(1, NG // 2 - 1) as i:
                    for s in range(2):
                        g = 2 * i + s
                        window(g, s, ctx_turned(g - 1), x_added(g - 1))
                window(NG - 2, 0, ctx_turned(NG - 3), x_added(NG - 3))
                window(NG - 1, 1, None, None)
                for i in range(Q):
                    scores_t(NG - 1, 1, hpg - 1, i)
                    times_v(NG - 1, hpg - 2, i)
                turn_ctx(NG - 2, 0, ctx_turned(NG - 2))
                for i in range(Q):
                    times_v(NG - 1, hpg - 1, i)
                project_out(NG - 2, x_added(NG - 2))
                turn_ctx(NG - 1, 1, ctx_turned(NG - 1))
                project_out(NG - 1, x_added(NG - 1))

            @block.scalar
            def _(act):
                def high_of_q(g, s, h):
                    if h == 0:
                        act.wait_ge(*q_full(g + 1))
                    if split8 and h == 0:
                        act.activation(q_f[:], turn_ps[:], ACT.Identity, scale=q_scale,
                                       bias=qb_s[:, bass.ds(in_batch(g), 1)]).then_inc(q_plain.sem, 1)
                        act.wait_ge(*q_plain(g + 1))
                        act.copy(q_h[:], q_f[:]).then_inc(q_high.sem, 1)
                    elif not split8:
                        act.mul(q_st[half(h), s, h, :], turn_ps[half(h), :], q_scale).then_inc(q_high.sem, 1)

                def highs_of_k(g, s, h):
                    if h == 0:
                        act.wait_ge(*k_full(g + 1))
                    if split8 and h == 0:
                        act.activation(k_f[:], add_ps[:], ACT.Identity, scale=k_scale,
                                       bias=kb_s[:, bass.ds(in_batch(g), 1)]).then_inc(k_plain.sem, 1)
                        act.wait_ge(*k_plain(g + 1))
                        act.copy(k_h[:], k_f[:]).then_inc(k_high.sem, 1)
                    elif not split8:
                        for rows in (half(h), other(h)):
                            last = act.mul(k_a[rows, s, h, :], add_ps[half(h), :], k_scale)
                        last.then_inc(k_high.sem, 1)

                def repeat_low_of_k(g, s, h):
                    act.wait_ge(*k_low(hpg * g + h + 1))
                    act.copy(k_b[other(h), s, h, :], k_b[half(h), s, h, :].bitcast(F32)).then_inc(k_made.sem, 1)

                def exps(g, h, i):
                    n = (g * hpg + h) * Q + i
                    act.wait_ge(*probs_full(n + 1))
                    act.activation(pt[:, h % 2, i, seen_by(i)], p_ps[:, i % 2, seen_by(i)], ACT.Exp)\
                        .then_inc(probs.sem, 1)

                def copy_ctx(g):
                    act.wait_ge(*ctx_t_full(g + 1))
                    act.copy(ctx_t[0:hv, :], turn_ps[0:hv, :]).then_inc(ctx_turned.sem, 1)

                def window(g, s, first=False, out=True, last=False):
                    for h in range(hpg):
                        for i in range(Q):
                            step = h * Q + i
                            if not split8 and step in (1, 2) and not among_first(g, 0, 1):
                                repeat_low_of_k(g, s, step - 1)
                            if step == 2 and out:
                                copy_ctx(g - 2)
                            if h >= 1:
                                exps(g, h - 1, i)
                            elif not first:
                                exps(g - 1, hpg - 1, i)
                            if step - Q_STEP in (1, 2) and not last:
                                high_of_q(g + 1, 1 - s, step - Q_STEP - 1)
                            if step - Q_STEP in (2, 3) and not last:
                                highs_of_k(g + 1, 1 - s, step - Q_STEP - 2)

                act.wait_ge(*loaded(loads))
                act.wait_ge(*q_cleared(1))
                if hv < P:
                    act.wait_ge(*rows_cleared(clears))
                for h in range(2):
                    high_of_q(0, 0, h)
                    highs_of_k(0, 0, h)
                if not split8:
                    for h in range(hpg):
                        repeat_low_of_k(0, 0, h)
                window(0, 0, first=True, out=False)
                window(1, 1, out=False)
                with act.Fori(1, NG // 2 - 1) as i:
                    window(2 * i, 0)
                    window(2 * i + 1, 1)
                window(NG - 2, 0)
                window(NG - 1, 1, last=True)
                for i in range(Q):
                    exps(NG - 1, hpg - 1, i)
                copy_ctx(NG - 2)
                copy_ctx(NG - 1)

            @block.vector
            def _(dve):
                def low_of_q(g, s, h):
                    if split8:
                        dve.wait_ge(*q_high(g + 1))
                        r = slice(h * 32, h * 32 + 32)
                        dve.scalar_tensor_tensor(q_st[r, s, h, :], q_h[r, :].bitcast(F32), minus_s[r, 0:1], q_f[r, :],
                                                 ALU.mult, ALU.add).then_inc(q_made.sem, 1)
                    else:
                        dve.wait_ge(*q_high(g * hpg + h + 1))
                        dve.scalar_tensor_tensor(q_st[other(h), s, h, :], turn_ps[half(h), :], q_scale,
                                                 q_st[half(h), s, h, :].bitcast(F32), ALU.mult, ALU.subtract)\
                           .then_inc(q_made.sem, 1)

                def lows_of_k(g, s, h):
                    if split8:
                        dve.wait_ge(*k_high(g + 1))
                        dve.scalar_tensor_tensor(k_a[:, s, 0, :], k_h[:].bitcast(F32), minus_s[:, 1:2], k_f[:],
                                                 ALU.mult, ALU.add).then_inc(k_made.sem, 1)
                    else:
                        dve.wait_ge(*k_high(hpg * g + h + 1))
                        dve.scalar_tensor_tensor(k_b[half(h), s, h, :], add_ps[half(h), :], k_scale,
                                                 k_a[half(h), s, h, :].bitcast(F32), ALU.mult, ALU.subtract)\
                           .then_inc(k_low.sem, 1)

                def maxima(g, h, i):
                    n = (g * hpg + h) * Q + i
                    dve.wait_ge(*s_full(n + 1))
                    q = tile_of(i)
                    dve.tensor_reduce(nm[:, h % 2, q:q + 1], s_ps[:, i % 2, 0:keys(q)], AX_X, ALU.max, negate=True)\
                        .then_inc(neg_max.sem, 1)
                    dve.wait_ge(*neg_max(n + 1))
                    dve.tensor_scalar(diag[:, h % 2, q, :], core.ident[:], nm[:, h % 2, q:q + 1], None, ALU.mult)\
                        .then_inc(diag_made.sem, 1)

                def normalise(g, s, h):
                    j = g * hpg + h
                    dve.wait_ge(*o_full(j + 1))
                    dve.reciprocal(inv[:, h % 2, :], o_ps[:, h % 2, :, dv]).then_inc(sums_inverse.sem, 1)
                    dve.wait_ge(*sums_inverse(j + 1))
                    dve.tensor_tensor(ctx_sb[:, s, :, h, :], o_ps[:, h % 2, :, 0:dv],
                                      inv[:, h % 2, :].unsqueeze(2).broadcast_to([P, Q, dv]), ALU.mult)\
                        .then_inc(ctx_ready.sem, 1)

                def add_to_x(g):
                    dve.wait_ge(*y_full(g + 1))
                    xb = core.x[:, bass.ds(batch(g) * Q, Q), :]
                    dve.tensor_tensor(xb, xb, add_ps[:].rearrange("p (q d) -> p q d", q=Q), ALU.add)\
                       .then_inc(x_added.sem, 1)

                def window(g, s, out=True, last=False):
                    for h in range(hpg):
                        for i in range(Q):
                            maxima(g, h, i)
                            step = h * Q + i
                            if i == 0:
                                back = (hpg - 1 - (h - 3)) // hpg
                                if not among_first(g, h, 3):
                                    normalise(g - back, (s + back) % 2, h - 3 + back * hpg)
                            if step == 4 and out:
                                add_to_x(g - 2)
                            if step - Q_STEP - 2 in range(hpg) and not last:
                                low_of_q(g + 1, 1 - s, step - Q_STEP - 2)
                            if split8 and step == Q_STEP + 4 and not last:
                                lows_of_k(g + 1, 1 - s, 0)
                            if not split8 and step in (0, 1) and not among_first(g, 0, 1):
                                lows_of_k(g, s, step)

                dve.wait_ge(*loaded(loads))
                dve.wait_ge(*q_cleared(1))
                for h in range(hpg):
                    low_of_q(0, 0, h)
                for h in range(k_heads):
                    lows_of_k(0, 0, h)
                window(0, 0, out=False)
                window(1, 1, out=False)
                dve.wait_ge(*x_biased(B))
                with dve.Fori(1, NG // 2 - 1) as i:
                    window(2 * i, 0)
                    window(2 * i + 1, 1)
                window(NG - 2, 0)
                window(NG - 1, 1, last=True)
                for j in range(NG * hpg - 3, NG * hpg):
                    normalise(j // hpg, j // hpg % 2, j % hpg)
                add_to_x(NG - 2)
                add_to_x(NG - 1)
    heads = NG * hpg
    stage_ends(core, loaded=loads, weights_slot0=16 * NG, weights_slot1=16 * NG, out_scaled=2 * B, x_biased=B,
               q_full=NG, k_full=NG, q_plain=NG if split8 else 0, k_plain=NG if split8 else 0, q_high=NG if split8 else heads,
               k_high=NG if split8 else heads, q_made=heads, k_made=NG * k_heads, s_full=heads * Q, neg_max=heads * Q,
               diag_made=heads * Q, probs_full=heads * Q, probs=heads * Q, o_full=heads, sums_inverse=heads,
               ctx_ready=heads, ctx_t_full=NG, ctx_turned=NG, y_full=NG, x_added=NG, q_cleared=1,
               rows_cleared=clears, masked=heads * Q if causal else 0, k_low=0 if split8 else heads)


def route(core, layer, E, gate_w, gate_b, kind, source=None, chosen=None):
    nc = core.nc
    K = 3 if kind == "renormed" else 2
    loaded, full, step, to_exp, exped, iotas = (signal(core, n) for n in
                                                ("loaded", "logits_full", "dve_step", "to_exp", "exped", "iotas"))
    counts = {}
    with ExitStack() as ctx:
        tmp = lambda name, shape, dt=F32: ctx.enter_context(nc.sbuf_tensor(f"{name}_r{layer}", shape, dt))
        gw = tmp("gate_w", [P, E])
        gb = tmp("gate_b", [P, E])
        lg = tmp("logits", [P, NT, E])
        top = tmp("top", [P, NT, 8])
        idx = tmp("idx", [P, NT, 8], U32)
        iota_i = tmp("iota_i", [P, E], I32)
        iota = tmp("iota", [P, E])
        wide = [tmp(f"wide{n}", [P, NT, E]) for n in range(4)]
        if chosen is None:
            hot, ws, idx_f = tmp("hot", [P, K, NT, E]), tmp("ws", [P, K, NT]), tmp("idx_f", [P, NT, 8])
        else:
            hot, ws, idx_f = chosen
        thin = [tmp(f"thin{n}", [P, NT]) for n in range(4)]
        ps = ctx.enter_context(nc.psum_tensor(f"logits_ps{layer}", [P, NT, E], F32))
        g = core.g if chosen is None else None
        source = core.h if source is None else source
        over_e = lambda a: a.unsqueeze(2).broadcast_to([P, NT, E])
        val = lambda k: top[:, :, k]
        with nc.Block() as block:

            @block.sync
            def _(sp):
                sp.dma_start(gw[:], gate_w).then_inc(loaded.sem, 16)
                if gate_b is not None:
                    sp.dma_start(gb[:], gate_b.broadcast_to([P, E])).then_inc(loaded.sem, 16)

            @block.gpsimd
            def _(pool):
                pool.iota(iota_i[:], pattern=[[1, E]], base=0, channel_multiplier=0).then_inc(iotas.sem, 1)
                if kind == "renormed":
                    pool.memset(g[:, E:E + 2, :], 1.0).then_inc(iotas.sem, 1)

            @block.tensor
            def _(pe):
                pe.wait_ge(*loaded(16 if gate_b is None else 32))
                for t in range(NT):
                    mm = pe.matmul(ps[:, t, :], source[:, t * P:(t + 1) * P], gw[:], start=True, stop=True)
                mm.then_inc(full.sem, 1)

            @block.vector
            def _(dve):
                n = 0

                def link(ins):
                    nonlocal n
                    n += 1
                    ins.then_inc(step.sem, 1)
                    dve.wait_ge(*step(n))

                exps = 0

                def exp_of(out):
                    nonlocal exps
                    exps += 1
                    dve.wait_ge(*exped(exps))

                dve.wait_ge(*iotas(2 if kind == "renormed" else 1))
                link(dve.tensor_copy(iota[:], iota_i[:]))
                dve.wait_ge(*full(1))
                if gate_b is not None:
                    dve.wait_ge(*loaded(32))
                    link(dve.tensor_tensor(lg[:], ps[:], gb[:].unsqueeze(1).broadcast_to([P, NT, E]), ALU.add))
                else:
                    link(dve.tensor_copy(lg[:], ps[:]))
                for t in range(NT):
                    last = dve.max(out=top[:, t, :], in_=lg[:, t, :])
                link(last)
                for t in range(NT):
                    last = dve.max_index(out=idx[:, t, :], in_max=top[:, t, :], in_values=lg[:, t, :])
                link(last)
                link(dve.tensor_copy(idx_f[:], idx[:]))
                for k in range(K):
                    last = dve.tensor_tensor(hot[:, k], iota[:].unsqueeze(1).broadcast_to([P, NT, E]),
                                             over_e(idx_f[:, :, k]), ALU.is_equal)
                link(last)
                if kind == "softmax":
                    dve.tensor_tensor(thin[0][:], val(1), val(0), ALU.subtract).then_inc(to_exp.sem, 1)
                    exp_of(thin[1])
                    link(dve.tensor_scalar(thin[2][:], thin[1][:], 1.0, None, ALU.add))
                    link(dve.reciprocal(ws[:, 0], thin[2][:]))
                    link(dve.tensor_tensor(ws[:, 1], thin[1][:], ws[:, 0], ALU.mult))
                elif kind == "jitter":
                    link(dve.scalar_tensor_tensor(wide[3][:].rearrange("p t e -> p (t e)"),
                                                  lg[:].rearrange("p t e -> p (t e)"), -1.0,
                                                  lg[:].rearrange("p t e -> p (t e)"), ALU.mult, ALU.max))
                    for k in range(2):
                        link(dve.tensor_tensor(wide[0][:], over_e(val(k)), lg[:], ALU.subtract))
                        link(dve.tensor_tensor(wide[1][:], wide[3][:], over_e(val(k)), ALU.max))
                        link(dve.tensor_scalar(wide[1][:], wide[1][:], 0.02, None, ALU.mult))
                        link(dve.tensor_tensor(wide[1][:], wide[0][:], wide[1][:], ALU.is_le))
                        if k == 1:
                            link(dve.tensor_tensor(wide[2][:], wide[1][:], hot[:, 0], ALU.mult))
                            link(dve.tensor_tensor(wide[1][:], wide[1][:], wide[2][:], ALU.subtract))
                        dve.tensor_scalar(wide[0][:], wide[0][:], 0.0, None, ALU.max).then_inc(to_exp.sem, 1)
                        exp_of(wide[2])
                        link(dve.tensor_tensor(wide[2][:], wide[2][:], wide[1][:], ALU.mult))
                        link(dve.tensor_reduce(thin[0][:], wide[2][:], AX_X, ALU.add))
                        link(dve.reciprocal(ws[:, k], thin[0][:]))
                else:
                    dve.tensor_tensor(wide[0][:], lg[:], over_e(val(0)), ALU.subtract).then_inc(to_exp.sem, 1)
                    exp_of(wide[2])
                    link(dve.tensor_reduce(thin[0][:], wide[2][:], AX_X, ALU.add))
                    link(dve.reciprocal(thin[0][:], thin[0][:]))
                    for k in range(K):
                        link(dve.tensor_tensor(wide[0][:], wide[2][:], hot[:, k], ALU.mult))
                        link(dve.tensor_reduce(ws[:, k], wide[0][:], AX_X, ALU.add))
                        link(dve.tensor_tensor(ws[:, k], ws[:, k], thin[0][:], ALU.mult))
                    link(dve.tensor_tensor(thin[1][:], ws[:, 0], ws[:, 1], ALU.add))
                    link(dve.tensor_tensor(thin[1][:], thin[1][:], ws[:, 2], ALU.add))
                    link(dve.tensor_scalar(thin[1][:], thin[1][:], 1e-20, None, ALU.add))
                    link(dve.reciprocal(thin[1][:], thin[1][:]))
                    for k in range(K):
                        last = dve.tensor_tensor(ws[:, k], ws[:, k], thin[1][:], ALU.mult)
                    link(last)
                if chosen is None:
                    for k in range(K):
                        last = dve.tensor_tensor(wide[k][:], hot[:, k], over_e(ws[:, k]), ALU.mult)
                    link(last)
                    if K == 3:
                        link(dve.tensor_tensor(wide[1][:], wide[1][:], wide[2][:], ALU.add))
                    link(dve.tensor_tensor(g[:, 0:E, :].rearrange("p e t -> p t e"), wide[0][:], wide[1][:],
                                           ALU.add))
                counts.update(step=n, exps=exps)

            @block.scalar
            def _(act):
                src, dst, sign = {"softmax": (thin[0], thin[1], 1.0), "jitter": (wide[0], wide[2], -1.0),
                                  "renormed": (wide[0], wide[2], 1.0)}[kind]
                for k in range(counts["exps"]):
                    act.wait_ge(*to_exp(k + 1))
                    act.activation(dst[:], src[:], ACT.Exp, scale=sign).then_inc(exped.sem, 1)
    stage_ends(core, loaded=16 if gate_b is None else 32, logits_full=1, dve_step=counts["step"], to_exp=counts["exps"],
             exped=counts["exps"], iotas=2 if kind == "renormed" else 1)


def gate_rows(core, layer, E, b2):
    nc = core.nc
    loaded, turned, g_copied, g_stored = (signal(core, n) for n in ("loaded", "g_turned", "g_copied", "g_stored"))
    with ExitStack() as ctx:
        t_ps = ctx.enter_context(nc.psum_tensor(f"g_t_ps_{layer}", [P, B, S], F32))
        with nc.Block() as block:

            @block.sync
            def _(sp):
                if b2 is not None:
                    sp.dma_start(core.b2[0:E, :], b2).then_inc(loaded.sem, 16)
                sp.wait_ge(*g_copied(B))
                sp.dma_start(core.g_rows[0:E, :], core.g_t[0:E, :]).then_inc(g_stored.sem, 16)
                sp.wait_ge(*g_stored(16))
                if b2 is not None:
                    sp.wait_ge(*loaded(16))

            @block.tensor
            def _(pe):
                for b in range(B):
                    for q in range(Q):
                        mm = pe.transpose(t_ps[0:E, b, q * P:(q + 1) * P], core.g[:, 0:E, b * Q + q], core.ident[:])
                    mm.then_inc(turned.sem, 1)

            @block.scalar
            def _(act):
                for b in range(B):
                    act.wait_ge(*turned(b + 1))
                    act.copy(core.g_t[0:E, b * S:(b + 1) * S], t_ps[0:E, b, :]).then_inc(g_copied.sem, 1)
    stage_ends(core, loaded=0 if b2 is None else 16, g_turned=B, g_copied=B, g_stored=16)


def experts(core, layer, E, FR, FB, func, w1, w2, b1=None, mult=None, biased=True):
    nc = core.nc
    parts = w1.shape[2] // (FB * FR)
    glu = parts == 2
    U = B * FB
    LAG = 4
    R = 4 // parts
    (h_high, h_split, up_full, activated, product_made, weighed, a_high, a_made, down_done, w1_high, w1_split, w2_scaled,
     w2_high, w2_split, y_copied, y_turned, final) = (signal(core, n) for n in (
         "h_high", "h_split", "up_full", "activated", "product_made", "weighed", "a_high", "a_made", "down_done",
         "w1_high", "w1_split", "w2_scaled", "w2_high", "w2_split", "y_copied", "y_turned", "dve_step"))
    wslot = [signal(core, "weights_slot0"), signal(core, "weights_slot1")]
    loads = 2 + (mult is not None)
    bslot = [signal(core, "biases_slot0"), signal(core, "biases_slot1")]
    gslot = [[signal(core, f"token_weights_slot{s}_half{k}") for k in range(2)] for s in range(2)]
    head = 3 if E % 2 else 2
    with ExitStack() as ctx:
        tmp = lambda name, shape, dt=F32: ctx.enter_context(nc.sbuf_tensor(f"{name}_e{layer}", shape, dt))
        h_hi, h_lo = tmp("h_high", [P, T], F32R), tmp("h_low", [P, T], F32R)
        C1, C2 = FB * parts * FR, FB * P
        w1_s, w2_s = tmp("w1_slot", [P, 2, C1]), tmp("w2_slot", [FR, 2, C2])
        w1_hi, w1_lo = tmp("w1_high", [P, 2, C1], F32R), tmp("w1_low", [P, 2, C1], F32R)
        w2_hi, w2_lo = tmp("w2_high", [FR, 2, C2], F32R), tmp("w2_low", [FR, 2, C2], F32R)
        b1_s = tmp("b1_slot", [FR, 2, FB * parts])
        mu_s = tmp("mult_slot", [FR, 2, 1])
        w2_m = tmp("w2_scaled", [FR, 2, C2]) if mult is not None else w2_s
        g_s = tmp("g_slot", [P, 2, T])
        act_s = tmp("activated", [FR, 2, S])
        prod = tmp("product", [FR, 2, S]) if glu else act_s
        a_f = tmp("weighed", [FR, 4, S])
        a_hi, a_lo = tmp("a_high", [FR, 4, S], F32R), tmp("a_low", [FR, 4, S], F32R)
        y_sb = tmp("y_feat", [P, B, S])
        y_x = tmp("y_tok", [P, B, S])
        up = ctx.enter_context(nc.psum_tensor(f"up_ps_{layer}", [P, R, parts, S], F32))
        y_ps = ctx.enter_context(nc.psum_tensor(f"y_ps_{layer}", [P, B, S], F32))
        token_bank = lambda b: up[:, b // parts, b % parts, :]

        def run(eng, window):
            for e in range(head):
                window(e, e % 2, first=e == 0)
            with eng.Fori(0, (E - head - 2) // 2) as i:
                window(2 * i + head, head % 2)
                window(2 * i + head + 1, 1 - head % 2)
            window(E - 2, E % 2)
            window(E - 1, 1 - E % 2, last=True)

        old = lambda e, n: not isinstance(e, int) or e >= n
        with nc.Block() as block:

            @block.sync
            def _(sp):
                def load_weights(e, s):
                    if old(e, 2):
                        sp.wait_ge(*w2_split(e - 1))
                    sp.dma_start(w1_s[:, s, :], w1[e, :, :]).then_inc(wslot[s].sem, 16)
                    sp.dma_start(w2_s[:, s, :], w2[e, :, :]).then_inc(wslot[s].sem, 16)
                    if mult is not None:
                        sp.dma_start(mu_s[:, s, :], mult[e, :, :]).then_inc(wslot[s].sem, 16)

                def window(e, s, first=False, last=False):
                    if not last:
                        load_weights(e + 1, 1 - s)
                    for k in range(2):
                        if old(e, 2):
                            sp.wait_ge(*weighed((e - 2) * U + (k + 1) * U // 2))
                        half = slice(k * T // 2, (k + 1) * T // 2)
                        sp.dma_start(g_s[:, s, half], core.g_rows[bass.ds(e, 1), half].broadcast_to([P, T // 2]))\
                          .then_inc(gslot[s][k].sem, 16)
                        if b1 is not None and k == 0:
                            if old(e, 2):
                                sp.wait_ge(*(product_made if glu else activated)((e - 1) * U))
                            sp.dma_start(b1_s[:, s, :], b1[e, :, :]).then_inc(bslot[s].sem, 16)

                load_weights(0, 0)
                run(sp, window)

            @block.gpsimd
            def _(pool):
                def split(high, low, full, made_high, made_low, e):
                    nothing = core.zeros[0:full.shape[0], 0:full.shape[1]]
                    pool.tensor_tensor(high, full, nothing, ALU.add).then_inc(made_high.sem, 1)
                    pool.wait_ge(*made_high(e + 1))
                    pool.tensor_tensor(low, full, high.bitcast(F32), ALU.subtract).then_inc(made_low.sem, 1)

                def window(e, s, first=False, last=False):
                    pool.wait_ge(*wslot[s](16 * loads * (e // 2 + 1)))
                    if old(e, 2):
                        pool.wait_ge(*up_full((e - 1) * U))
                    split(w1_hi[:, s, :], w1_lo[:, s, :], w1_s[:, s, :], w1_high, w1_split, e)
                    if old(e, 2):
                        pool.wait_ge(*down_done((e - 1) * U))
                    if mult is not None:
                        pool.tensor_tensor(w2_m[:, s, :], w2_s[:, s, :], mu_s[:, s, :].broadcast_to([FR, C2]),
                                           ALU.mult).then_inc(w2_scaled.sem, 1)
                        pool.wait_ge(*w2_scaled(e + 1))
                    split(w2_hi[:, s, :], w2_lo[:, s, :], w2_m[:, s, :], w2_high, w2_split, e)

                run(pool, window)

            @block.tensor
            def _(pe):
                def three_passes(out, w_hi, w_lo, a_hi, a_lo, start):
                    pe.matmul(out, w_hi, a_hi, start=start, stop=False, skip_group_check=True)
                    pe.matmul(out, w_hi, a_lo, start=False, stop=False, skip_group_check=True)
                    return pe.matmul(out, w_lo, a_hi, start=False, stop=True, skip_group_check=True)

                def up_proj(e, s, u, first):
                    n = e * U + u
                    c, f = divmod(u, FB)
                    if u == 0:
                        pe.wait_ge(*w1_split(e + 1))
                    if first and f == 0:
                        pe.wait_ge(*h_split(c + 1))
                    if not (first and u < R):
                        pe.wait_ge(*(product_made if glu else activated)(n - R + 1))
                    for k in range(parts):
                        w = slice((f * parts + k) * FR, (f * parts + k + 1) * FR)
                        t = slice(c * S, (c + 1) * S)
                        mm = three_passes(up[0:FR, u % R, k, :], w1_hi[:, s, w], w1_lo[:, s, w], h_hi[:, t], h_lo[:, t],
                                          True)
                    mm.then_inc(up_full.sem, 1)

                def down_proj(e, s, u):
                    n = e * U + u
                    c, f = divmod(u, FB)
                    if u == 0:
                        pe.wait_ge(*w2_split(e + 1))
                    pe.wait_ge(*a_made(n + 1))
                    w = slice(f * P, (f + 1) * P)
                    begins = not biased and isinstance(e, int) and e == 0 and f == 0
                    three_passes(y_ps[:, c, :], w2_hi[:, s, w], w2_lo[:, s, w], a_hi[:, u % 4, :], a_lo[:, u % 4, :],
                                 begins).then_inc(down_done.sem, 1)

                def window(e, s, first=False, last=False):
                    for u in range(U):
                        up_proj(e, s, u, first)
                        if u >= LAG:
                            down_proj(e, s, u - LAG)
                        elif not first:
                            down_proj(e - 1, 1 - s, u - LAG + U)
                    if last:
                        for u in range(U - LAG, U):
                            down_proj(e, s, u)

                if biased:
                    for b in range(B):
                        pe.matmul(y_ps[:, b, :], core.b2[0:E, :], core.g_t[0:E, b * S:(b + 1) * S], start=True,
                                  stop=True, skip_group_check=True)
                run(pe, window)
                for b in range(B):
                    pe.wait_ge(*y_copied(b + 1))
                    for q in range(Q):
                        mm = pe.transpose(token_bank(b)[:, q * P:(q + 1) * P], y_sb[:, b, q * P:(q + 1) * P],
                                          core.ident[:])
                    mm.then_inc(y_turned.sem, 1)

            @block.scalar
            def _(act):
                ahead = 2 if glu else 1

                def high(n, u):
                    act.wait_ge(*weighed(n + 1))
                    if not isinstance(n, int) or n >= 4:
                        act.wait_ge(*down_done(n - 4 + 1))
                    act.copy(a_hi[:, u % 4, :], a_f[:, u % 4, :]).then_inc(a_high.sem, 1)

                def window(e, s, first=False, last=False):
                    for u in range(U):
                        n = e * U + u
                        f = u % FB
                        act.wait_ge(*up_full(n + 1))
                        if u == 0 and b1 is not None:
                            act.wait_ge(*bslot[s](16 * (e // 2 + 1)))
                        if not (first and u < 2):
                            act.wait_ge(*(product_made if glu else weighed)(n - 2 + 1))
                        bias = b1_s[:, s, parts * f:parts * f + 1] if b1 is not None else 0.0
                        act.activation(act_s[:, u % 2, :], up[0:FR, u % R, 0, :], func, bias=bias)\
                           .then_inc(activated.sem, 1)
                        if not (first and u < ahead):
                            high(n - ahead, (u - ahead) % U)
                    if last:
                        for u in range(U - ahead, U):
                            high(e * U + u, u)

                for b in range(B):
                    act.copy(h_hi[:, b * S:(b + 1) * S], core.h[:, b * S:(b + 1) * S]).then_inc(h_high.sem, 1)
                run(act, window)
                for b in range(B):
                    act.wait_ge(*down_done(E * U - U + (b + 1) * FB))
                    act.copy(y_sb[:, b, :], y_ps[:, b, :]).then_inc(y_copied.sem, 1)

            @block.vector
            def _(dve):
                def product(e, s, u, first):
                    n = e * U + u
                    f = u % FB
                    if u == 0 and b1 is not None:
                        dve.wait_ge(*bslot[s](16 * (e // 2 + 1)))
                    dve.wait_ge(*activated(n + 1))
                    if not (first and u < 2):
                        dve.wait_ge(*weighed(n - 2 + 1))
                    out, lin = prod[:, u % 2, :], up[0:FR, u % R, 1, :]
                    if b1 is None:
                        ins = dve.tensor_tensor(out, lin, act_s[:, u % 2, :], ALU.mult)
                    else:
                        ins = dve.scalar_tensor_tensor(out, lin, b1_s[:, s, 2 * f + 1:2 * f + 2],
                                                       act_s[:, u % 2, :], ALU.add, ALU.mult)
                    ins.then_inc(product_made.sem, 1)

                def weigh(e, s, u, first):
                    n = e * U + u
                    c = u // FB
                    if u % (U // 2) == 0:
                        dve.wait_ge(*gslot[s][u // (U // 2)](16 * (e // 2 + 1)))
                    dve.wait_ge(*(product_made if glu else activated)(n + 1))
                    if not (first and u < 4):
                        dve.wait_ge(*a_made(n - 4 + 1))
                    dve.tensor_tensor(a_f[:, u % 4, :], prod[:, u % 2, :], g_s[0:FR, s, c * S:(c + 1) * S],
                                      ALU.mult).then_inc(weighed.sem, 1)

                def low(n, u):
                    dve.wait_ge(*a_high(n + 1))
                    dve.tensor_tensor(a_lo[:, u % 4, :], a_f[:, u % 4, :], a_hi[:, u % 4, :].bitcast(F32), ALU.subtract)\
                       .then_inc(a_made.sem, 1)

                behind = 1 if glu else 0

                def window(e, s, first=False, last=False):
                    for u in range(U):
                        if glu:
                            product(e, s, u, first)
                        if u >= behind:
                            weigh(e, s, u - behind, first)
                        elif not first:
                            weigh(e - 1, 1 - s, u - behind + U, False)
                        if not (first and u < behind + 1):
                            low(e * U + u - behind - 1, (u - behind - 1) % U)
                    if last:
                        for u in range(U - behind, U):
                            weigh(e, s, u, False)
                        for u in range(U - behind - 1, U):
                            low(e * U + u, u)

                for b in range(B):
                    t = slice(b * S, (b + 1) * S)
                    dve.wait_ge(*h_high(b + 1))
                    dve.tensor_tensor(h_lo[:, t], core.h[:, t], h_hi[:, t].bitcast(F32), ALU.subtract)\
                       .then_inc(h_split.sem, 1)
                run(dve, window)
                for b in range(B):
                    dve.wait_ge(*y_turned(b + 1))
                    dve.tensor_tensor(y_x[:, b, :].rearrange("p (q d) -> p q d", q=Q),
                                      token_bank(b).rearrange("p (q d) -> p q d", q=Q),
                                      core.gate[:, layer, 1, b, :].unsqueeze(1).broadcast_to([P, Q, P]),
                                      ALU.mult).then_inc(final.sem, 1)
                    dve.wait_ge(*final(b + 1))
                    xb = core.x[:, Q * b:Q * b + Q, :]
                    dve.tensor_tensor(xb, xb, y_x[:, b, :].rearrange("p (q d) -> p q d", q=Q), ALU.add)
    units = E * U
    stage_ends(core, h_high=B, h_split=B, up_full=units, activated=units, product_made=units if glu else 0,
               weighed=units, a_high=units, a_made=units, down_done=units, w1_high=E, w1_split=E,
               w2_scaled=E if mult is not None else 0, w2_high=E, w2_split=E, y_copied=B, y_turned=B, dve_step=B,
               weights_slot0=16 * loads * ((E + 1) // 2), weights_slot1=16 * loads * (E // 2),
               biases_slot0=16 * ((E + 1) // 2) if b1 is not None else 0,
               biases_slot1=16 * (E // 2) if b1 is not None else 0,
               **{f"token_weights_slot{s}_half{k}": 16 * ((E + 1 - s) // 2) for s in range(2) for k in range(2)})


def latents(core, wkd, bkd, out):
    nc = core.nc
    loaded, full, gelu, lat = (signal(core, n) for n in ("loaded", "lat_psum", "lat_gelu", "lat_made"))
    rest_set = signal(core, "lat_rest_set")
    with ExitStack() as ctx:
        w = ctx.enter_context(nc.sbuf_tensor("wkd_sb", [P, 2, 32], F32))
        bb = ctx.enter_context(nc.sbuf_tensor("bkd_sb", [32, 2], F32))
        g = ctx.enter_context(nc.sbuf_tensor("lat_gelu_sb", [32, B, 2, S], F32))
        ps = ctx.enter_context(nc.psum_tensor("lat_ps", [32, B, 2, S], F32))
        with nc.Block() as block:

            @block.sync
            def _(sp):
                sp.dma_start(w[:], wkd.rearrange("a k n -> k a n")).then_inc(loaded.sem, 16)
                sp.dma_start(bb[:], bkd).then_inc(loaded.sem, 16)

            @block.gpsimd
            def _(pool):
                pool.memset(out[:], 0.0).then_inc(rest_set.sem, 1)
                pool.wait_ge(*rest_set(1))
                pool.memset(out[32:33, :], 1.0).then_inc(rest_set.sem, 1)

            @block.tensor
            def _(pe):
                pe.wait_ge(*loaded(32))
                for b in range(B):
                    for a in range(2):
                        mm = pe.matmul(ps[:, b, a, :], w[:, a, :], core.h[:, b * S:(b + 1) * S], start=True, stop=True)
                    mm.then_inc(full.sem, 1)

            @block.scalar
            def _(act):
                for b in range(B):
                    act.wait_ge(*full(b + 1))
                    for a in range(2):
                        ins = act.activation(g[:, b, a, :], ps[:, b, a, :], ACT.Gelu, bias=bb[:, a:a + 1])
                    ins.then_inc(gelu.sem, 1)

            @block.vector
            def _(dve):
                dve.wait_ge(*rest_set(1))
                for b in range(B):
                    dve.wait_ge(*gelu(b + 1))
                    dve.tensor_tensor(out[0:32, b * S:(b + 1) * S], g[:, b, 0, :], g[:, b, 1, :], ALU.add)\
                       .then_inc(lat.sem, 1)
    stage_ends(core, loaded=32, lat_psum=B, lat_gelu=B, lat_made=B, lat_rest_set=2)


def rms_norm(core, name, layer, half, eps, w, out_tok, out_feat):
    nc = core.nc
    names = ("loaded", "squared", "sq_summed", "rms_step", "rms_root", "h_turned", "h_scaled", "n_turned", "n_made")
    (loaded, squared, summed, step, root, h_turned, h_scaled, n_turned, n_made) = (signal(core, n) for n in names)
    with ExitStack() as ctx:
        tmp = lambda nm, shape, dt=F32: ctx.enter_context(nc.sbuf_tensor(f"{nm}_{name}", shape, dt))
        w_sb = tmp("rms_w", [P, 1])
        sq = tmp("rms_sq", [P, T])
        ms = tmp("rms_ms", [P, NT])
        sd = tmp("rms_sd", [P, NT])
        rs = tmp("rms_rs", [P, NT])
        hg = tmp("rms_hg", [P, 2, Q, P])
        s_ps = ctx.enter_context(nc.psum_tensor(f"rms_s_{name}", [P, NT], F32))
        h_ps = ctx.enter_context(nc.psum_tensor(f"rms_h_{name}", [P, 2, S], F32))
        n_ps = ctx.enter_context(nc.psum_tensor(f"rms_n_{name}", [P, 2, S], F32))
        with nc.Block() as block:

            @block.sync
            def _(sp):
                sp.dma_start(w_sb[:], w).then_inc(loaded.sem, 16)

            @block.scalar
            def _(act):
                act.wait_ge(*loaded(16))
                for b in range(B):
                    act.activation(sq[:, b * S:(b + 1) * S], core.h[:, b * S:(b + 1) * S], ACT.Square)\
                       .then_inc(squared.sem, 1)
                act.wait_ge(*step(1))
                act.activation(sd[:], ms[:], ACT.Sqrt).then_inc(root.sem, 1)
                for b in range(B):
                    act.wait_ge(*n_turned(b + 1))
                    act.activation(out_feat[:, b * S:(b + 1) * S], n_ps[:, b % 2, :], ACT.Copy, scale=w_sb[:, 0:1])\
                       .then_inc(n_made.sem, 1)

            def turn_back(pe, b):
                pe.wait_ge(*h_scaled(b + 1))
                if b >= 2:
                    pe.wait_ge(*n_made(b - 1))
                for q in range(Q):
                    mm = pe.transpose(n_ps[:, b % 2, q * P:(q + 1) * P], out_tok[:, b * Q + q, :], core.ident[:])
                mm.then_inc(n_turned.sem, 1)

            @block.tensor
            def _(pe):
                for b in range(B):
                    pe.wait_ge(*squared(b + 1))
                    for t in range(b * Q, b * Q + Q):
                        mm = pe.matmul(s_ps[:, t:t + 1], sq[:, t * P:(t + 1) * P], core.ones[:, 0:1], start=True,
                                       stop=True)
                mm.then_inc(summed.sem, 1)
                for b in range(B):
                    if b >= 2:
                        pe.wait_ge(*h_scaled(b - 1))
                    for q in range(Q):
                        t = b * Q + q
                        mm = pe.transpose(h_ps[:, b % 2, q * P:(q + 1) * P], core.h[:, t * P:(t + 1) * P], core.ident[:])
                    mm.then_inc(h_turned.sem, 1)
                    if b >= 1:
                        turn_back(pe, b - 1)
                turn_back(pe, B - 1)

            @block.vector
            def _(dve):
                dve.wait_ge(*summed(1))
                dve.tensor_scalar(ms[:], s_ps[:], 1.0 / P, eps, ALU.mult, ALU.add).then_inc(step.sem, 1)
                dve.wait_ge(*root(1))
                dve.reciprocal(rs[:], sd[:]).then_inc(step.sem, 1)
                dve.wait_ge(*step(2))
                for b in range(B):
                    dve.wait_ge(*h_turned(b + 1))
                    h3 = h_ps[:, b % 2, :].rearrange("p (q d) -> p q d", q=Q)
                    dve.tensor_tensor(hg[:, b % 2], h3, core.gate[:, layer, half, b, :].unsqueeze(1)
                                      .broadcast_to([P, Q, P]), ALU.mult).then_inc(step.sem, 1)
                    dve.tensor_tensor(out_tok[:, b * Q:b * Q + Q, :], h3,
                                      rs[:, b * Q:b * Q + Q].unsqueeze(2).broadcast_to([P, Q, P]), ALU.mult)\
                       .then_inc(h_scaled.sem, 1)
                    dve.wait_ge(*step(3 + b))
                    xb = core.x[:, b * Q:b * Q + Q, :]
                    dve.tensor_tensor(xb, xb, hg[:, b % 2], ALU.add)
    stage_ends(core, loaded=16, squared=B, sq_summed=1, rms_step=2 + B, rms_root=1, h_turned=B, h_scaled=B, n_turned=B,
             n_made=B)


def gated_scan(core, layer, xn, w_in, b_uz, b_g, w_x, w_dt, b_xdt, w_out, b_out):
    nc = core.nc
    H = 64
    names = ("loaded", "p_full", "uz_made", "sg_made", "ud_full", "ut_made", "dt_made", "scan_step", "y_made",
             "out_full", "out_added", "gs_cleared")
    (loaded, p_full, uz_made, sg_made, ud_full, ut_made, dt_made, step, y_made, out_full, out_added, cleared) = (
        signal(core, n) for n in names)
    with ExitStack() as ctx:
        tmp = lambda nm, shape, dt=F32: ctx.enter_context(nc.sbuf_tensor(f"gs_{nm}", shape, dt))
        win = tmp("w_in", [P, 3 * H])
        buz, bg = tmp("b_uz", [P, 1]), tmp("b_g", [H, 1])
        wxdt = tmp("w_xdt", [P, P])
        bxdt = tmp("b_xdt", [P, 1])
        wout = tmp("w_out", [P, P])
        uz, sg, ut, dt, a, bb, h, y = (tmp(n, [P, 2, S]) for n in "uz sg ut dt a b h y".split())
        r = slice(H, P)
        og = tmp("og", [P, 2, Q, P])
        p_ps = ctx.enter_context(nc.psum_tensor("gs_p", [P, 2, S], F32))
        ud_ps = ctx.enter_context(nc.psum_tensor("gs_ud", [P, S], F32))
        o_ps = ctx.enter_context(nc.psum_tensor("gs_o", [P, 2, S], F32))
        with nc.Block() as block:

            @block.sync
            def _(sp):
                for dst, src in ((win, w_in), (buz, b_uz), (bg, b_g), (bxdt, b_xdt)):
                    sp.dma_start(dst[:], src).then_inc(loaded.sem, 16)
                sp.wait_ge(*cleared(4))
                for dst, src in ((wxdt[0:H, 0:H], w_x), (wxdt[r, r], w_dt), (wout[r, :], w_out), (wout[0:1, :], b_out)):
                    sp.dma_start(dst, src).then_inc(loaded.sem, 16)

            @block.gpsimd
            def _(pool):
                for m in (wxdt, wout, y):
                    pool.memset(m[:], 0.0).then_inc(cleared.sem, 1)
                pool.wait_ge(*cleared(3))
                pool.memset(y[0:1], 1.0).then_inc(cleared.sem, 1)

            @block.tensor
            def _(pe):
                def project_in(b):
                    if b:
                        pe.wait_ge(*uz_made(b))
                        pe.wait_ge(*sg_made(b))
                    for k, m in enumerate((P, H)):
                        mm = pe.matmul(p_ps[0:m, k, :], win[:, k * P:k * P + m], xn[:, b * S:(b + 1) * S], start=True,
                                       stop=True)
                    mm.then_inc(p_full.sem, 1)

                pe.wait_ge(*loaded(16 * 8))
                project_in(0)
                for b in range(B):
                    pe.wait_ge(*uz_made(b + 1))
                    if b:
                        pe.wait_ge(*ut_made(b))
                        pe.wait_ge(*dt_made(b))
                    pe.matmul(ud_ps[:], wxdt[:], uz[:, b % 2, :], start=True, stop=True).then_inc(ud_full.sem, 1)
                    if b + 1 < B:
                        project_in(b + 1)
                    pe.wait_ge(*y_made(b + 1))
                    if b >= 2:
                        pe.wait_ge(*out_added(b - 1))
                    for q in range(Q):
                        at = slice(q * P, (q + 1) * P)
                        mm = pe.matmul(o_ps[:, b % 2, at], y[:, b % 2, at], wout[:], start=True, stop=True)
                    mm.then_inc(out_full.sem, 1)

            @block.scalar
            def _(act):
                act.wait_ge(*loaded(16 * 8))
                for b in range(B):
                    act.wait_ge(*p_full(b + 1))
                    act.activation(uz[:, b % 2, :], p_ps[:, 0, :], ACT.Identity, bias=buz[:, 0:1])\
                       .then_inc(uz_made.sem, 1)
                    if b >= 2:
                        act.wait_ge(*y_made(b - 1))
                    act.activation(sg[r, b % 2, :], p_ps[0:H, 1, :], ACT.Sigmoid, bias=bg[:, 0:1])\
                       .then_inc(sg_made.sem, 1)
                    act.wait_ge(*ud_full(b + 1))
                    act.activation(ut[r, b % 2, :], ud_ps[0:H, :], ACT.Tanh, bias=bxdt[0:H, 0:1]).then_inc(ut_made.sem, 1)
                    act.activation(dt[r, b % 2, :], ud_ps[r, :], ACT.Sigmoid, bias=bxdt[r, 0:1])\
                       .then_inc(dt_made.sem, 1)

            @block.vector
            def _(dve):
                dve.wait_ge(*cleared(4))
                n = 0
                for b in range(B):
                    k = b % 2
                    dve.wait_ge(*ut_made(b + 1))
                    dve.wait_ge(*dt_made(b + 1))
                    dve.tensor_scalar(a[r, k, :], dt[r, k, :], -1.0, 1.0, ALU.mult, ALU.add).then_inc(step.sem, 1)
                    dve.tensor_tensor(bb[r, k, :], dt[r, k, :], ut[r, k, :], ALU.mult).then_inc(step.sem, 1)
                    dve.wait_ge(*step(n + 2))
                    dve.tensor_tensor_scan(h[r, k, :], a[r, k, :], bb[r, k, :], 0.0, ALU.mult, ALU.add)\
                       .then_inc(step.sem, 1)
                    dve.wait_ge(*step(n + 3))
                    dve.wait_ge(*sg_made(b + 1))
                    dve.tensor_tensor(y[r, k, :], h[r, k, :], sg[r, k, :], ALU.mult).then_inc(y_made.sem, 1)
                    dve.wait_ge(*out_full(b + 1))
                    dve.tensor_tensor(og[:, k], o_ps[:, k, :].rearrange("p (q d) -> p q d", q=Q),
                                      core.gate[:, layer, 0, b, :].unsqueeze(1).broadcast_to([P, Q, P]), ALU.mult)\
                       .then_inc(out_added.sem, 1)
                    dve.wait_ge(*out_added(b + 1))
                    xb = core.x[:, b * Q:b * Q + Q, :]
                    dve.tensor_tensor(xb, xb, og[:, k], ALU.add)
                    n += 3
    stage_ends(core, loaded=128, gs_cleared=4, p_full=B, uz_made=B, sg_made=B, ud_full=B, ut_made=B, dt_made=B, scan_step=3 * B,
             y_made=B, out_full=B, out_added=B)


def dispatch(core, hot, ws, idx_f, slot, tokens):
    nc = core.nc
    step, tri_set, m_set, r_set, pos_full, slot_set, scattered = (signal(core, n) for n in (
        "dve_step", "tri_set", "m_set", "r_set", "pos_full", "slot_set", "scattered"))
    zeroed = signal(core, "slots_zeroed")
    E = L3_E
    counts = {}
    with ExitStack() as ctx:
        tmp = lambda name, shape, dt=F32: ctx.enter_context(nc.sbuf_tensor(f"d_{name}", shape, dt))
        tri = tmp("tri", [P, P], BF16)
        ones = tmp("ones", [P, P], BF16)
        m = tmp("m", [P, NT, E], BF16)
        before = tmp("before", [P, NT, E], BF16)
        wide = tmp("wide", [P, NT, E])
        pos = tmp("pos", [P, 2, NT])
        over = tmp("over", [P, 2, NT])
        slot_f = tmp("slot_f", [P, 2, NT])
        ps = ctx.enter_context(nc.psum_tensor("pos_ps", [P, NT, E], F32))
        with nc.Block() as block:

            @block.gpsimd
            def _(pool):
                pool.memset(ones[:], 1.0).then_inc(tri_set.sem, 1)
                pool.wait_ge(*tri_set(1))
                pool.affine_select(out=tri[:], in_=ones[:], compare_op=ALU.is_gt, fill=0.0, base=0, pattern=[[1, P]],
                                   channel_multiplier=-1).then_inc(tri_set.sem, 1)
                pool.wait_ge(*zeroed(16 * ZERO_FILLS))
                pool.wait_ge(*slot_set(1))
                for k in range(2):
                    for t in range(NT):
                        pool.indirect_dma_start(out=core.slots_in,
                                                out_offset=bass.IndirectOffsetOnAxis(ap=slot[:, k, t:t + 1], axis=0),
                                                in_=tokens[:, t, :], in_offset=None, bounds_check=L3_SLOTS - 1,
                                                oob_is_err=False).then_inc(scattered.sem, 16)
                pool.wait_ge(*scattered(16 * 2 * NT))

            @block.tensor
            def _(pe):
                pe.wait_ge(*tri_set(2))
                pe.wait_ge(*m_set(1))
                pe.wait_ge(*r_set(NT))
                for t in range(NT):
                    pe.matmul(ps[:, t, :], tri[:], m[:, t, :], start=True, stop=False)
                    mm = pe.matmul(ps[:, t, :], ones[:], before[:, t, :], start=False, stop=True)
                mm.then_inc(pos_full.sem, 1)

            @block.vector
            def _(dve):
                n = 0

                def link(ins):
                    nonlocal n
                    n += 1
                    ins.then_inc(step.sem, 1)
                    dve.wait_ge(*step(n))

                dve.tensor_tensor(m[:], hot[:, 0], hot[:, 1], ALU.add).then_inc(m_set.sem, 1)
                dve.memset(before[:, 0, :], 0.0).then_inc(r_set.sem, 1)
                dve.wait_ge(*m_set(1))
                for t in range(1, NT):
                    dve.wait_ge(*r_set(t))
                    dve.tensor_tensor(before[:, t, :], before[:, t - 1, :], m[:, t - 1, :], ALU.add)\
                       .then_inc(r_set.sem, 1)
                dve.wait_ge(*pos_full(1))
                for k in range(2):
                    link(dve.tensor_tensor(wide[:], ps[:], hot[:, k], ALU.mult))
                    link(dve.tensor_reduce(pos[:, k, :], wide[:], AX_X, ALU.add))
                link(dve.tensor_scalar(over[:], pos[:], float(CAP), None, ALU.is_lt))
                link(dve.tensor_tensor(ws[:], ws[:], over[:], ALU.mult))
                for k in range(2):
                    last = dve.tensor_scalar(slot_f[:, k, :], idx_f[:, :, k], float(CAP), None, ALU.mult)
                link(last)
                link(dve.tensor_tensor(slot_f[:], slot_f[:], pos[:], ALU.add))
                link(dve.tensor_scalar(over[:], pos[:], float(CAP), float(4 * L3_SLOTS), ALU.is_ge, ALU.mult))
                link(dve.tensor_tensor(slot_f[:], slot_f[:], over[:], ALU.add))
                dve.tensor_copy(slot[:], slot_f[:]).then_inc(slot_set.sem, 1)
                counts.update(step=n)
    stage_ends(core, dve_step=counts["step"], tri_set=2, m_set=1, r_set=NT, pos_full=1, slot_set=1, scattered=32 * NT,
             slots_zeroed=16 * ZERO_FILLS)


def slot_experts(core, rms_w, w13, w2):
    nc = core.nc
    G = 4
    NW = L3_E // G
    RING = 4
    H = 64
    names = ("loaded", "xb_turned", "xt_made", "gu_full", "silu_made", "hh_made", "yb_full", "yb_copied")
    (loaded, xb_turned, xt_made, gu_full, silu_made, hh_made, yb_full, yb_copied) = (signal(core, n) for n in names)
    hh_cleared = signal(core, "hh_cleared")
    ring = [signal(core, f"ring_slot{k}") for k in range(RING)]
    stored = [signal(core, "stored_even"), signal(core, "stored_odd")]
    src = core.slots_in.rearrange("(w j p) d -> w p j d", j=G, p=P)
    dst = core.slots_out.rearrange("(w j p) d -> w p j d", j=G, p=P)
    w13_v = w13.rearrange("(w j) k n -> w k j n", j=G)
    w2_v = w2.rearrange("(w a t) k n -> w (t k) a n", a=G // 2, t=2)
    with ExitStack() as ctx:
        tmp = lambda name, shape, dt=F32: ctx.enter_context(nc.sbuf_tensor(f"se_{name}", shape, dt))
        rw = tmp("rms_w", [P, 1])
        xb = tmp("xb", [P, RING, G, P])
        w13_s = tmp("w13", [P, RING, G, P])
        w2_s = tmp("w2", [P, RING, G // 2, P])
        xt = tmp("xt", [P, 2, S])
        sg = tmp("sg", [P, 2, S])
        hh = tmp("hh", [P, 2, S])
        y = tmp("y", [P, 2, G, P])
        t_ps = ctx.enter_context(nc.psum_tensor("se_t", [P, 2, S], F32))
        gu_ps = ctx.enter_context(nc.psum_tensor("se_gu", [P, 2, S], F32))
        y_ps = ctx.enter_context(nc.psum_tensor("se_y_ps", [P, 2, S], F32))

        def run(eng, window):
            for i in range(RING):
                window(i, i)
            with eng.Fori(1, NW // RING) as r:
                for k in range(RING):
                    window(r * RING + k, k)
            for i in range(NW, NW + 2):
                window(i, i % RING)

        new = lambda i: not isinstance(i, int) or i < NW
        old = lambda i, n: not isinstance(i, int) or i >= n
        with nc.Block() as block:

            @block.sync
            def _(sp):
                sp.dma_start(rw[:], rms_w).then_inc(loaded.sem, 16)

                def window(i, k):
                    if new(i):
                        if old(i, RING):
                            sp.wait_ge(*yb_full(i - RING + 1))
                        sp.dma_start(xb[:, k], src[i]).then_inc(ring[k].sem, 16)
                        sp.dma_start(w13_s[:, k], w13_v[i]).then_inc(ring[k].sem, 16)
                        sp.dma_start(w2_s[:, k], w2_v[i]).then_inc(ring[k].sem, 16)

                run(sp, window)

            @block.tensor
            def _(pe):
                def window(i, k):
                    if new(i):
                        pe.wait_ge(*ring[k](48 * (i // RING + 1)))
                        if old(i, 2):
                            pe.wait_ge(*xt_made(i - 1))
                        for j in range(G):
                            mm = pe.transpose(t_ps[:, k % 2, j * P:(j + 1) * P], xb[:, k, j, :], core.ident[:])
                        mm.then_inc(xb_turned.sem, 1)
                    if old(i, 1) and (not isinstance(i, int) or i - 1 < NW):
                        kk = (k - 1) % RING
                        pe.wait_ge(*xt_made(i))
                        if old(i, 3):
                            pe.wait_ge(*hh_made(i - 2))
                        for j in range(G):
                            at = slice(j * P, (j + 1) * P)
                            mm = pe.matmul(gu_ps[:, kk % 2, at], w13_s[:, kk, j, :], xt[:, kk % 2, at], start=True,
                                           stop=True)
                        mm.then_inc(gu_full.sem, 1)
                    if old(i, 2):
                        kk = (k - 2) % RING
                        pe.wait_ge(*hh_made(i - 1))
                        if old(i, 4):
                            pe.wait_ge(*yb_copied(i - 3))
                        for j in range(G):
                            at = slice(j * P, (j + 1) * P)
                            mm = pe.matmul(y_ps[:, kk % 2, at], hh[:, kk % 2, at], w2_s[:, kk, j // 2, :], start=True,
                                           stop=True)
                        mm.then_inc(yb_full.sem, 1)

                run(pe, window)

            @block.scalar
            def _(act):
                def window(i, k):
                    if new(i):
                        act.wait_ge(*xb_turned(i + 1))
                        if old(i, 2):
                            act.wait_ge(*gu_full(i - 1))
                        act.activation(xt[:, k % 2, :], t_ps[:, k % 2, :], ACT.Copy, scale=rw[:, 0:1])\
                           .then_inc(xt_made.sem, 1)
                    if old(i, 1) and (not isinstance(i, int) or i - 1 < NW):
                        kk = (k - 1) % RING
                        act.wait_ge(*gu_full(i))
                        act.activation(sg[H:P, kk % 2, :], gu_ps[0:H, kk % 2, :], ACT.Silu).then_inc(silu_made.sem, 1)

                act.wait_ge(*loaded(16))
                run(act, window)

            @block.vector
            def _(dve):
                def window(i, k):
                    if old(i, 1) and (not isinstance(i, int) or i - 1 < NW):
                        kk = (k - 1) % RING
                        dve.wait_ge(*silu_made(i))
                        if old(i, 3):
                            dve.wait_ge(*yb_full(i - 2))
                        for t in range(2):
                            mine = lambda a, rows: a[rows, kk % 2, :].rearrange("p (a t c) -> p a t c", t=2,
                                                                                c=P)[:, :, t, :]
                            up = slice(H, P)
                            last = dve.tensor_tensor(mine(hh, slice(t * H, t * H + H)), mine(sg, up),
                                                     mine(gu_ps, up), ALU.mult)
                        last.then_inc(hh_made.sem, 1)
                    if old(i, 2):
                        kk = (k - 2) % RING
                        dve.wait_ge(*yb_full(i - 1))
                        if old(i, 4):
                            dve.wait_ge(*stored[kk % 2](16 * ((i - 2) // 2)))
                        dve.tensor_copy(y[:, kk % 2], y_ps[:, kk % 2, :].rearrange("p (j d) -> p j d", j=G))\
                           .then_inc(yb_copied.sem, 1)

                dve.wait_ge(*hh_cleared(1))
                run(dve, window)

            @block.gpsimd
            def _(pool):
                pool.memset(hh[:], 0.0).then_inc(hh_cleared.sem, 1)

                def window(i, k):
                    if old(i, 2):
                        kk = (k - 2) % RING
                        pool.wait_ge(*yb_copied(i - 1))
                        pool.dma_start(dst[i - 2], y[:, kk % 2]).then_inc(stored[kk % 2].sem, 16)

                run(pool, window)
                for s in stored:
                    pool.wait_ge(*s(16 * NW // 2))
    stage_ends(core, loaded=16, hh_cleared=1, xb_turned=NW, xt_made=NW, gu_full=NW, silu_made=NW, hh_made=NW, yb_full=NW, yb_copied=NW,
             ring_slot0=12 * NW, ring_slot1=12 * NW, ring_slot2=12 * NW, ring_slot3=12 * NW,
             stored_even=8 * NW, stored_odd=8 * NW)


def combine(core, xn, ws, slot, w_gate, w_up, w_down):
    nc = core.nc
    H = 64
    names = ("loaded", "y_cleared", "gu_full", "silu_made", "hh_made", "shared_full", "mix_step")
    (loaded, cleared, gu_full, silu_made, hh_made, shared_full, step) = (signal(core, n) for n in names)
    gathered = [signal(core, f"gathered{b}") for b in range(B)]
    with ExitStack() as ctx:
        tmp = lambda name, shape, dt=F32: ctx.enter_context(nc.sbuf_tensor(f"cm_{name}", shape, dt))
        wg, wu = tmp("w_gate", [P, H]), tmp("w_up", [P, H])
        wd = tmp("w_down", [H, P])
        y = tmp("y", [P, 2, NT, P])
        sg, hh = tmp("sg", [H, 2, S]), tmp("hh", [H, 2, S])
        acc = tmp("acc", [P, NT, P])
        gu = ctx.enter_context(nc.psum_tensor("cm_gu", [H, 2, 2, S], F32))
        sh = ctx.enter_context(nc.psum_tensor("cm_sh", [P, B, S], F32))
        with nc.Block() as block:

            @block.sync
            def _(sp):
                for dst, src in ((wg, w_gate), (wu, w_up), (wd, w_down)):
                    sp.dma_start(dst[:], src).then_inc(loaded.sem, 16)

            @block.gpsimd
            def _(pool):
                pool.memset(y[:], 0.0).then_inc(cleared.sem, 1)
                pool.wait_ge(*cleared(1))
                for t in range(NT):
                    for k in range(2):
                        pool.indirect_dma_start(out=y[:, k, t, :], out_offset=None, in_=core.slots_out,
                                                in_offset=bass.IndirectOffsetOnAxis(ap=slot[:, k, t:t + 1], axis=0),
                                                bounds_check=L3_SLOTS - 1, oob_is_err=False)\
                            .then_inc(gathered[t // Q].sem, 16)

            @block.tensor
            def _(pe):
                def up(b):
                    if b >= 2:
                        pe.wait_ge(*hh_made(b - 1))
                    pe.matmul(gu[:, b % 2, 0, :], wg[:], xn[:, b * S:(b + 1) * S], start=True, stop=True)
                    pe.matmul(gu[:, b % 2, 1, :], wu[:], xn[:, b * S:(b + 1) * S], start=True, stop=True)\
                      .then_inc(gu_full.sem, 1)

                pe.wait_ge(*loaded(48))
                up(0)
                for b in range(B):
                    if b + 1 < B:
                        up(b + 1)
                    pe.wait_ge(*hh_made(b + 1))
                    for q in range(Q):
                        mm = pe.matmul(sh[:, b, q * P:(q + 1) * P], hh[:, b % 2, q * P:(q + 1) * P], wd[:], start=True,
                                       stop=True)
                    mm.then_inc(shared_full.sem, 1)

            @block.scalar
            def _(act):
                for b in range(B):
                    act.wait_ge(*gu_full(b + 1))
                    act.activation(sg[:, b % 2, :], gu[:, b % 2, 0, :], ACT.Silu).then_inc(silu_made.sem, 1)

            @block.vector
            def _(dve):
                for b in range(B):
                    dve.wait_ge(*silu_made(b + 1))
                    if b >= 2:
                        dve.wait_ge(*shared_full(b - 1))
                    dve.tensor_tensor(hh[:, b % 2, :], sg[:, b % 2, :], gu[:, b % 2, 1, :], ALU.mult)\
                       .then_inc(hh_made.sem, 1)
                n = 0
                for b in range(B):
                    dve.wait_ge(*shared_full(b + 1))
                    dve.wait_ge(*gathered[b](16 * 2 * Q))
                    for k in range(2):
                        for q in range(Q):
                            t = b * Q + q
                            base = sh[:, b, q * P:(q + 1) * P] if k == 0 else acc[:, t, :]
                            last = dve.scalar_tensor_tensor(acc[:, t, :], y[:, k, t, :], ws[:, k, t:t + 1], base, ALU.mult,
                                                            ALU.add)
                        last.then_inc(step.sem, 1)
                        n += 1
                        dve.wait_ge(*step(n))
                    ab, xb = acc[:, b * Q:b * Q + Q, :], core.x[:, b * Q:b * Q + Q, :]
                    dve.tensor_tensor(ab, ab, core.gate[:, 3, 1, b, :].unsqueeze(1).broadcast_to([P, Q, P]), ALU.mult)\
                       .then_inc(step.sem, 1)
                    n += 1
                    dve.wait_ge(*step(n))
                    dve.tensor_tensor(xb, xb, ab, ALU.add)
    stage_ends(core, loaded=48, y_cleared=1, gu_full=B, silu_made=B, hh_made=B, shared_full=B, mix_step=3 * B,
             **{f"gathered{b}": 32 * Q for b in range(B)})


INS = {
    "x": lambda a: a["L0_attn_x"],
    "ct": lambda a: np.concatenate([a[f"L{l}_c"] for l in range(LAYERS)], 0).T,
    "wmod": lambda a: np.stack([a[f"L{l}_wmod"].reshape(P, 6, P) for l in range(LAYERS)], 1),
    "l0_wq": lambda a: by_groups(a["L0_attn_Wq"], 8),
    "l0_wk": lambda a: by_groups(a["L0_attn_Wk"], 8),
    "l0_wv": lambda a: a["L0_attn_Wv"],
    "l0_wo": lambda a: a["L0_attn_Wo"].reshape(8, P, P),
    "l0_bo": lambda a: a["L0_attn_bo"].reshape(1, P),
    "l0_gw": lambda a: a["L0_ffn_gate_w"],
    "l0_gb": lambda a: a["L0_ffn_gate_b"].reshape(1, 8),
    "l0_w1": lambda a: a["L0_ffn_W1"],
    "l0_b1": lambda a: a["L0_ffn_b1"].reshape(8, 4, P).transpose(0, 2, 1),
    "l0_w2": lambda a: by_rows(a["L0_ffn_W2"], 4),
    "l0_b2": lambda a: a["L0_ffn_b2"],
    "l1_wq": lambda a: spread_heads(a["L1_attn_Wq"]),
    "l1_bq": lambda a: spread_heads(a["L1_attn_bq"].reshape(1, P))[:, 0, :].T,
    "l1_wkd": lambda a: a["L1_attn_Wkd"].reshape(P, 2, 32).transpose(1, 0, 2),
    "l1_bkd": lambda a: a["L1_attn_bkd"].reshape(2, 32).T,
    "l1_wku": lambda a: spread_heads(a["L1_attn_Wku"][:, :P]),
    "l1_minus": lambda a: low_blocks(),
    "l1_bku": lambda a: spread_heads(a["L1_attn_bku"][:P].reshape(1, P))[:, 0, :].T,
    "l1_wv": lambda a: a["L1_attn_Wku"][:, P:],
    "l1_bv": lambda a: a["L1_attn_bku"][P:].reshape(1, P),
    "l1_wo": lambda a: a["L1_attn_Wo"].reshape(4, 32, P),
    "l1_bo": lambda a: a["L1_attn_bo"].reshape(1, P),
    "l1_gw": lambda a: a["L1_ffn_gate_w"].T,
    "l1_w1": lambda a: two_parts(a["L1_ffn_w1"], a["L1_ffn_w3"], 4),
    "l1_w2": lambda a: by_rows(a["L1_ffn_w2"].transpose(0, 2, 1), 4),
    "l2_nw": lambda a: a["L2_attn_norm_w"].reshape(P, 1),
    "l2_win": lambda a: a["L2_attn_W_in"],
    "l2_buz": lambda a: a["L2_attn_b_in"][:P].reshape(P, 1),
    "l2_bg": lambda a: a["L2_attn_b_in"][P:].reshape(64, 1),
    "l2_wx": lambda a: a["L2_attn_W_x"],
    "l2_wdt": lambda a: a["L2_attn_W_dt"],
    "l2_bxdt": lambda a: np.concatenate([a["L2_attn_b_x"], a["L2_attn_b_dt"]])[:, None],
    "l2_wout": lambda a: a["L2_attn_W_out"],
    "l2_bout": lambda a: a["L2_attn_b_out"].reshape(1, P),
    "l2_gw": lambda a: a["L2_ffn_gate_w"].T,
    "l2_w1": lambda a: two_parts(
        np.concatenate([a["L2_ffn_fc1_w"][:, P:], a["L2_ffn_s_fc1_w"][2 * P:].reshape(2, P, P)]),
        np.concatenate([a["L2_ffn_fc1_w"][:, :P], a["L2_ffn_s_fc1_w"][:2 * P].reshape(2, P, P)]), 1),
    "l2_b1": lambda a: np.stack([
        np.concatenate([a["L2_ffn_fc1_b"][:, P:], a["L2_ffn_s_fc1_b"][2 * P:].reshape(2, P)]),
        np.concatenate([a["L2_ffn_fc1_b"][:, :P], a["L2_ffn_s_fc1_b"][:2 * P].reshape(2, P)])], 2),
    "l2_mult": lambda a: np.concatenate([a["L2_ffn_geglu_mult"], a["L2_ffn_s_geglu_mult"].reshape(2, P)])[:, :, None],
    "l2_w2": lambda a: np.concatenate([a["L2_ffn_fc2_w"].transpose(0, 2, 1),
                                       a["L2_ffn_s_fc2_w"].T.reshape(2, P, P)]),
    "l2_b2": lambda a: np.concatenate([a["L2_ffn_fc2_b"], a["L2_ffn_s_fc2_b"].reshape(1, P),
                                       np.zeros((1, P), np.float32)]),
    "l3_wq": lambda a: by_groups(a["L3_attn_Wq"], 8),
    "l3_wk": lambda a: by_groups(a["L3_attn_Wk"], 8),
    "l3_wv": lambda a: a["L3_attn_Wv"],
    "l3_wo": lambda a: a["L3_attn_Wo"].reshape(8, P, P),
    "l3_bo": lambda a: a["L3_attn_bo"].reshape(1, P),
    "l3_rw": lambda a: a["L3_ffn_rms_w"].reshape(P, 1),
    "l3_gw": lambda a: a["L3_ffn_gate_w"].T,
    "l3_w13": lambda a: a["L3_ffn_w13"],
    "l3_w2": lambda a: a["L3_ffn_w2"],
    "l3_sg": lambda a: a["L3_ffn_sw_gate"],
    "l3_su": lambda a: a["L3_ffn_sw_up"],
    "l3_sd": lambda a: a["L3_ffn_sw_down"],
}


def by_groups(w, groups):
    return w.reshape(w.shape[0], groups, -1).transpose(1, 0, 2)


def by_rows(w, blocks):
    e, f, n = w.shape
    return w.reshape(e, blocks, f // blocks, n).transpose(0, 2, 1, 3).reshape(e, f // blocks, blocks * n)


def two_parts(first, second, blocks):
    e, f, k = first.shape
    both = np.stack([w.reshape(e, blocks, f // blocks, k) for w in (first, second)], 2)
    return both.transpose(0, 4, 1, 2, 3).reshape(e, k, 2 * f)


def spread_heads(w):
    k = w.shape[0]
    out = np.repeat(w.reshape(k, 4, 4, 1, 8), 4, 3)
    return out.transpose(1, 0, 2, 3, 4).reshape(4, k, P)


def low_blocks():
    block = np.arange(P) // 8 % 4
    return np.stack([-(block % 2), -(block // 2)], 1).astype(np.float32)


@contextmanager
def moe_tensors(core, layer, E):
    nc = core.nc
    with nc.sbuf_tensor(f"g{layer}", [P, E, NT], F32) as core.g, \
         nc.sbuf_tensor(f"g_t{layer}", [E, T], F32) as core.g_t, \
         nc.sbuf_tensor(f"b2_{layer}", [E, P], F32) as core.b2:
        yield


def build(nc, d, out, stages=None):
    on = lambda s: stages is None or s in stages
    with ExitStack() as ctx:
        core = Core(nc, ctx)
        setup(core, d["x"], d["ct"], d["wmod"])
        if on("a0"):
            layer_norm(core, 0, 0)
            with nc.sbuf_tensor("v0", [P, NT, v_width(64)], F32) as core.v:
                values(core, "l0", core.h, d["l0_wv"], None, HEADS * 64)
                attention(core, 0, 8, 64, False, core.h, d["l0_wq"], d["l0_wk"], d["l0_wo"], d["l0_bo"],
                          q_scale=64 ** -0.5)
        if on("f0"):
            layer_norm(core, 0, 1)
            with moe_tensors(core, 0, 8):
                route(core, 0, 8, d["l0_gw"], d["l0_gb"], "softmax")
                gate_rows(core, 0, 8, d["l0_b2"])
                experts(core, 0, 8, P, 4, ACT.Silu, d["l0_w1"], d["l0_w2"], b1=d["l0_b1"])
        if on("a1"):
            layer_norm(core, 1, 0)
            with nc.sbuf_tensor("v1", [P, NT, v_width(8)], F32) as core.v, nc.sbuf_tensor("lat", [P, T], F32) as lat:
                latents(core, d["l1_wkd"], d["l1_bkd"], lat)
                values(core, "l1", lat, d["l1_wv"], d["l1_bv"], P)
                attention(core, 1, 4, 8, True, lat, d["l1_wq"], d["l1_wku"], d["l1_wo"], d["l1_bo"],
                          q_bias=d["l1_bq"], k_bias=d["l1_bku"], k_scale=8 ** -0.5, minus=d["l1_minus"])
        if on("f1"):
            layer_norm(core, 1, 1)
            with moe_tensors(core, 1, 8):
                route(core, 1, 8, d["l1_gw"], None, "jitter")
                gate_rows(core, 1, 8, None)
                experts(core, 1, 8, 112, 4, ACT.Silu, d["l1_w1"], d["l1_w2"], biased=False)
        if on("a2"):
            layer_norm(core, 2, 0)
            with nc.sbuf_tensor("xn2", [P, T], F32) as xn, nc.sbuf_tensor("xnt2", [P, NT, P], F32) as xn_tok:
                rms_norm(core, "l2", 2, 0, 1e-8, d["l2_nw"], xn_tok, xn)
                gated_scan(core, 2, xn, d["l2_win"], d["l2_buz"], d["l2_bg"], d["l2_wx"], d["l2_wdt"], d["l2_bxdt"], d["l2_wout"],
                           d["l2_bout"])
        if on("f2"):
            layer_norm(core, 2, 1)
            with moe_tensors(core, 2, 17):
                route(core, 2, 15, d["l2_gw"], None, "renormed")
                gate_rows(core, 2, 17, d["l2_b2"])
                experts(core, 2, 17, P, 1, ACT.Gelu, d["l2_w1"], d["l2_w2"], b1=d["l2_b1"], mult=d["l2_mult"])
        if on("a3"):
            layer_norm(core, 3, 0)
            with nc.sbuf_tensor("v3", [P, NT, v_width(64)], F32) as core.v:
                values(core, "l3", core.h, d["l3_wv"], None, HEADS * 64)
                attention(core, 3, 8, 64, True, core.h, d["l3_wq"], d["l3_wk"], d["l3_wo"], d["l3_bo"],
                          q_scale=64 ** -0.5)
        if on("f3"):
            layer_norm(core, 3, 1)
            with ExitStack() as half:
                sb = lambda name, shape, dt=F32: half.enter_context(nc.sbuf_tensor(name, shape, dt))
                xn, xn_tok = sb("xn3", [P, T]), sb("xnt3", [P, NT, P])
                hot, ws, idx_f = sb("hot3", [P, 2, NT, L3_E]), sb("ws3", [P, 2, NT]), sb("idx3", [P, NT, 8])
                slot = sb("slot3", [P, 2, NT], U32)
                rms_norm(core, "l3", 3, 1, 1e-6, d["l3_rw"], xn_tok, xn)
                route(core, 3, L3_E, d["l3_gw"], None, "softmax", source=xn, chosen=(hot, ws, idx_f))
                dispatch(core, hot, ws, idx_f, slot, xn_tok)
                slot_experts(core, d["l3_rw"], d["l3_w13"], d["l3_w2"])
                combine(core, xn, ws, slot, d["l3_sg"], d["l3_su"], d["l3_sd"])
        store(core, out)


def store(core, out):
    nc = core.nc
    stored = signal(core, "stored")
    with nc.Block() as block:

        @block.sync
        def _(sp):
            sp.dma_start(out.rearrange("b (q p) d -> p (b q) d", p=P), core.x[:]).then_inc(stored.sem, 16)
            sp.wait_ge(*stored(16))


def kernel(**inputs):
    import concourse.bacc as bacc
    from concourse.bass_utils import run_bass_kernel_spmd

    nc = bacc.Bacc("TRN2", target_bir_lowering=False, num_devices=1)
    arrays, d = {}, {}
    for name, layout in INS.items():
        arrays[name] = np.ascontiguousarray(layout(inputs))
        d[name] = nc.dram_tensor(name, arrays[name].shape, F32, kind="ExternalInput").ap()
    out = nc.dram_tensor("out", (B, S, P), F32, kind="ExternalOutput").ap()
    build(nc, d, out)
    r = run_bass_kernel_spmd(nc, [arrays], core_ids=[0])
    return r.results[0]["out"]
```

```python
from contextlib import ExitStack, contextmanager

import concourse.bass as bass
from concourse import mybir
import numpy as np

ALU = mybir.AluOpType
ACT = mybir.ActivationFunctionType
F32 = mybir.dt.float32
F32R = mybir.dt.float32r
BF16 = mybir.dt.bfloat16
I32 = mybir.dt.int32
U32 = mybir.dt.uint32
AX_X = mybir.AxisListType.X

P = 128
B = 4
S = 512
Q = S // P
NT = B * Q
T = B * S
LAYERS = 4
HEADS = 16
L3_E, CAP = 64, 128
L3_SLOTS = L3_E * CAP
ZERO_FILLS = L3_SLOTS * P // (P * 1024)
PV_COLS = 96
NEG = -1.0e30


class Signal:

    def __init__(self, sem):
        self.sem = sem
        self.base = 0

    def __call__(self, n):
        return self.sem, self.base + n


class Core:

    def __init__(self, nc, ctx):
        self.nc = nc
        self.ctx = ctx
        self.signals = {}


def signal(core, name):
    if name not in core.signals:
        core.signals[name] = Signal(core.ctx.enter_context(core.nc.semaphore(name)))
    return core.signals[name]


def stage_ends(core, **totals):
    for name, total in totals.items():
        core.signals[name].base += total


def three_passes(pe, out, w_hi, w_lo, a_hi, a_lo, start=True):
    pe.matmul(out, w_hi, a_hi, start=start, stop=False, skip_group_check=True)
    pe.matmul(out, w_hi, a_lo, start=False, stop=False, skip_group_check=True)
    return pe.matmul(out, w_lo, a_hi, start=False, stop=True, skip_group_check=True)


def setup(core, x, ct, wmod):
    nc = core.nc
    sb = lambda name, shape, dt=F32: core.ctx.enter_context(nc.sbuf_tensor(name, shape, dt))
    core.x = sb("x_tok", [P, NT, P])
    core.h = sb("h_feat", [P, T])
    core.ident = sb("ident", [P, P])
    core.ident_bf = sb("ident_bf", [P, P], BF16)
    core.mask = sb("causal_mask", [P, P], BF16)
    core.gate_f = sb("gate_feat", [P, 2, LAYERS, B])
    core.own_tile = sb("own_tile", [P, S])
    core.ones = sb("ones", [P, P])
    core.ones_r = sb("ones_r", [P, P], F32R)
    core.shift = sb("shift", [P, LAYERS, 2, B])
    core.scale = sb("scale", [P, LAYERS, 2, B])
    core.gate = sb("gate", [P, LAYERS, 2, B, P])

    core.g_rows = nc.dram_tensor("g_rows", [17, T], F32).ap()
    core.zeros = sb("zeros", [P, 1024])
    core.slots_in = nc.dram_tensor("slots_in", [L3_SLOTS, P], F32).ap()
    core.slots_out = nc.dram_tensor("slots_out", [L3_SLOTS, P], F32).ap()
    zeroed = signal(core, "slots_zeroed")
    x_loaded = signal(core, "x_loaded")
    CONSTS = 11
    (loaded, consts, silu_c, mod_psum, mod_free, gate_step, gate_psum, by_act, by_dve) = (signal(core, n) for n in (
        "loaded", "consts", "silu_c", "mod_psum", "mod_free", "gate_step", "gate_psum", "gate_by_act", "gate_by_dve"))
    rows = [(l, k) for l in range(LAYERS) for k in range(2)]
    with ExitStack() as ctx:
        tmp = lambda name, shape, dt=F32: ctx.enter_context(nc.sbuf_tensor(name, shape, dt))
        w_sb = tmp("wmod_sb", [P, LAYERS, 6, P])
        c_sb = tmp("c_sb", [P, LAYERS * B])
        sc = tmp("silu_c_sb", [P, LAYERS * B])
        sign = tmp("gate_sign", [P, 2, LAYERS, B])
        mag = tmp("gate_mag", [P, 2, LAYERS, B])
        mod_ps = ctx.enter_context(nc.psum_tensor("mod_ps", [P, 6, LAYERS, B], F32))
        gate_ps = ctx.enter_context(nc.psum_tensor("gate_ps", [P, 4, B, P], F32))
        with nc.Block() as block:

            @block.sync
            def _(sp):
                sp.dma_start(c_sb[:], ct).then_inc(loaded.sem, 16)
                sp.dma_start(w_sb[:], wmod).then_inc(loaded.sem, 16)
                sp.dma_start(core.x[:], x.rearrange("b (q p) d -> p (b q) d", p=P)).then_inc(x_loaded.sem, 16)
                sp.wait_ge(*consts(7))
                for k in range(ZERO_FILLS):
                    part = L3_SLOTS // ZERO_FILLS
                    sp.dma_start(core.slots_in[k * part:(k + 1) * part, :].rearrange("(p r) d -> p (r d)", p=P),
                                 core.zeros[:]).then_inc(zeroed.sem, 16)
                sp.wait_ge(*x_loaded(16))

            @block.gpsimd
            def _(pool):
                pool.memset(core.zeros[:], 0.0).then_inc(consts.sem, 1)
                for m in (core.ident, core.ident_bf, core.mask):
                    pool.memset(m[:], 0.0).then_inc(consts.sem, 1)
                for m in (core.ones[:], core.ones_r[:].bitcast(F32)):
                    pool.memset(m, 1.0).then_inc(consts.sem, 1)
                pool.memset(core.own_tile[:], 0.0).then_inc(consts.sem, 1)
                pool.wait_ge(*consts(7))
                pool.affine_select(out=core.own_tile[:], in_=core.own_tile[:], compare_op=ALU.not_equal, fill=1.0,
                                   base=0, pattern=[[-1, Q], [0, P]], channel_multiplier=1).then_inc(consts.sem, 1)
                for m in (core.ident, core.ident_bf):
                    pool.affine_select(out=m[:], in_=m[:], compare_op=ALU.not_equal, fill=1.0, base=0,
                                       pattern=[[-1, P]], channel_multiplier=1).then_inc(consts.sem, 1)
                pool.affine_select(out=core.mask[:], in_=core.mask[:], compare_op=ALU.is_ge, fill=NEG, base=0,
                                   pattern=[[-1, P]], channel_multiplier=1).then_inc(consts.sem, 1)

            @block.scalar
            def _(act):
                act.wait_ge(*loaded(32))
                act.activation(sc[:], c_sb[:], ACT.Silu).then_inc(silu_c.sem, 1)
                for n, (l, k) in enumerate(rows):
                    if n % 2:
                        act.wait_ge(*gate_psum(n + 1))
                        act.copy(core.gate[:, l, k], gate_ps[:, n % 4]).then_inc(by_act.sem, 1)

            @block.tensor
            def _(pe):
                pe.wait_ge(*silu_c(1))
                pe.wait_ge(*loaded(32))
                for j, part in enumerate((2, 5, 0, 1, 3, 4)):
                    for l in range(LAYERS):
                        mm = pe.matmul(mod_ps[:, j, l, :], w_sb[:, l, part, :], sc[:, l * B:(l + 1) * B],
                                       start=True, stop=True)
                mm.then_inc(mod_psum.sem, 1)
                pe.wait_ge(*gate_step(4))
                pe.wait_ge(*consts(CONSTS))
                for n, (l, k) in enumerate(rows):
                    if n >= 4:
                        pe.wait_ge(*(by_act if n % 2 else by_dve)((n - 4) // 2 + 1))
                    for b in range(B):
                        mm = pe.matmul(gate_ps[:, n % 4, b, :], core.gate_f[:, k, l, b:b + 1].broadcast_to([P, P]),
                                       core.ident[:], start=True, stop=True)
                    mm.then_inc(gate_psum.sem, 1)

            @block.vector
            def _(dve):
                dve.wait_ge(*mod_psum(1))
                g = mod_ps[:, 0:2]
                dve.tensor_scalar(sign[:], g, 0.0, 2.0, ALU.is_ge, ALU.mult).then_inc(gate_step.sem, 1)
                dve.wait_ge(*gate_step(1))
                dve.tensor_scalar(sign[:], sign[:], -1.0, None, ALU.add).then_inc(gate_step.sem, 1)
                dve.wait_ge(*gate_step(2))
                dve.tensor_tensor(mag[:], g, sign[:], ALU.mult).then_inc(gate_step.sem, 1)
                dve.wait_ge(*gate_step(3))
                flat = lambda a: a[:].rearrange("p k l b -> p (k l b)")
                dve.scalar_tensor_tensor(flat(core.gate_f), flat(mag), 0.25, flat(sign), ALU.max, ALU.mult)\
                   .then_inc(gate_step.sem, 1)
                for half in range(2):
                    dve.tensor_copy(core.shift[:, :, half, :], mod_ps[:, 2 + 2 * half]).then_inc(mod_free.sem, 1)
                    dve.tensor_scalar(core.scale[:, :, half, :], mod_ps[:, 3 + 2 * half], 1.0, None,
                                      ALU.add).then_inc(mod_free.sem, 1)
                for n, (l, k) in enumerate(rows):
                    if n % 2 == 0:
                        dve.wait_ge(*gate_psum(n + 1))
                        dve.tensor_copy(core.gate[:, l, k], gate_ps[:, n % 4]).then_inc(by_dve.sem, 1)
    stage_ends(core, loaded=32, x_loaded=16, consts=CONSTS, silu_c=1, mod_psum=1, mod_free=4, gate_step=4,
               gate_psum=2 * LAYERS, gate_by_act=LAYERS, gate_by_dve=LAYERS)


def layer_norm(core, layer, half):
    nc = core.nc
    stats, aggr, var, std, rstd, shift, xn_dve, xn_act, tr, done = (signal(core, n) for n in (
        "ln_stats", "ln_aggr", "ln_var", "ln_std", "ln_rstd", "ln_shift", "ln_normed_dve", "ln_normed_act",
        "ln_transposed", "ln_h"))
    with ExitStack() as ctx:
        tmp = lambda name, shape, dt=F32: ctx.enter_context(nc.sbuf_tensor(f"{name}_{layer}{half}", shape, dt))
        st = tmp("ln_st", [P, NT, 6])
        mv = tmp("ln_mv", [P, NT, 2])
        ve = tmp("ln_ve", [P, NT])
        sd = tmp("ln_sd", [P, NT])
        rs = tmp("ln_rs", [P, NT])
        nb = tmp("ln_nb", [P, NT])
        xm = tmp("ln_xn", [P, NT, P])
        ps = ctx.enter_context(nc.psum_tensor(f"ln_ps_{layer}{half}", [P, 2, S], F32))
        tiles = lambda b: range(Q * b, Q * b + Q)
        all_tiles = lambda b: slice(Q * b, Q * b + Q)
        by_dve, by_act = lambda b: tiles(b)[:Q // 2], lambda b: tiles(b)[Q // 2:]
        with nc.Block() as block:

            @block.vector
            def _(dve):
                def statistics(b):
                    for t in tiles(b):
                        last = dve.bn_stats(st[:, t, :], core.x[:, t, :])
                    last.then_inc(stats.sem, 1)

                def variance(b):
                    dve.wait_ge(*stats(b + 1))
                    for t in tiles(b):
                        last = dve.bn_aggr(mv[:, t, :], st[:, t, :])
                    last.then_inc(aggr.sem, 1)
                    dve.wait_ge(*aggr(b + 1))
                    dve.tensor_scalar(ve[:, all_tiles(b)], mv[:, all_tiles(b), 1], 1e-5, None, ALU.add)\
                       .then_inc(var.sem, 1)

                def normalise(b):
                    dve.wait_ge(*std(b + 1))
                    dve.reciprocal(rs[:, all_tiles(b)], sd[:, all_tiles(b)]).then_inc(rstd.sem, 1)
                    dve.wait_ge(*rstd(b + 1))
                    dve.scalar_tensor_tensor(nb[:, all_tiles(b)], mv[:, all_tiles(b), 0], -1.0, rs[:, all_tiles(b)],
                                             ALU.mult, ALU.mult).then_inc(shift.sem, 1)
                    for t in by_dve(b):
                        last = dve.tensor_scalar(xm[:, t, :], core.x[:, t, :], mv[:, t, 0:1], rs[:, t:t + 1],
                                                 ALU.subtract, ALU.mult)
                    last.then_inc(xn_dve.sem, 1)

                statistics(0)
                for b in range(B):
                    if b + 1 < B:
                        statistics(b + 1)
                    variance(b)
                    if b:
                        normalise(b - 1)
                normalise(B - 1)

            @block.scalar
            def _(act):
                def root(b):
                    act.wait_ge(*var(b + 1))
                    act.activation(sd[:, all_tiles(b)], ve[:, all_tiles(b)], ACT.Sqrt).then_inc(std.sem, 1)

                def normalise(b):
                    act.wait_ge(*shift(b + 1))
                    for t in by_act(b):
                        last = act.activation(xm[:, t, :], core.x[:, t, :], ACT.Identity, bias=nb[:, t:t + 1],
                                              scale=rs[:, t:t + 1])
                    last.then_inc(xn_act.sem, 1)

                def modulate(b):
                    act.wait_ge(*tr(b + 1))
                    act.activation(core.h[:, b * S:(b + 1) * S], ps[:, b % 2, :], ACT.Identity,
                                   bias=core.shift[:, layer, half, b:b + 1],
                                   scale=core.scale[:, layer, half, b:b + 1]).then_inc(done.sem, 1)

                root(0)
                for b in range(B):
                    if b + 1 < B:
                        root(b + 1)
                    normalise(b)
                    if b:
                        modulate(b - 1)
                modulate(B - 1)

            @block.tensor
            def _(pe):
                for b in range(B):
                    pe.wait_ge(*xn_dve(b + 1))
                    pe.wait_ge(*xn_act(b + 1))
                    if b >= 2:
                        pe.wait_ge(*done(b - 1))
                    for q in range(Q):
                        mm = pe.transpose(ps[:, b % 2, q * P:(q + 1) * P], xm[:, Q * b + q, :], core.ident[:])
                    mm.then_inc(tr.sem, 1)
    stage_ends(core, ln_stats=B, ln_aggr=B, ln_var=B, ln_std=B, ln_rstd=B, ln_shift=B, ln_normed_dve=B,
               ln_normed_act=B, ln_transposed=B, ln_h=B)


def v_width(dv):
    return HEADS * (dv + 1) + PV_COLS - (dv + 1)


def values(core, name, source, w, bias, width):
    nc = core.nc
    loaded, vps, va, vd, v_ones = (signal(core, n) for n in ("loaded", "v_psum", "v_by_act", "v_by_dve", "v_ones"))
    w_cleared = signal(core, "w_cleared")
    v = core.v
    dv = width // HEADS
    K = w.shape[0]
    per = max(1, 512 // width)
    parts = max(1, width // 512)
    jobs = [(t, c) for t in range(0, NT, per) for c in range(parts)]
    with ExitStack() as ctx:
        w_sb = ctx.enter_context(nc.sbuf_tensor(f"wv_{name}", [P, width], F32))
        ps = ctx.enter_context(nc.psum_tensor(f"v_ps_{name}", [P, 4, 512], F32))
        cols = min(width, 512)

        heads = cols // dv
        head_columns = lambda tiles, h, n: v[:, tiles, h * (dv + 1):(h + n) * (dv + 1)]\
            .rearrange("p t (h e) -> p t h e", e=dv + 1)

        def out_of(t, c):
            return head_columns(slice(t, t + per), c * heads, heads)[:, :, :, 0:dv]

        with nc.Block() as block:

            @block.gpsimd
            def _(pool):
                if bias is not None:
                    pool.memset(w_sb[:], 0.0).then_inc(w_cleared.sem, 1)
                pool.memset(head_columns(slice(0, NT), 0, HEADS)[:, :, :, dv], 1.0).then_inc(v_ones.sem, 1)
                pool.memset(v[:, :, HEADS * (dv + 1):], 0.0).then_inc(v_ones.sem, 1)

            @block.sync
            def _(sp):
                if bias is not None:
                    sp.wait_ge(*w_cleared(1))
                sp.dma_start(w_sb[0:K, :], w).then_inc(loaded.sem, 16)
                if bias is not None:
                    sp.dma_start(w_sb[K:K + 1, :], bias).then_inc(loaded.sem, 16)

            @block.tensor
            def _(pe):
                pe.wait_ge(*loaded(16 if bias is None else 32))
                for n, (t, c) in enumerate(jobs):
                    if n >= 4:
                        m = n - 4
                        pe.wait_ge(*(va if m % 2 else vd)(m // 2 + 1))
                    for k in range(per):
                        mm = pe.matmul(ps[:, n % 4, k * cols:(k + 1) * cols], source[:, (t + k) * P:(t + k + 1) * P],
                                       w_sb[:, c * cols:(c + 1) * cols], start=True, stop=True)
                    mm.then_inc(vps.sem, 1)

            @block.scalar
            def _(act):
                for n, (t, c) in enumerate(jobs):
                    if n % 2:
                        act.wait_ge(*vps(n + 1))
                        act.activation(out_of(t, c), ps[:, n % 4, :].rearrange("p (k h c) -> p k h c", k=per, c=dv), ACT.Copy)\
                           .then_inc(va.sem, 1)

            @block.vector
            def _(dve):
                for n, (t, c) in enumerate(jobs):
                    if n % 2 == 0:
                        dve.wait_ge(*vps(n + 1))
                        dve.tensor_copy(out_of(t, c), ps[:, n % 4, :].rearrange("p (k h c) -> p k h c", k=per, c=dv))\
                           .then_inc(vd.sem, 1)
    stage_ends(core, loaded=16 if bias is None else 32, v_psum=len(jobs), v_by_act=len(jobs) // 2,
             v_by_dve=len(jobs) // 2, v_ones=2,
             w_cleared=0 if bias is None else 1)


def values_by_parts(core, name, w, width):
    nc = core.nc
    loaded, vps, va, vd, v_ones, w_high, w_split, h_high, h_split = (signal(core, n) for n in (
        "loaded", "v_psum", "v_by_act", "v_by_dve", "v_ones", "w1_high", "w1_split", "h_high", "h_split"))
    v, dv, C = core.v, width // HEADS, 512
    jobs = [(t, c) for t in range(NT) for c in range(width // C)]
    with ExitStack() as ctx:
        tmp = lambda n, dt=F32: ctx.enter_context(nc.sbuf_tensor(f"{n}_{name}", [P, width], dt))
        w_sb, w_hi, w_lo = tmp("wv"), tmp("wv_high", F32R), tmp("wv_low", F32R)
        ps = ctx.enter_context(nc.psum_tensor(f"v_ps_{name}", [P, 4, C], F32))
        heads = C // dv
        head_columns = lambda t, h, n: v[:, t, h * (dv + 1):(h + n) * (dv + 1)]\
            .rearrange("p (h e) -> p h e", e=dv + 1)
        out_of = lambda t, c: head_columns(t, c * heads, heads)[:, :, 0:dv]
        bank = lambda n: ps[:, n % 4, :].rearrange("p (h c) -> p h c", c=dv)
        columns = lambda c: slice(c * C, (c + 1) * C)
        tokens = lambda b: slice(b * S, (b + 1) * S)
        with nc.Block() as block:

            @block.gpsimd
            def _(pool):
                ones = v[:, :, 0:HEADS * (dv + 1)].rearrange("p t (h e) -> p t h e", e=dv + 1)[:, :, :, dv]
                pool.memset(ones, 1.0).then_inc(v_ones.sem, 1)
                pool.memset(v[:, :, HEADS * (dv + 1):], 0.0).then_inc(v_ones.sem, 1)

            @block.sync
            def _(sp):
                sp.dma_start(w_sb[:], w).then_inc(loaded.sem, 16)

            @block.tensor
            def _(pe):
                for n, (t, c) in enumerate(jobs):
                    if t == 0:
                        pe.wait_ge(*w_split(c + 1))
                    if t % Q == 0 and c == 0:
                        pe.wait_ge(*h_split(t // Q + 1))
                    if n >= 4:
                        pe.wait_ge(*(va if n % 2 else vd)((n - 4) // 2 + 1))
                    at = slice(t * P, (t + 1) * P)
                    three_passes(pe, ps[:, n % 4, :], core.h_hi[:, at], core.h_lo[:, at], w_hi[:, columns(c)],
                                 w_lo[:, columns(c)]).then_inc(vps.sem, 1)

            @block.scalar
            def _(act):
                def high(b):
                    act.copy(core.h_hi[:, tokens(b)], core.h[:, tokens(b)]).then_inc(h_high.sem, 1)

                high(0)
                act.wait_ge(*loaded(16))
                for c in range(width // C):
                    act.copy(w_hi[:, columns(c)], w_sb[:, columns(c)]).then_inc(w_high.sem, 1)
                for n, (t, c) in enumerate(jobs):
                    if t % Q == 0 and c == 0 and t // Q + 1 < B:
                        high(t // Q + 1)
                    if n % 2:
                        act.wait_ge(*vps(n + 1))
                        act.activation(out_of(t, c), bank(n), ACT.Copy).then_inc(va.sem, 1)

            @block.vector
            def _(dve):
                def low(b):
                    dve.wait_ge(*h_high(b + 1))
                    dve.tensor_tensor(core.h_lo[:, tokens(b)], core.h[:, tokens(b)],
                                      core.h_hi[:, tokens(b)].bitcast(F32), ALU.subtract).then_inc(h_split.sem, 1)

                low(0)
                for c in range(width // C):
                    dve.wait_ge(*w_high(c + 1))
                    dve.tensor_tensor(w_lo[:, columns(c)], w_sb[:, columns(c)], w_hi[:, columns(c)].bitcast(F32),
                                      ALU.subtract).then_inc(w_split.sem, 1)
                for n, (t, c) in enumerate(jobs):
                    if t % Q == 0 and c == 0 and t // Q + 1 < B:
                        low(t // Q + 1)
                    if n % 2 == 0:
                        dve.wait_ge(*vps(n + 1))
                        dve.tensor_copy(out_of(t, c), bank(n)).then_inc(vd.sem, 1)
    stage_ends(core, loaded=16, v_psum=len(jobs), v_by_act=len(jobs) // 2, v_by_dve=len(jobs) // 2, v_ones=2,
               w1_high=width // C, w1_split=width // C, h_high=B, h_split=B)


def attention(core, layer, groups, dv, causal, k_source, wq, wk, wo, bo, q_bias=None, k_bias=None, minus=None,
              q_scale=1.0, k_scale=1.0):
    nc = core.nc
    hpg = HEADS // groups
    Q_STEP = 4
    hv = hpg * dv
    split8 = minus is not None
    KK = wk.shape[1]
    NG = B * groups
    (loaded, out_scaled, x_biased, q_full, k_full, q_plain, k_plain, q_high, k_high, q_made, k_made, s_full,
     neg_max, diag_made, probs_full, probs, o_full, sums_inverse, ctx_ready, ctx_t_full, ctx_turned, y_full, x_added,
     q_cleared) = (signal(core, n) for n in (
         "loaded", "out_scaled", "x_biased", "q_full", "k_full", "q_plain", "k_plain", "q_high", "k_high", "q_made",
         "k_made", "s_full", "neg_max", "diag_made", "probs_full", "probs", "o_full", "sums_inverse", "ctx_ready",
         "ctx_t_full", "ctx_turned", "y_full", "x_added", "q_cleared"))
    wslot = [signal(core, "weights_slot0"), signal(core, "weights_slot1")]
    loads = 16 * (5 if split8 else 2)
    rows_cleared = signal(core, "rows_cleared")
    masked, b_cleared, max_turned, max_placed = (signal(core, n) for n in (
        "masked", "b_cleared", "max_turned", "max_placed"))
    w_high, w_split = signal(core, "w_high"), signal(core, "w_split")
    clears = (KK < P) + 2 * (hv < P)

    with ExitStack() as ctx:
        tmp = lambda name, shape, dt=F32: ctx.enter_context(nc.sbuf_tensor(f"{name}_{layer}", shape, dt))
        psum = lambda name, shape: ctx.enter_context(nc.psum_tensor(f"{name}_{layer}", shape, F32))
        wq_s = tmp("wq_slot", [P, 2, P])
        wk_s = tmp("wk_slot", [P, 2, P])
        if not split8:
            w_hi, w_lo = tmp("w_high", [P, 2, 2, P], F32R), tmp("w_low", [P, 2, 2, P], F32R)
        if split8:
            qb_s, kb_s = tmp("qb_slot", [P, groups]), tmp("kb_slot", [P, groups])
            minus_s = tmp("minus_low", [P, 2])
            q_f, k_f = tmp("q_plain", [P, S]), tmp("k_plain", [P, S])
            q_h, k_h = tmp("q_high", [P, S], F32R), tmp("k_high", [P, S], F32R)
        wo_sb = tmp("wo_sb", [hv, groups, P])
        wog = tmp("wo_gated", [P, B, groups, P])
        bo_sb = tmp("bo_sb", [P, P])
        bog = tmp("bo_gated", [P, B, P])
        q_st = tmp("q_parts", [P, 2, hpg, S], F32R)
        k_heads = 1 if split8 else hpg
        k_a = tmp("k_parts_a", [P, 2, k_heads, S], F32R)
        if split8:
            diag = tmp("max_diag", [P, 2, Q, P], F32R)
        else:
            k_b = tmp("k_parts_b", [P, 2, hpg, S], F32R)
            q_b = tmp("q_parts_b", [P, 2, hpg, S], F32R)
        pt = tmp("probs_t", [P, 2, Q, S])
        nm = tmp("neg_max", [P, 2, Q])
        inv = tmp("inv_sums", [P, 2, Q])
        tick = tmp("tick", [P, hpg * Q])
        ctx_sb = tmp("ctx_sb", [P, 2, Q, hpg, dv])
        ctx_t = tmp("ctx_t", [P, S])
        s_ps = psum("s_ps", [P, 2, S])
        p_ps = psum("p_ps", [P, 2, S])
        o_ps = psum("o_ps", [P, 2, Q, P])
        turn_ps = psum("turn_ps", [P, S])
        add_ps = psum("add_ps", [P, S])

        batch = lambda g: g // groups
        in_batch = lambda g: g % groups
        tile_of = lambda i: Q - 1 - i if split8 else i
        keys = lambda i: (i + 1) * P if causal else S
        seen_by = lambda i: slice(i * P if causal else 0, S)
        half = lambda h: slice(h % 2 * 64, h % 2 * 64 + 64)
        other = lambda h: half(h + 1)
        probs_in = lambda i: (i,) if split8 else ((), (0,), (1,), (2, 3))[i]
        max_rows = lambda h: slice(other(h).start, other(h).start + Q)
        turned_max = lambda h: o_ps[0:Q, h % 2, :, PV_COLS:]
        among_first = lambda g, h, n: isinstance(g, int) and g * hpg + h < n

        with nc.Block() as block:

            @block.sync
            def _(sp):
                sp.dma_start(wo_sb[:], wo.rearrange("g f n -> f g n")).then_inc(loaded.sem, 16)
                sp.dma_start(bo_sb[:], bo.broadcast_to([P, P])).then_inc(loaded.sem, 16)
                if split8:
                    sp.dma_start(qb_s[:], q_bias).then_inc(loaded.sem, 16)
                    sp.dma_start(kb_s[:], k_bias).then_inc(loaded.sem, 16)
                    sp.dma_start(minus_s[:], minus).then_inc(loaded.sem, 16)

                def load(g, s):
                    sp.dma_start(wq_s[:, s, :], wq[in_batch(g), :, :]).then_inc(wslot[s].sem, 16)
                    sp.dma_start(wk_s[0:KK, s, :], wk[in_batch(g), :, :]).then_inc(wslot[s].sem, 16)

                if KK < P:
                    sp.wait_ge(*rows_cleared(1))
                load(0, 0)
                load(1, 1)
                with sp.Fori(1, NG // 2) as i:
                    for s in range(2):
                        sp.wait_ge(*(k_full if split8 else w_split)(2 * (i - 1) + s + 1))
                        load(2 * i + s, s)

            @block.gpsimd
            def _(pool):
                def split(g, s):
                    pool.wait_ge(*wslot[s](32 * (g // 2) + 32))
                    if not (isinstance(g, int) and g < 2):
                        pool.wait_ge(*k_full(g - 2 + 1))
                    for m, w in enumerate((wq_s, wk_s)):
                        last = pool.tensor_tensor(w_hi[:, s, m, :], w[:, s, :], core.zeros[:, 0:P], ALU.add)
                    last.then_inc(w_high.sem, 1)
                    pool.wait_ge(*w_high(g + 1))
                    for m, w in enumerate((wq_s, wk_s)):
                        last = pool.tensor_tensor(w_lo[:, s, m, :], w[:, s, :], w_hi[:, s, m, :].bitcast(F32),
                                                  ALU.subtract)
                    last.then_inc(w_split.sem, 1)

                if not split8:
                    split(0, 0)
                    split(1, 1)
                    for m in (q_b, k_b):
                        pool.memset(m[:].bitcast(F32), 0.0).then_inc(b_cleared.sem, 1)
                    for h in range(hpg):
                        pool.wait_ge(*b_cleared(2 + h))
                        pool.memset(k_b[max_rows(h), :, h, :].bitcast(F32), 1.0).then_inc(b_cleared.sem, 1)
                    pool.wait_ge(*b_cleared(2 + hpg))
                if KK < P:
                    pool.memset(wk_s[:], 0.0).then_inc(rows_cleared.sem, 1)
                pool.memset(q_st[:].bitcast(F32), 0.0).then_inc(q_cleared.sem, 1)
                if hv < P:
                    pool.memset(ctx_t[:], 0.0).then_inc(rows_cleared.sem, 1)
                    pool.memset(wog[:], 0.0).then_inc(rows_cleared.sem, 1)
                    pool.wait_ge(*rows_cleared(clears))
                pool.wait_ge(*loaded(loads))
                for b in range(B):
                    pool.tensor_tensor(wog[0:hv, b], wo_sb[:],
                                       core.gate[0:hv, layer, 0, b, :].unsqueeze(1).broadcast_to([hv, groups, P]),
                                       ALU.mult).then_inc(out_scaled.sem, 1)
                for b in range(B):
                    pool.tensor_tensor(bog[:, b], bo_sb[:], core.gate[:, layer, 0, b, :], ALU.mult)\
                        .then_inc(out_scaled.sem, 1)
                pool.wait_ge(*out_scaled(2 * B))
                for b in range(B):
                    xb = core.x[:, Q * b:Q * b + Q, :]
                    pool.tensor_tensor(xb, xb, bog[:, b, :].unsqueeze(1).broadcast_to([P, Q, P]), ALU.add)\
                        .then_inc(x_biased.sem, 1)
                if causal or not split8:
                    def select(g, h, i):
                        n = (g * hpg + h) * Q + i
                        pool.wait_ge(*probs(n + 1))
                        own = pt[:, h % 2, i, i * P:(i + 1) * P]
                        pool.tensor_tensor(tick[:, h * Q + i:h * Q + i + 1], core.zeros[:, 0:1], core.zeros[:, 0:1],
                                           ALU.add)
                        pool.affine_select(out=own, in_=own, compare_op=ALU.is_ge, fill=0.0, base=0, pattern=[[1, P]],
                                           channel_multiplier=-1).then_inc(masked.sem, 1)

                    def window(g, s, last=False):
                        if not split8 and not last:
                            split(g + 2, s)
                        if causal:
                            for h in range(hpg):
                                for i in range(Q):
                                    select(g, h, i)

                    with pool.Fori(0, NG // 2 - 1) as i:
                        window(2 * i, 0)
                        window(2 * i + 1, 1)
                    window(NG - 2, 0, last=True)
                    window(NG - 1, 1, last=True)

            @block.tensor
            def _(pe):
                def project(out, m, w, source, g, s):
                    tokens = bass.ds(batch(g) * S, S)
                    if split8:
                        return pe.matmul(out, w[:, s, :], source[:, tokens], start=True, stop=True)
                    return three_passes(pe, out, w_hi[:, s, m, :], w_lo[:, s, m, :], core.h_hi[:, tokens],
                                        core.h_lo[:, tokens])

                def project_q(g, s, turned):
                    pe.wait_ge(*(wslot[s](32 * (g // 2) + 32) if split8 else w_split(g + 1)))
                    if turned is not None:
                        pe.wait_ge(*turned)
                    project(turn_ps[:], 0, wq_s, core.h, g, s).then_inc(q_full.sem, 1)

                def project_k(g, s, added):
                    if added is not None:
                        pe.wait_ge(*added)
                    project(add_ps[:], 1, wk_s, k_source, g, s).then_inc(k_full.sem, 1)

                def scores(g, s, h, i):
                    n = (g * hpg + h) * Q + i
                    if i == 0:
                        pe.wait_ge(*q_made(g * hpg + h + 1))
                        pe.wait_ge(*(k_made(g + 1) if split8 else k_high(g * hpg + h + 1)))
                    if not (among_first(g, h, 1) and i < 2):
                        pe.wait_ge(*neg_max(n - 1))
                    q = tile_of(i)
                    mm = pe.matmul(s_ps[:, i % 2, 0:keys(q)], q_st[:, s, h, q * P:(q + 1) * P],
                                   k_a[:, s, h % k_heads, 0:keys(q)], start=True, stop=True)
                    if causal:
                        mm = pe.matmul(s_ps[:, i % 2, q * P:(q + 1) * P], core.ident_bf[:], core.mask[:],
                                       start=False, stop=True, skip_group_check=True)
                    mm.then_inc(s_full.sem, 1)

                def scores_t(g, s, h, i):
                    j = g * hpg + h
                    if not (among_first(g, h, 1) and i < 2):
                        pe.wait_ge(*probs(j * Q + i - 1))
                    if i == 0 and not split8:
                        pe.wait_ge(*k_made(j + 1))
                    into, seen = p_ps[:, i % 2, seen_by(i)], seen_by(i)
                    pe.matmul(into, k_a[:, s, h % k_heads, i * P:(i + 1) * P], q_st[:, s, h, seen], start=True,
                              stop=False)
                    if i == 0:
                        pe.wait_ge(*(diag_made((j + 1) * Q) if split8 else max_placed(j + 1)))
                    if split8:
                        mm = pe.matmul(into, core.ones_r[:],
                                       diag[:, h % 2, seen.start // P:Q, :].rearrange("p q k -> p (q k)"),
                                       start=False, stop=True)
                    else:
                        mm = pe.matmul(into, k_b[:, s, h, i * P:(i + 1) * P], q_b[:, s, h, seen], start=False,
                                       stop=True)
                    mm.then_inc(probs_full.sem, 1)

                def turn_max(g, h):
                    pe.wait_ge(*neg_max((g * hpg + h + 1) * Q))
                    pe.matmul(turned_max(h), nm[:, h % 2, :], core.ident[:].rearrange("p (a c) -> p a c", a=Q),
                              start=True, stop=True).then_inc(max_turned.sem, 1)

                def times_v(g, h, i):
                    j = g * hpg + h
                    pe.wait_ge(*(masked(j * Q + i + 1) if causal else probs((j + 1) * Q)))
                    if i == 0 and not among_first(g, h, 2):
                        pe.wait_ge(*ctx_ready(j - 1))
                    last = i if causal else Q - 1
                    for c in range(last + 1):
                        mm = pe.matmul(o_ps[:, h % 2, i, 0:PV_COLS], pt[:, h % 2, c, i * P:(i + 1) * P],
                                       core.v[:, batch(g) * Q + c,
                                              bass.ds((in_batch(g) * hpg + h) * (dv + 1), PV_COLS)],
                                       start=c == 0, stop=c == last)
                    if i == Q - 1:
                        mm.then_inc(o_full.sem, 1)

                def turn_ctx(g, s, left):
                    pe.wait_ge(*left)
                    pe.wait_ge(*ctx_ready((g + 1) * hpg))
                    for q in range(Q):
                        mm = pe.transpose(turn_ps[0:hv, q * P:(q + 1) * P],
                                          ctx_sb[:, s, q].rearrange("p h e -> p (h e)"), core.ident[:])
                    mm.then_inc(ctx_t_full.sem, 1)

                def project_out(g, left):
                    pe.wait_ge(*left)
                    pe.wait_ge(*ctx_turned(g + 1))
                    for q in range(Q):
                        mm = pe.matmul(add_ps[:, q * P:(q + 1) * P], ctx_t[:, q * P:(q + 1) * P],
                                       wog[:, batch(g), in_batch(g), :], start=True, stop=True)
                    mm.then_inc(y_full.sem, 1)

                def window(g, s, turned, added, first=False, out=True):
                    for h in range(hpg):
                        for i in range(Q):
                            scores(g, s, h, i)
                            def probs_step(i):
                                if h >= 1:
                                    scores_t(g, s, h - 1, i)
                                elif not first:
                                    scores_t(g - 1, 1 - s, hpg - 1, i)

                            def values_step():
                                if h >= 2:
                                    times_v(g, h - 2, i)
                                elif not first:
                                    times_v(g - 1, hpg + h - 2, i)

                            if i == 0 and not split8:
                                if h >= 1:
                                    turn_max(g, h - 1)
                                elif not first:
                                    turn_max(g - 1, hpg - 1)
                            if i == 1:
                                values_step()
                            for k in probs_in(i):
                                probs_step(k)
                            if i != 1:
                                values_step()
                            step = h * Q + i
                            if step == (1 if split8 else 2) and out:
                                turn_ctx(g - 2, s, q_made((g + 1) * hpg))
                            if step == 3 and out:
                                project_out(g - 2, k_made((g + 1) * k_heads))
                            if step == Q_STEP and turned is not None:
                                project_q(g + 1, 1 - s, turned)
                            if step == Q_STEP + 1 and added is not None:
                                project_k(g + 1, 1 - s, added)

                project_q(0, 0, None)
                project_k(0, 0, None)
                window(0, 0, q_made(hpg), k_made(k_heads), first=True, out=False)
                window(1, 1, q_made(2 * hpg), k_made(2 * k_heads), out=False)
                pe.wait_ge(*out_scaled(2 * B))
                with pe.Fori(1, NG // 2 - 1) as i:
                    for s in range(2):
                        g = 2 * i + s
                        window(g, s, ctx_turned(g - 1), x_added(g - 1))
                window(NG - 2, 0, ctx_turned(NG - 3), x_added(NG - 3))
                window(NG - 1, 1, None, None)
                if not split8:
                    turn_max(NG - 1, hpg - 1)
                for i in range(Q):
                    scores_t(NG - 1, 1, hpg - 1, i)
                    times_v(NG - 1, hpg - 2, i)
                turn_ctx(NG - 2, 0, ctx_turned(NG - 2))
                for i in range(Q):
                    times_v(NG - 1, hpg - 1, i)
                project_out(NG - 2, x_added(NG - 2))
                turn_ctx(NG - 1, 1, ctx_turned(NG - 1))
                project_out(NG - 1, x_added(NG - 1))

            @block.scalar
            def _(act):
                def high_of_q(g, s, h):
                    if h == 0:
                        act.wait_ge(*q_full(g + 1))
                    if split8 and h == 0:
                        act.activation(q_f[:], turn_ps[:], ACT.Identity, scale=q_scale,
                                       bias=qb_s[:, bass.ds(in_batch(g), 1)]).then_inc(q_plain.sem, 1)
                        act.wait_ge(*q_plain(g + 1))
                        act.copy(q_h[:], q_f[:]).then_inc(q_high.sem, 1)
                    elif not split8:
                        act.mul(q_b[half(h), s, h, :], turn_ps[half(h), :], q_scale)
                        act.mul(q_st[half(h), s, h, :], turn_ps[half(h), :], q_scale).then_inc(q_high.sem, 1)

                def highs_of_k(g, s, h):
                    if h == 0:
                        act.wait_ge(*k_full(g + 1))
                    if split8 and h == 0:
                        act.activation(k_f[:], add_ps[:], ACT.Identity, scale=k_scale,
                                       bias=kb_s[:, bass.ds(in_batch(g), 1)]).then_inc(k_plain.sem, 1)
                        act.wait_ge(*k_plain(g + 1))
                        act.copy(k_h[:], k_f[:]).then_inc(k_high.sem, 1)
                    elif not split8:
                        for rows in (half(h), other(h)):
                            last = act.mul(k_a[rows, s, h, :], add_ps[half(h), :], k_scale)
                        last.then_inc(k_high.sem, 1)

                def exps(g, h, i):
                    n = (g * hpg + h) * Q + i
                    act.wait_ge(*probs_full(n + 1))
                    act.activation(pt[:, h % 2, i, seen_by(i)], p_ps[:, i % 2, seen_by(i)], ACT.Exp)\
                        .then_inc(probs.sem, 1)

                def copy_ctx(g):
                    act.wait_ge(*ctx_t_full(g + 1))
                    act.copy(ctx_t[0:hv, :], turn_ps[0:hv, :]).then_inc(ctx_turned.sem, 1)

                def window(g, s, first=False, out=True, last=False):
                    for h in range(hpg):
                        for i in range(Q):
                            step = h * Q + i
                            if step == (2 if split8 else 3) and out:
                                copy_ctx(g - 2)
                            for k in probs_in(i):
                                if h >= 1:
                                    exps(g, h - 1, k)
                                elif not first:
                                    exps(g - 1, hpg - 1, k)
                            if step - Q_STEP in (1, 3) and not last:
                                high_of_q(g + 1, 1 - s, (step - Q_STEP) // 2)
                            if step == Q_STEP + 2 and not last:
                                highs_of_k(g + 1, 1 - s, 0)
                            if not split8 and step == 0 and not among_first(g, 0, 1):
                                highs_of_k(g, s, 1)

                act.wait_ge(*loaded(loads))
                act.wait_ge(*q_cleared(1))
                if not split8:
                    act.wait_ge(*b_cleared(2 + hpg))
                if hv < P:
                    act.wait_ge(*rows_cleared(clears))
                for h in range(2):
                    high_of_q(0, 0, h)
                    highs_of_k(0, 0, h)
                window(0, 0, first=True, out=False)
                window(1, 1, out=False)
                with act.Fori(1, NG // 2 - 1) as i:
                    window(2 * i, 0)
                    window(2 * i + 1, 1)
                window(NG - 2, 0)
                window(NG - 1, 1, last=True)
                for i in range(Q):
                    exps(NG - 1, hpg - 1, i)
                copy_ctx(NG - 2)
                copy_ctx(NG - 1)

            @block.vector
            def _(dve):
                def low_of_q(g, s, h):
                    if split8:
                        dve.wait_ge(*q_high(g + 1))
                        r = slice(h * 32, h * 32 + 32)
                        dve.scalar_tensor_tensor(q_st[r, s, h, :], q_h[r, :].bitcast(F32), minus_s[r, 0:1], q_f[r, :],
                                                 ALU.mult, ALU.add).then_inc(q_made.sem, 1)
                    else:
                        dve.wait_ge(*q_high(g * hpg + h + 1))
                        dve.scalar_tensor_tensor(q_st[other(h), s, h, :], turn_ps[half(h), :], q_scale,
                                                 q_st[half(h), s, h, :].bitcast(F32), ALU.mult, ALU.subtract)\
                           .then_inc(q_made.sem, 1)

                def lows_of_k(g, s, h):
                    if split8:
                        dve.wait_ge(*k_high(g + 1))
                        dve.scalar_tensor_tensor(k_a[:, s, 0, :], k_h[:].bitcast(F32), minus_s[:, 1:2], k_f[:],
                                                 ALU.mult, ALU.add).then_inc(k_made.sem, 1)
                    else:
                        dve.wait_ge(*k_high(hpg * g + h + 1))
                        dve.scalar_tensor_tensor(k_b[half(h), s, h, :], add_ps[half(h), :], k_scale,
                                                 k_a[half(h), s, h, :].bitcast(F32), ALU.mult, ALU.subtract)\
                           .then_inc(k_made.sem, 1)

                def maxima(g, h, i):
                    n = (g * hpg + h) * Q + i
                    dve.wait_ge(*s_full(n + 1))
                    q = tile_of(i)
                    dve.tensor_reduce(nm[:, h % 2, q:q + 1], s_ps[:, i % 2, 0:keys(q)], AX_X, ALU.max, negate=True)\
                        .then_inc(neg_max.sem, 1)
                    if split8:
                        dve.wait_ge(*neg_max(n + 1))
                        dve.tensor_scalar(diag[:, h % 2, q, :], core.ident[:], nm[:, h % 2, q:q + 1], None, ALU.mult)\
                            .then_inc(diag_made.sem, 1)

                def place_max(g, s, h):
                    dve.wait_ge(*max_turned(g * hpg + h + 1))
                    tiles = lambda a: a.rearrange("p (t a c) -> p t a c", t=Q, a=Q)
                    dve.tensor_tensor(tiles(q_b[max_rows(h), s, h, :]),
                                      turned_max(h).unsqueeze(1).broadcast_to([Q, Q, Q, P // Q]),
                                      tiles(core.own_tile[0:Q, :]), ALU.mult).then_inc(max_placed.sem, 1)

                def normalise(g, s, h):
                    j = g * hpg + h
                    dve.wait_ge(*o_full(j + 1))
                    dve.reciprocal(inv[:, h % 2, :], o_ps[:, h % 2, :, dv]).then_inc(sums_inverse.sem, 1)
                    dve.wait_ge(*sums_inverse(j + 1))
                    dve.tensor_tensor(ctx_sb[:, s, :, h, :], o_ps[:, h % 2, :, 0:dv],
                                      inv[:, h % 2, :].unsqueeze(2).broadcast_to([P, Q, dv]), ALU.mult)\
                        .then_inc(ctx_ready.sem, 1)

                def add_to_x(g):
                    dve.wait_ge(*y_full(g + 1))
                    xb = core.x[:, bass.ds(batch(g) * Q, Q), :]
                    dve.tensor_tensor(xb, xb, add_ps[:].rearrange("p (q d) -> p q d", q=Q), ALU.add)\
                       .then_inc(x_added.sem, 1)

                def window(g, s, out=True, last=False):
                    for h in range(hpg):
                        for i in range(Q):
                            if i == 0 and not split8 and not among_first(g, h, 1):
                                if h >= 1:
                                    place_max(g, s, h - 1)
                                else:
                                    place_max(g - 1, 1 - s, hpg - 1)
                            maxima(g, h, i)
                            step = h * Q + i
                            if i == 0:
                                back = (hpg - 1 - (h - 3)) // hpg
                                if not among_first(g, h, 3):
                                    normalise(g - back, (s + back) % 2, h - 3 + back * hpg)
                            if step == 4 and out:
                                add_to_x(g - 2)
                            if step - Q_STEP - 2 in (range(hpg) if split8 else (0,)) and not last:
                                low_of_q(g + 1, 1 - s, step - Q_STEP - 2)
                            if not split8 and step == 0 and not among_first(g, 0, 1):
                                low_of_q(g, s, 1)
                            if split8 and step == Q_STEP + 4 and not last:
                                lows_of_k(g + 1, 1 - s, 0)
                            if not split8 and step in (1, 2) and not among_first(g, 0, 1):
                                lows_of_k(g, s, step - 1)

                dve.wait_ge(*loaded(loads))
                dve.wait_ge(*q_cleared(1))
                for h in range(hpg):
                    low_of_q(0, 0, h)
                for h in range(k_heads):
                    lows_of_k(0, 0, h)
                window(0, 0, out=False)
                window(1, 1, out=False)
                dve.wait_ge(*x_biased(B))
                with dve.Fori(1, NG // 2 - 1) as i:
                    window(2 * i, 0)
                    window(2 * i + 1, 1)
                window(NG - 2, 0)
                window(NG - 1, 1, last=True)
                if not split8:
                    place_max(NG - 1, 1, hpg - 1)
                for j in range(NG * hpg - 3, NG * hpg):
                    normalise(j // hpg, j // hpg % 2, j % hpg)
                add_to_x(NG - 2)
                add_to_x(NG - 1)
    heads = NG * hpg
    stage_ends(core, loaded=loads, weights_slot0=16 * NG, weights_slot1=16 * NG, out_scaled=2 * B, x_biased=B,
               q_full=NG, k_full=NG, q_plain=NG if split8 else 0, k_plain=NG if split8 else 0,
               q_high=NG if split8 else heads,
               k_high=NG if split8 else heads, q_made=heads, k_made=NG * k_heads, s_full=heads * Q, neg_max=heads * Q,
               diag_made=heads * Q if split8 else 0, probs_full=heads * Q, probs=heads * Q, o_full=heads,
               sums_inverse=heads,
               ctx_ready=heads, ctx_t_full=NG, ctx_turned=NG, y_full=NG, x_added=NG, q_cleared=1,
               rows_cleared=clears, masked=heads * Q if causal else 0, b_cleared=0 if split8 else 2 + hpg,
               max_turned=0 if split8 else heads,
               max_placed=0 if split8 else heads,
               w_high=0 if split8 else NG, w_split=0 if split8 else NG)


def route(core, layer, E, gate_w, gate_b, kind, source=None, chosen=None, weights=None):
    nc = core.nc
    K = 3 if kind == "renormed" else 2
    loaded, full, step, to_exp, exped, iotas = (signal(core, n) for n in
                                                ("loaded", "logits_full", "dve_step", "to_exp", "exped", "iotas"))
    g_cleared = signal(core, "g_cleared")
    counts = {}
    with ExitStack() as ctx:
        tmp = lambda name, shape, dt=F32: ctx.enter_context(nc.sbuf_tensor(f"{name}_r{layer}", shape, dt))
        gw = tmp("gate_w", [P, E])
        gb = tmp("gate_b", [P, E])
        lg = tmp("logits", [P, NT, E])
        top = tmp("top", [P, NT, 8])
        idx = tmp("idx", [P, NT, 8], U32)
        iota_i = tmp("iota_i", [P, E], I32)
        iota = tmp("iota", [P, E])
        wide = [tmp(f"wide{n}", [P, NT, E]) for n in range(4)]
        if chosen is None:
            hot, ws, idx_f = tmp("hot", [P, K, NT, E]), tmp("ws", [P, K, NT]), tmp("idx_f", [P, NT, 8])
        else:
            hot, ws, idx_f = chosen
        thin = [tmp(f"thin{n}", [P, NT]) for n in range(4)]
        ps = ctx.enter_context(nc.psum_tensor(f"logits_ps{layer}", [P, NT, E], F32))
        g = core.g if chosen is None else None
        source = core.h if source is None else source
        over_e = lambda a: a.unsqueeze(2).broadcast_to([P, NT, E])
        val = lambda k: top[:, :, k]
        with nc.Block() as block:

            @block.sync
            def _(sp):
                if weights is not None:
                    weights.load(sp, 0, 0)
                sp.dma_start(gw[:], gate_w).then_inc(loaded.sem, 16)
                if gate_b is not None:
                    sp.dma_start(gb[:], gate_b.broadcast_to([P, E])).then_inc(loaded.sem, 16)

            @block.gpsimd
            def _(pool):
                pool.iota(iota_i[:], pattern=[[1, E]], base=0, channel_multiplier=0).then_inc(iotas.sem, 1)
                if kind == "renormed":
                    pool.memset(g[:, E:E + 2, :], 1.0).then_inc(iotas.sem, 1)
                if chosen is None:
                    pool.memset(core.g_t[:], 0.0).then_inc(g_cleared.sem, 1)
                    pool.memset(core.b2[:], 0.0).then_inc(g_cleared.sem, 1)
                if weights is not None:
                    pool.wait_ge(*weights.slot[0](16 * weights.loads))
                    weights.split_w1(pool, 0, 0)
                    weights.split_w2(pool, 0, 0)

            @block.tensor
            def _(pe):
                pe.wait_ge(*loaded(16 if gate_b is None else 32))
                for t in range(NT):
                    mm = pe.matmul(ps[:, t, :], source[:, t * P:(t + 1) * P], gw[:], start=True, stop=True)
                mm.then_inc(full.sem, 1)

            @block.vector
            def _(dve):
                n = 0

                def link(ins):
                    nonlocal n
                    n += 1
                    ins.then_inc(step.sem, 1)
                    dve.wait_ge(*step(n))

                exps = 0

                def exp_of(out):
                    nonlocal exps
                    exps += 1
                    dve.wait_ge(*exped(exps))

                dve.wait_ge(*iotas(2 if kind == "renormed" else 1))
                link(dve.tensor_copy(iota[:], iota_i[:]))
                dve.wait_ge(*full(1))
                if gate_b is not None:
                    dve.wait_ge(*loaded(32))
                    link(dve.tensor_tensor(lg[:], ps[:], gb[:].unsqueeze(1).broadcast_to([P, NT, E]), ALU.add))
                else:
                    link(dve.tensor_copy(lg[:], ps[:]))
                for t in range(NT):
                    last = dve.max(out=top[:, t, :], in_=lg[:, t, :])
                link(last)
                for t in range(NT):
                    last = dve.max_index(out=idx[:, t, :], in_max=top[:, t, :], in_values=lg[:, t, :])
                link(last)
                link(dve.tensor_copy(idx_f[:], idx[:]))
                for k in range(K):
                    last = dve.tensor_tensor(hot[:, k], iota[:].unsqueeze(1).broadcast_to([P, NT, E]),
                                             over_e(idx_f[:, :, k]), ALU.is_equal)
                link(last)
                if kind == "softmax":
                    dve.tensor_tensor(thin[0][:], val(1), val(0), ALU.subtract).then_inc(to_exp.sem, 1)
                    exp_of(thin[1])
                    link(dve.tensor_scalar(thin[2][:], thin[1][:], 1.0, None, ALU.add))
                    link(dve.reciprocal(ws[:, 0], thin[2][:]))
                    link(dve.tensor_tensor(ws[:, 1], thin[1][:], ws[:, 0], ALU.mult))
                elif kind == "jitter":
                    link(dve.scalar_tensor_tensor(wide[3][:].rearrange("p t e -> p (t e)"),
                                                  lg[:].rearrange("p t e -> p (t e)"), -1.0,
                                                  lg[:].rearrange("p t e -> p (t e)"), ALU.mult, ALU.max))
                    for k in range(2):
                        link(dve.tensor_tensor(wide[0][:], over_e(val(k)), lg[:], ALU.subtract))
                        link(dve.tensor_tensor(wide[1][:], wide[3][:], over_e(val(k)), ALU.max))
                        link(dve.tensor_scalar(wide[1][:], wide[1][:], 0.02, None, ALU.mult))
                        link(dve.tensor_tensor(wide[1][:], wide[0][:], wide[1][:], ALU.is_le))
                        if k == 1:
                            link(dve.tensor_tensor(wide[2][:], wide[1][:], hot[:, 0], ALU.mult))
                            link(dve.tensor_tensor(wide[1][:], wide[1][:], wide[2][:], ALU.subtract))
                        dve.tensor_scalar(wide[0][:], wide[0][:], 0.0, None, ALU.max).then_inc(to_exp.sem, 1)
                        exp_of(wide[2])
                        link(dve.tensor_tensor(wide[2][:], wide[2][:], wide[1][:], ALU.mult))
                        link(dve.tensor_reduce(thin[0][:], wide[2][:], AX_X, ALU.add))
                        link(dve.reciprocal(ws[:, k], thin[0][:]))
                else:
                    dve.tensor_tensor(wide[0][:], lg[:], over_e(val(0)), ALU.subtract).then_inc(to_exp.sem, 1)
                    exp_of(wide[2])
                    link(dve.tensor_reduce(thin[0][:], wide[2][:], AX_X, ALU.add))
                    link(dve.reciprocal(thin[0][:], thin[0][:]))
                    for k in range(K):
                        link(dve.tensor_tensor(wide[0][:], wide[2][:], hot[:, k], ALU.mult))
                        link(dve.tensor_reduce(ws[:, k], wide[0][:], AX_X, ALU.add))
                        link(dve.tensor_tensor(ws[:, k], ws[:, k], thin[0][:], ALU.mult))
                    link(dve.tensor_tensor(thin[1][:], ws[:, 0], ws[:, 1], ALU.add))
                    link(dve.tensor_tensor(thin[1][:], thin[1][:], ws[:, 2], ALU.add))
                    link(dve.tensor_scalar(thin[1][:], thin[1][:], 1e-20, None, ALU.add))
                    link(dve.reciprocal(thin[1][:], thin[1][:]))
                    for k in range(K):
                        last = dve.tensor_tensor(ws[:, k], ws[:, k], thin[1][:], ALU.mult)
                    link(last)
                if chosen is None:
                    for k in range(K):
                        last = dve.tensor_tensor(wide[k][:], hot[:, k], over_e(ws[:, k]), ALU.mult)
                    link(last)
                    if K == 3:
                        link(dve.tensor_tensor(wide[1][:], wide[1][:], wide[2][:], ALU.add))
                    link(dve.tensor_tensor(g[:, 0:E, :].rearrange("p e t -> p t e"), wide[0][:], wide[1][:],
                                           ALU.add))
                counts.update(step=n, exps=exps)

            @block.scalar
            def _(act):
                src, dst, sign = {"softmax": (thin[0], thin[1], 1.0), "jitter": (wide[0], wide[2], -1.0),
                                  "renormed": (wide[0], wide[2], 1.0)}[kind]
                for k in range(counts["exps"]):
                    act.wait_ge(*to_exp(k + 1))
                    act.activation(dst[:], src[:], ACT.Exp, scale=sign).then_inc(exped.sem, 1)
    stage_ends(core, loaded=16 if gate_b is None else 32, logits_full=1, dve_step=counts["step"], to_exp=counts["exps"],
             exped=counts["exps"], g_cleared=2 if chosen is None else 0, iotas=2 if kind == "renormed" else 1)


class ExpertWeights:

    def __init__(self, core, ctx, layer, w1, w2, mult=None):
        tmp = lambda name, shape, dt=F32: ctx.enter_context(core.nc.sbuf_tensor(f"{name}_e{layer}", shape, dt))
        self.w1, self.w2, self.mult, self.zeros = w1, w2, mult, core.zeros
        self.FR, C1, C2 = w2.shape[1], w1.shape[2], w2.shape[2]
        self.w1_s, self.w2_s = tmp("w1_slot", [P, 2, C1]), tmp("w2_slot", [self.FR, 2, C2])
        self.w1_hi, self.w1_lo = tmp("w1_high", [P, 2, C1], F32R), tmp("w1_low", [P, 2, C1], F32R)
        self.w2_hi, self.w2_lo = tmp("w2_high", [self.FR, 2, C2], F32R), tmp("w2_low", [self.FR, 2, C2], F32R)
        self.mu_s = tmp("mult_slot", [self.FR, 2, 1])
        self.w2_m = tmp("w2_scaled", [self.FR, 2, C2]) if mult is not None else self.w2_s
        self.slot = [signal(core, "weights_slot0"), signal(core, "weights_slot1")]
        self.loads = 2 + (mult is not None)
        (self.w1_high, self.w1_split, self.w2_scaled, self.w2_high, self.w2_split) = (
            signal(core, n) for n in ("w1_high", "w1_split", "w2_scaled", "w2_high", "w2_split"))

    def load(self, sp, e, s):
        sp.dma_start(self.w1_s[:, s, :], self.w1[e, :, :]).then_inc(self.slot[s].sem, 16)
        sp.dma_start(self.w2_s[:, s, :], self.w2[e, :, :]).then_inc(self.slot[s].sem, 16)
        if self.mult is not None:
            sp.dma_start(self.mu_s[:, s, :], self.mult[e, :, :]).then_inc(self.slot[s].sem, 16)

    def split(self, pool, high, low, full, made_high, made_low, e):
        pool.tensor_tensor(high, full, self.zeros[0:full.shape[0], 0:full.shape[1]], ALU.add).then_inc(made_high.sem, 1)
        pool.wait_ge(*made_high(e + 1))
        pool.tensor_tensor(low, full, high.bitcast(F32), ALU.subtract).then_inc(made_low.sem, 1)

    def split_w1(self, pool, e, s):
        self.split(pool, self.w1_hi[:, s, :], self.w1_lo[:, s, :], self.w1_s[:, s, :], self.w1_high, self.w1_split, e)

    def split_w2(self, pool, e, s):
        if self.mult is not None:
            pool.tensor_tensor(self.w2_m[:, s, :], self.w2_s[:, s, :],
                               self.mu_s[:, s, :].broadcast_to([self.FR, self.w2_m.shape[2]]), ALU.mult)\
                .then_inc(self.w2_scaled.sem, 1)
            pool.wait_ge(*self.w2_scaled(e + 1))
        self.split(pool, self.w2_hi[:, s, :], self.w2_lo[:, s, :], self.w2_m[:, s, :], self.w2_high, self.w2_split, e)


def gate_rows(core, layer, E, b2):
    nc = core.nc
    loaded, turned, g_copied, g_stored = (signal(core, n) for n in ("loaded", "g_turned", "g_copied", "g_stored"))
    with ExitStack() as ctx:
        t_ps = ctx.enter_context(nc.psum_tensor(f"g_t_ps_{layer}", [P, B, S], F32))
        with nc.Block() as block:

            @block.sync
            def _(sp):
                if b2 is not None:
                    sp.dma_start(core.b2[0:E, :], b2).then_inc(loaded.sem, 16)
                sp.wait_ge(*g_copied(B))
                sp.dma_start(core.g_rows[0:E, :], core.g_t[0:E, :]).then_inc(g_stored.sem, 16)
                sp.wait_ge(*g_stored(16))
                if b2 is not None:
                    sp.wait_ge(*loaded(16))

            @block.tensor
            def _(pe):
                for b in range(B):
                    for q in range(Q):
                        mm = pe.transpose(t_ps[0:E, b, q * P:(q + 1) * P], core.g[:, 0:E, b * Q + q], core.ident[:])
                    mm.then_inc(turned.sem, 1)

            @block.scalar
            def _(act):
                for b in range(B):
                    act.wait_ge(*turned(b + 1))
                    act.copy(core.g_t[0:E, b * S:(b + 1) * S], t_ps[0:E, b, :]).then_inc(g_copied.sem, 1)
    stage_ends(core, loaded=0 if b2 is None else 16, g_turned=B, g_copied=B, g_stored=16)


def experts(core, layer, E, FR, FB, func, weights, b1=None, biased=True):
    nc = core.nc
    parts = weights.w1.shape[2] // (FB * FR)
    glu = parts == 2
    U = B * FB
    LAG = 4
    R = 4 // parts
    (h_high, h_split, up_full, activated, product_made, weighed, a_high, a_made, down_done, y_copied, y_turned) = (
        signal(core, n) for n in (
         "h_high", "h_split", "up_full", "activated", "product_made", "weighed", "a_high", "a_made", "down_done",
         "y_copied", "y_turned"))
    loads, w1_split, w2_split = weights.loads, weights.w1_split, weights.w2_split
    w1_hi, w1_lo, w2_hi, w2_lo = weights.w1_hi, weights.w1_lo, weights.w2_hi, weights.w2_lo
    bslot = [signal(core, "biases_slot0"), signal(core, "biases_slot1")]
    gslot = [[signal(core, f"token_weights_slot{s}_half{k}") for k in range(2)] for s in range(2)]
    head = 3 if E % 2 else 2
    with ExitStack() as ctx:
        tmp = lambda name, shape, dt=F32: ctx.enter_context(nc.sbuf_tensor(f"{name}_e{layer}", shape, dt))
        h_hi, h_lo = tmp("h_high", [P, T], F32R), tmp("h_low", [P, T], F32R)
        b1_s = tmp("b1_slot", [FR, 2, FB * parts])
        g_s = tmp("g_slot", [P, 2, T])
        act_s = tmp("activated", [FR, 2, S])
        prod = tmp("product", [FR, 2, S]) if glu else act_s
        a_f = tmp("weighed", [FR, 4, S])
        a_hi, a_lo = tmp("a_high", [FR, 4, S], F32R), tmp("a_low", [FR, 4, S], F32R)
        y_sb = tmp("y_feat", [P, B, S])
        up = ctx.enter_context(nc.psum_tensor(f"up_ps_{layer}", [P, R, parts, S], F32))
        y_ps = ctx.enter_context(nc.psum_tensor(f"y_ps_{layer}", [P, B, S], F32))
        token_bank = lambda b: up[:, b // parts, b % parts, :]

        def run(eng, window):
            for e in range(head):
                window(e, e % 2, first=e == 0)
            with eng.Fori(0, (E - head - 2) // 2) as i:
                window(2 * i + head, head % 2)
                window(2 * i + head + 1, 1 - head % 2)
            window(E - 2, E % 2)
            window(E - 1, 1 - E % 2, last=True)

        old = lambda e, n: not isinstance(e, int) or e >= n
        with nc.Block() as block:

            @block.sync
            def _(sp):
                def load_biases(e, s):
                    if old(e, 2):
                        sp.wait_ge(*(product_made if glu else activated)((e - 1) * U))
                    sp.dma_start(b1_s[:, s, :], b1[e, :, :]).then_inc(bslot[s].sem, 16)

                def load_token_weights(e, s, k):
                    if old(e, 2):
                        sp.wait_ge(*weighed((e - 2) * U + (k + 1) * U // 2))
                    half = slice(k * T // 2, (k + 1) * T // 2)
                    sp.dma_start(g_s[:, s, half], core.g_rows[bass.ds(e, 1), half].broadcast_to([P, T // 2]))\
                      .then_inc(gslot[s][k].sem, 16)

                def load_next_weights(e, s):
                    if old(e, 1):
                        sp.wait_ge(*w2_split(e))
                    weights.load(sp, e + 1, 1 - s)

                def window(e, s, first=False, last=False):
                    if not last and not first:
                        load_next_weights(e, s)
                    if first and b1 is not None:
                        load_biases(e, s)
                    load_token_weights(e, s, 0)
                    if not first and b1 is not None:
                        load_biases(e, s)
                    load_token_weights(e, s, 1)
                    if first:
                        load_next_weights(e, s)

                run(sp, window)

            @block.gpsimd
            def _(pool):
                def window(e, s, first=False, last=False):
                    if not first:
                        pool.wait_ge(*weights.slot[s](16 * loads * (e // 2 + 1)))
                        if old(e, 2):
                            pool.wait_ge(*up_full((e - 1) * U))
                        weights.split_w1(pool, e, s)
                        if old(e, 2):
                            pool.wait_ge(*down_done((e - 1) * U))
                        weights.split_w2(pool, e, s)

                run(pool, window)

            @block.tensor
            def _(pe):
                def up_proj(e, s, u, first):
                    n = e * U + u
                    c, f = divmod(u, FB)
                    if u == 0:
                        pe.wait_ge(*w1_split(e + 1))
                    if first and f == 0:
                        pe.wait_ge(*h_split(c + 1))
                    if not (first and u < R):
                        pe.wait_ge(*(product_made if glu else activated)(n - R + 1))
                    for k in range(parts):
                        w = slice((f * parts + k) * FR, (f * parts + k + 1) * FR)
                        t = slice(c * S, (c + 1) * S)
                        mm = three_passes(pe, up[0:FR, u % R, k, :], w1_hi[:, s, w], w1_lo[:, s, w], h_hi[:, t],
                                          h_lo[:, t])
                    mm.then_inc(up_full.sem, 1)

                def down_proj(e, s, u):
                    n = e * U + u
                    c, f = divmod(u, FB)
                    if u == 0:
                        pe.wait_ge(*w2_split(e + 1))
                    pe.wait_ge(*a_made(n + 1))
                    w = slice(f * P, (f + 1) * P)
                    begins = isinstance(e, int) and e == 0 and f == 0
                    three_passes(pe, y_ps[:, c, :], w2_hi[:, s, w], w2_lo[:, s, w], a_hi[:, u % 4, :], a_lo[:, u % 4, :],
                                 begins).then_inc(down_done.sem, 1)

                def window(e, s, first=False, last=False):
                    for u in range(U):
                        up_proj(e, s, u, first)
                        if u >= LAG:
                            down_proj(e, s, u - LAG)
                        elif not first:
                            down_proj(e - 1, 1 - s, u - LAG + U)
                    if biased and isinstance(e, int) and e == 1:
                        for b in range(B):
                            pe.matmul(y_ps[:, b, :], core.b2[:], core.g_t[:, b * S:(b + 1) * S], start=False,
                                      stop=True, skip_group_check=True)
                    if last:
                        for u in range(U - LAG, U):
                            down_proj(e, s, u)

                run(pe, window)
                for b in range(B):
                    pe.wait_ge(*y_copied(b + 1))
                    for q in range(Q):
                        mm = pe.transpose(token_bank(b)[:, q * P:(q + 1) * P], y_sb[:, b, q * P:(q + 1) * P],
                                          core.ident[:])
                    mm.then_inc(y_turned.sem, 1)

            @block.scalar
            def _(act):
                ahead = 2 if glu else 1

                def high(n, u):
                    act.wait_ge(*weighed(n + 1))
                    if not isinstance(n, int) or n >= 4:
                        act.wait_ge(*down_done(n - 4 + 1))
                    act.copy(a_hi[:, u % 4, :], a_f[:, u % 4, :]).then_inc(a_high.sem, 1)

                def window(e, s, first=False, last=False):
                    for u in range(U):
                        n = e * U + u
                        f = u % FB
                        act.wait_ge(*up_full(n + 1))
                        if u == 0 and b1 is not None:
                            act.wait_ge(*bslot[s](16 * (e // 2 + 1)))
                        if not (first and u < 2):
                            act.wait_ge(*(product_made if glu else weighed)(n - 2 + 1))
                        bias = b1_s[:, s, parts * f:parts * f + 1] if b1 is not None else 0.0
                        act.activation(act_s[:, u % 2, :], up[0:FR, u % R, 0, :], func, bias=bias)\
                           .then_inc(activated.sem, 1)
                        if not (first and u < ahead):
                            high(n - ahead, (u - ahead) % U)
                    if last:
                        for u in range(U - ahead, U):
                            high(e * U + u, u)

                for b in range(B):
                    act.copy(h_hi[:, b * S:(b + 1) * S], core.h[:, b * S:(b + 1) * S]).then_inc(h_high.sem, 1)
                run(act, window)
                for b in range(B):
                    act.wait_ge(*down_done(E * U - U + (b + 1) * FB))
                    act.activation(y_sb[:, b, :], y_ps[:, b, :], ACT.Copy, scale=core.gate_f[:, 1, layer, b:b + 1])\
                       .then_inc(y_copied.sem, 1)

            @block.vector
            def _(dve):
                def product(e, s, u, first):
                    n = e * U + u
                    f = u % FB
                    if u == 0 and b1 is not None:
                        dve.wait_ge(*bslot[s](16 * (e // 2 + 1)))
                    dve.wait_ge(*activated(n + 1))
                    if not (first and u < 2):
                        dve.wait_ge(*weighed(n - 2 + 1))
                    out, lin = prod[:, u % 2, :], up[0:FR, u % R, 1, :]
                    if b1 is None:
                        ins = dve.tensor_tensor(out, lin, act_s[:, u % 2, :], ALU.mult)
                    else:
                        ins = dve.scalar_tensor_tensor(out, lin, b1_s[:, s, 2 * f + 1:2 * f + 2],
                                                       act_s[:, u % 2, :], ALU.add, ALU.mult)
                    ins.then_inc(product_made.sem, 1)

                def weigh(e, s, u, first):
                    n = e * U + u
                    c = u // FB
                    if u % (U // 2) == 0:
                        dve.wait_ge(*gslot[s][u // (U // 2)](16 * (e // 2 + 1)))
                    dve.wait_ge(*(product_made if glu else activated)(n + 1))
                    if not (first and u < 4):
                        dve.wait_ge(*a_made(n - 4 + 1))
                    dve.tensor_tensor(a_f[:, u % 4, :], prod[:, u % 2, :], g_s[0:FR, s, c * S:(c + 1) * S],
                                      ALU.mult).then_inc(weighed.sem, 1)

                def low(n, u):
                    dve.wait_ge(*a_high(n + 1))
                    dve.tensor_tensor(a_lo[:, u % 4, :], a_f[:, u % 4, :], a_hi[:, u % 4, :].bitcast(F32), ALU.subtract)\
                       .then_inc(a_made.sem, 1)

                behind = 1 if glu else 0

                def window(e, s, first=False, last=False):
                    for u in range(U):
                        if glu:
                            product(e, s, u, first)
                        if u >= behind:
                            weigh(e, s, u - behind, first)
                        elif not first:
                            weigh(e - 1, 1 - s, u - behind + U, False)
                        if not (first and u < behind + 1):
                            low(e * U + u - behind - 1, (u - behind - 1) % U)
                    if last:
                        for u in range(U - behind, U):
                            weigh(e, s, u, False)
                        for u in range(U - behind - 1, U):
                            low(e * U + u, u)

                for b in range(B):
                    t = slice(b * S, (b + 1) * S)
                    dve.wait_ge(*h_high(b + 1))
                    dve.tensor_tensor(h_lo[:, t], core.h[:, t], h_hi[:, t].bitcast(F32), ALU.subtract)\
                       .then_inc(h_split.sem, 1)
                run(dve, window)
                for b in range(B):
                    dve.wait_ge(*y_turned(b + 1))
                    xb = core.x[:, Q * b:Q * b + Q, :]
                    dve.tensor_tensor(xb, xb, token_bank(b).rearrange("p (q d) -> p q d", q=Q), ALU.add)
    units = E * U
    stage_ends(core, h_high=B, h_split=B, up_full=units, activated=units, product_made=units if glu else 0,
               weighed=units, a_high=units, a_made=units, down_done=units, w1_high=E, w1_split=E,
               w2_scaled=E if weights.mult is not None else 0, w2_high=E, w2_split=E, y_copied=B, y_turned=B,
               weights_slot0=16 * loads * ((E + 1) // 2), weights_slot1=16 * loads * (E // 2),
               biases_slot0=16 * ((E + 1) // 2) if b1 is not None else 0,
               biases_slot1=16 * (E // 2) if b1 is not None else 0,
               **{f"token_weights_slot{s}_half{k}": 16 * ((E + 1 - s) // 2) for s in range(2) for k in range(2)})


def latents(core, wkd, bkd, out):
    nc = core.nc
    loaded, full, gelu, lat = (signal(core, n) for n in ("loaded", "lat_psum", "lat_gelu", "lat_made"))
    rest_set = signal(core, "lat_rest_set")
    with ExitStack() as ctx:
        w = ctx.enter_context(nc.sbuf_tensor("wkd_sb", [P, 2, 32], F32))
        bb = ctx.enter_context(nc.sbuf_tensor("bkd_sb", [32, 2], F32))
        g = ctx.enter_context(nc.sbuf_tensor("lat_gelu_sb", [32, B, 2, S], F32))
        ps = ctx.enter_context(nc.psum_tensor("lat_ps", [32, B, 2, S], F32))
        with nc.Block() as block:

            @block.sync
            def _(sp):
                sp.dma_start(w[:], wkd.rearrange("a k n -> k a n")).then_inc(loaded.sem, 16)
                sp.dma_start(bb[:], bkd).then_inc(loaded.sem, 16)

            @block.gpsimd
            def _(pool):
                pool.memset(out[:], 0.0).then_inc(rest_set.sem, 1)
                pool.wait_ge(*rest_set(1))
                pool.memset(out[32:33, :], 1.0).then_inc(rest_set.sem, 1)

            @block.tensor
            def _(pe):
                pe.wait_ge(*loaded(32))
                for b in range(B):
                    for a in range(2):
                        mm = pe.matmul(ps[:, b, a, :], w[:, a, :], core.h[:, b * S:(b + 1) * S], start=True, stop=True)
                    mm.then_inc(full.sem, 1)

            @block.scalar
            def _(act):
                for b in range(B):
                    act.wait_ge(*full(b + 1))
                    for a in range(2):
                        ins = act.activation(g[:, b, a, :], ps[:, b, a, :], ACT.Gelu, bias=bb[:, a:a + 1])
                    ins.then_inc(gelu.sem, 1)

            @block.vector
            def _(dve):
                dve.wait_ge(*rest_set(1))
                for b in range(B):
                    dve.wait_ge(*gelu(b + 1))
                    dve.tensor_tensor(out[0:32, b * S:(b + 1) * S], g[:, b, 0, :], g[:, b, 1, :], ALU.add)\
                       .then_inc(lat.sem, 1)
    stage_ends(core, loaded=32, lat_psum=B, lat_gelu=B, lat_made=B, lat_rest_set=2)


def rms_norm(core, name, layer, half, eps, w, out_tok, out_feat):
    nc = core.nc
    names = ("loaded", "squared", "sq_summed", "rms_step", "rms_root", "h_turned", "h_scaled", "n_turned", "n_made")
    (loaded, squared, summed, step, root, h_turned, h_scaled, n_turned, n_made) = (signal(core, n) for n in names)
    with ExitStack() as ctx:
        tmp = lambda nm, shape, dt=F32: ctx.enter_context(nc.sbuf_tensor(f"{nm}_{name}", shape, dt))
        w_sb = tmp("rms_w", [P, 1])
        sq = tmp("rms_sq", [P, T])
        ms = tmp("rms_ms", [P, NT])
        sd = tmp("rms_sd", [P, NT])
        rs = tmp("rms_rs", [P, NT])
        hg = tmp("rms_hg", [P, 2, Q, P])
        s_ps = ctx.enter_context(nc.psum_tensor(f"rms_s_{name}", [P, NT], F32))
        h_ps = ctx.enter_context(nc.psum_tensor(f"rms_h_{name}", [P, 2, S], F32))
        n_ps = ctx.enter_context(nc.psum_tensor(f"rms_n_{name}", [P, 2, S], F32))
        with nc.Block() as block:

            @block.sync
            def _(sp):
                sp.dma_start(w_sb[:], w).then_inc(loaded.sem, 16)

            @block.scalar
            def _(act):
                act.wait_ge(*loaded(16))
                for b in range(B):
                    act.activation(sq[:, b * S:(b + 1) * S], core.h[:, b * S:(b + 1) * S], ACT.Square)\
                       .then_inc(squared.sem, 1)
                act.wait_ge(*step(1))
                act.activation(sd[:], ms[:], ACT.Sqrt).then_inc(root.sem, 1)
                for b in range(B):
                    act.wait_ge(*n_turned(b + 1))
                    act.activation(out_feat[:, b * S:(b + 1) * S], n_ps[:, b % 2, :], ACT.Copy, scale=w_sb[:, 0:1])\
                       .then_inc(n_made.sem, 1)

            def turn_back(pe, b):
                pe.wait_ge(*h_scaled(b + 1))
                if b >= 2:
                    pe.wait_ge(*n_made(b - 1))
                for q in range(Q):
                    mm = pe.transpose(n_ps[:, b % 2, q * P:(q + 1) * P], out_tok[:, b * Q + q, :], core.ident[:])
                mm.then_inc(n_turned.sem, 1)

            @block.tensor
            def _(pe):
                for b in range(B):
                    pe.wait_ge(*squared(b + 1))
                    for t in range(b * Q, b * Q + Q):
                        mm = pe.matmul(s_ps[:, t:t + 1], sq[:, t * P:(t + 1) * P], core.ones[:, 0:1], start=True,
                                       stop=True)
                mm.then_inc(summed.sem, 1)
                for b in range(B):
                    if b >= 2:
                        pe.wait_ge(*h_scaled(b - 1))
                    for q in range(Q):
                        t = b * Q + q
                        mm = pe.transpose(h_ps[:, b % 2, q * P:(q + 1) * P], core.h[:, t * P:(t + 1) * P], core.ident[:])
                    mm.then_inc(h_turned.sem, 1)
                    if b >= 1:
                        turn_back(pe, b - 1)
                turn_back(pe, B - 1)

            @block.vector
            def _(dve):
                dve.wait_ge(*summed(1))
                dve.tensor_scalar(ms[:], s_ps[:], 1.0 / P, eps, ALU.mult, ALU.add).then_inc(step.sem, 1)
                dve.wait_ge(*root(1))
                dve.reciprocal(rs[:], sd[:]).then_inc(step.sem, 1)
                dve.wait_ge(*step(2))
                for b in range(B):
                    dve.wait_ge(*h_turned(b + 1))
                    h3 = h_ps[:, b % 2, :].rearrange("p (q d) -> p q d", q=Q)
                    dve.tensor_tensor(hg[:, b % 2], h3, core.gate[:, layer, half, b, :].unsqueeze(1)
                                      .broadcast_to([P, Q, P]), ALU.mult).then_inc(step.sem, 1)
                    dve.tensor_tensor(out_tok[:, b * Q:b * Q + Q, :], h3,
                                      rs[:, b * Q:b * Q + Q].unsqueeze(2).broadcast_to([P, Q, P]), ALU.mult)\
                       .then_inc(h_scaled.sem, 1)
                    dve.wait_ge(*step(3 + b))
                    xb = core.x[:, b * Q:b * Q + Q, :]
                    dve.tensor_tensor(xb, xb, hg[:, b % 2], ALU.add)
    stage_ends(core, loaded=16, squared=B, sq_summed=1, rms_step=2 + B, rms_root=1, h_turned=B, h_scaled=B, n_turned=B,
             n_made=B)


def gated_scan(core, layer, xn, w_in, b_uz, b_g, w_x, w_dt, b_xdt, w_out, b_out):
    nc = core.nc
    H = 64
    names = ("loaded", "p_full", "uz_made", "sg_made", "ud_full", "ut_made", "dt_made", "scan_step", "y_made",
             "out_full", "out_added", "gs_cleared")
    (loaded, p_full, uz_made, sg_made, ud_full, ut_made, dt_made, step, y_made, out_full, out_added, cleared) = (
        signal(core, n) for n in names)
    with ExitStack() as ctx:
        tmp = lambda nm, shape, dt=F32: ctx.enter_context(nc.sbuf_tensor(f"gs_{nm}", shape, dt))
        win = tmp("w_in", [P, 3 * H])
        buz, bg = tmp("b_uz", [P, 1]), tmp("b_g", [H, 1])
        wxdt = tmp("w_xdt", [P, P])
        bxdt = tmp("b_xdt", [P, 1])
        wout = tmp("w_out", [P, P])
        uz, sg, ut, dt, a, bb, h, y = (tmp(n, [P, 2, S]) for n in "uz sg ut dt a b h y".split())
        r = slice(H, P)
        og = tmp("og", [P, 2, Q, P])
        p_ps = ctx.enter_context(nc.psum_tensor("gs_p", [P, 2, S], F32))
        ud_ps = ctx.enter_context(nc.psum_tensor("gs_ud", [P, S], F32))
        o_ps = ctx.enter_context(nc.psum_tensor("gs_o", [P, 2, S], F32))
        with nc.Block() as block:

            @block.sync
            def _(sp):
                for dst, src in ((win, w_in), (buz, b_uz), (bg, b_g), (bxdt, b_xdt)):
                    sp.dma_start(dst[:], src).then_inc(loaded.sem, 16)
                sp.wait_ge(*cleared(4))
                for dst, src in ((wxdt[0:H, 0:H], w_x), (wxdt[r, r], w_dt), (wout[r, :], w_out), (wout[0:1, :], b_out)):
                    sp.dma_start(dst, src).then_inc(loaded.sem, 16)

            @block.gpsimd
            def _(pool):
                for m in (wxdt, wout, y):
                    pool.memset(m[:], 0.0).then_inc(cleared.sem, 1)
                pool.wait_ge(*cleared(3))
                pool.memset(y[0:1], 1.0).then_inc(cleared.sem, 1)

            @block.tensor
            def _(pe):
                def project_in(b):
                    if b:
                        pe.wait_ge(*uz_made(b))
                        pe.wait_ge(*sg_made(b))
                    for k, m in enumerate((P, H)):
                        mm = pe.matmul(p_ps[0:m, k, :], win[:, k * P:k * P + m], xn[:, b * S:(b + 1) * S], start=True,
                                       stop=True)
                    mm.then_inc(p_full.sem, 1)

                pe.wait_ge(*loaded(16 * 8))
                project_in(0)
                for b in range(B):
                    pe.wait_ge(*uz_made(b + 1))
                    if b:
                        pe.wait_ge(*ut_made(b))
                        pe.wait_ge(*dt_made(b))
                    pe.matmul(ud_ps[:], wxdt[:], uz[:, b % 2, :], start=True, stop=True).then_inc(ud_full.sem, 1)
                    if b + 1 < B:
                        project_in(b + 1)
                    pe.wait_ge(*y_made(b + 1))
                    if b >= 2:
                        pe.wait_ge(*out_added(b - 1))
                    for q in range(Q):
                        at = slice(q * P, (q + 1) * P)
                        mm = pe.matmul(o_ps[:, b % 2, at], y[:, b % 2, at], wout[:], start=True, stop=True)
                    mm.then_inc(out_full.sem, 1)

            @block.scalar
            def _(act):
                act.wait_ge(*loaded(16 * 8))
                for b in range(B):
                    act.wait_ge(*p_full(b + 1))
                    act.activation(uz[:, b % 2, :], p_ps[:, 0, :], ACT.Identity, bias=buz[:, 0:1])\
                       .then_inc(uz_made.sem, 1)
                    if b >= 2:
                        act.wait_ge(*y_made(b - 1))
                    act.activation(sg[r, b % 2, :], p_ps[0:H, 1, :], ACT.Sigmoid, bias=bg[:, 0:1])\
                       .then_inc(sg_made.sem, 1)
                    act.wait_ge(*ud_full(b + 1))
                    act.activation(ut[r, b % 2, :], ud_ps[0:H, :], ACT.Tanh, bias=bxdt[0:H, 0:1]).then_inc(ut_made.sem, 1)
                    act.activation(dt[r, b % 2, :], ud_ps[r, :], ACT.Sigmoid, bias=bxdt[r, 0:1])\
                       .then_inc(dt_made.sem, 1)

            @block.vector
            def _(dve):
                dve.wait_ge(*cleared(4))
                n = 0
                for b in range(B):
                    k = b % 2
                    dve.wait_ge(*ut_made(b + 1))
                    dve.wait_ge(*dt_made(b + 1))
                    dve.tensor_scalar(a[r, k, :], dt[r, k, :], -1.0, 1.0, ALU.mult, ALU.add).then_inc(step.sem, 1)
                    dve.tensor_tensor(bb[r, k, :], dt[r, k, :], ut[r, k, :], ALU.mult).then_inc(step.sem, 1)
                    dve.wait_ge(*step(n + 2))
                    dve.tensor_tensor_scan(h[r, k, :], a[r, k, :], bb[r, k, :], 0.0, ALU.mult, ALU.add)\
                       .then_inc(step.sem, 1)
                    dve.wait_ge(*step(n + 3))
                    dve.wait_ge(*sg_made(b + 1))
                    dve.tensor_tensor(y[r, k, :], h[r, k, :], sg[r, k, :], ALU.mult).then_inc(y_made.sem, 1)
                    dve.wait_ge(*out_full(b + 1))
                    dve.tensor_tensor(og[:, k], o_ps[:, k, :].rearrange("p (q d) -> p q d", q=Q),
                                      core.gate[:, layer, 0, b, :].unsqueeze(1).broadcast_to([P, Q, P]), ALU.mult)\
                       .then_inc(out_added.sem, 1)
                    dve.wait_ge(*out_added(b + 1))
                    xb = core.x[:, b * Q:b * Q + Q, :]
                    dve.tensor_tensor(xb, xb, og[:, k], ALU.add)
                    n += 3
    stage_ends(core, loaded=128, gs_cleared=4, p_full=B, uz_made=B, sg_made=B, ud_full=B, ut_made=B, dt_made=B, scan_step=3 * B,
             y_made=B, out_full=B, out_added=B)


def dispatch(core, hot, ws, idx_f, slot, tokens):
    nc = core.nc
    step, tri_set, m_set, r_set, pos_full, slot_set, scattered = (signal(core, n) for n in (
        "dve_step", "tri_set", "m_set", "r_set", "pos_full", "slot_set", "scattered"))
    zeroed = signal(core, "slots_zeroed")
    E = L3_E
    counts = {}
    with ExitStack() as ctx:
        tmp = lambda name, shape, dt=F32: ctx.enter_context(nc.sbuf_tensor(f"d_{name}", shape, dt))
        tri = tmp("tri", [P, P], BF16)
        ones = tmp("ones", [P, P], BF16)
        m = tmp("m", [P, NT, E], BF16)
        before = tmp("before", [P, NT, E], BF16)
        wide = tmp("wide", [P, NT, E])
        pos = tmp("pos", [P, 2, NT])
        over = tmp("over", [P, 2, NT])
        slot_f = tmp("slot_f", [P, 2, NT])
        ps = ctx.enter_context(nc.psum_tensor("pos_ps", [P, NT, E], F32))
        with nc.Block() as block:

            @block.gpsimd
            def _(pool):
                pool.memset(ones[:], 1.0).then_inc(tri_set.sem, 1)
                pool.wait_ge(*tri_set(1))
                pool.affine_select(out=tri[:], in_=ones[:], compare_op=ALU.is_gt, fill=0.0, base=0, pattern=[[1, P]],
                                   channel_multiplier=-1).then_inc(tri_set.sem, 1)
                pool.wait_ge(*zeroed(16 * ZERO_FILLS))
                pool.wait_ge(*slot_set(1))
                for k in range(2):
                    for t in range(NT):
                        pool.indirect_dma_start(out=core.slots_in,
                                                out_offset=bass.IndirectOffsetOnAxis(ap=slot[:, k, t:t + 1], axis=0),
                                                in_=tokens[:, t, :], in_offset=None, bounds_check=L3_SLOTS - 1,
                                                oob_is_err=False).then_inc(scattered.sem, 16)
                pool.wait_ge(*scattered(16 * 2 * NT))

            @block.tensor
            def _(pe):
                pe.wait_ge(*tri_set(2))
                pe.wait_ge(*m_set(1))
                pe.wait_ge(*r_set(NT))
                for t in range(NT):
                    pe.matmul(ps[:, t, :], tri[:], m[:, t, :], start=True, stop=False)
                    mm = pe.matmul(ps[:, t, :], ones[:], before[:, t, :], start=False, stop=True)
                mm.then_inc(pos_full.sem, 1)

            @block.vector
            def _(dve):
                n = 0

                def link(ins):
                    nonlocal n
                    n += 1
                    ins.then_inc(step.sem, 1)
                    dve.wait_ge(*step(n))

                dve.tensor_tensor(m[:], hot[:, 0], hot[:, 1], ALU.add).then_inc(m_set.sem, 1)
                dve.memset(before[:, 0, :], 0.0).then_inc(r_set.sem, 1)
                dve.wait_ge(*m_set(1))
                for t in range(1, NT):
                    dve.wait_ge(*r_set(t))
                    dve.tensor_tensor(before[:, t, :], before[:, t - 1, :], m[:, t - 1, :], ALU.add)\
                       .then_inc(r_set.sem, 1)
                dve.wait_ge(*pos_full(1))
                for k in range(2):
                    link(dve.tensor_tensor(wide[:], ps[:], hot[:, k], ALU.mult))
                    link(dve.tensor_reduce(pos[:, k, :], wide[:], AX_X, ALU.add))
                link(dve.tensor_scalar(over[:], pos[:], float(CAP), None, ALU.is_lt))
                link(dve.tensor_tensor(ws[:], ws[:], over[:], ALU.mult))
                for k in range(2):
                    last = dve.tensor_scalar(slot_f[:, k, :], idx_f[:, :, k], float(CAP), None, ALU.mult)
                link(last)
                link(dve.tensor_tensor(slot_f[:], slot_f[:], pos[:], ALU.add))
                link(dve.tensor_scalar(over[:], pos[:], float(CAP), float(4 * L3_SLOTS), ALU.is_ge, ALU.mult))
                link(dve.tensor_tensor(slot_f[:], slot_f[:], over[:], ALU.add))
                dve.tensor_copy(slot[:], slot_f[:]).then_inc(slot_set.sem, 1)
                counts.update(step=n)
    stage_ends(core, dve_step=counts["step"], tri_set=2, m_set=1, r_set=NT, pos_full=1, slot_set=1, scattered=32 * NT,
             slots_zeroed=16 * ZERO_FILLS)


def slot_experts(core, rms_w, w13, w2, y_next):
    nc = core.nc
    G = 4
    NW = L3_E // G
    RING = 4
    H = 64
    names = ("loaded", "xb_turned", "xt_made", "gu_full", "silu_made", "hh_made", "yb_full", "yb_copied")
    (loaded, xb_turned, xt_made, gu_full, silu_made, hh_made, yb_full, yb_copied) = (signal(core, n) for n in names)
    hh_cleared, y_cleared = signal(core, "hh_cleared"), signal(core, "y_cleared")
    ring = [signal(core, f"ring_slot{k}") for k in range(RING)]
    stored = [signal(core, "stored_even"), signal(core, "stored_odd")]
    src = core.slots_in.rearrange("(w j p) d -> w p j d", j=G, p=P)
    dst = core.slots_out.rearrange("(w j p) d -> w p j d", j=G, p=P)
    w13_v = w13.rearrange("(w j) k n -> w k j n", j=G)
    w2_v = w2.rearrange("(w a t) k n -> w (t k) a n", a=G // 2, t=2)
    with ExitStack() as ctx:
        tmp = lambda name, shape, dt=F32: ctx.enter_context(nc.sbuf_tensor(f"se_{name}", shape, dt))
        rw = tmp("rms_w", [P, 1])
        xb = tmp("xb", [P, RING, G, P])
        w13_s = tmp("w13", [P, RING, G, P])
        w2_s = tmp("w2", [P, RING, G // 2, P])
        xt = tmp("xt", [P, 2, S])
        sg = tmp("sg", [P, 2, S])
        hh = tmp("hh", [P, 2, S])
        y = tmp("y", [P, 2, G, P])
        t_ps = ctx.enter_context(nc.psum_tensor("se_t", [P, 2, S], F32))
        gu_ps = ctx.enter_context(nc.psum_tensor("se_gu", [P, 2, S], F32))
        y_ps = ctx.enter_context(nc.psum_tensor("se_y_ps", [P, 2, S], F32))

        def run(eng, window):
            for i in range(RING):
                window(i, i)
            with eng.Fori(1, NW // RING) as r:
                for k in range(RING):
                    window(r * RING + k, k)
            for i in range(NW, NW + 2):
                window(i, i % RING)

        new = lambda i: not isinstance(i, int) or i < NW
        old = lambda i, n: not isinstance(i, int) or i >= n
        with nc.Block() as block:

            @block.sync
            def _(sp):
                sp.dma_start(rw[:], rms_w).then_inc(loaded.sem, 16)

                def window(i, k):
                    if new(i):
                        if old(i, RING):
                            sp.wait_ge(*yb_full(i - RING + 1))
                        sp.dma_start(xb[:, k], src[i]).then_inc(ring[k].sem, 16)
                        sp.dma_start(w13_s[:, k], w13_v[i]).then_inc(ring[k].sem, 16)
                        sp.dma_start(w2_s[:, k], w2_v[i]).then_inc(ring[k].sem, 16)

                run(sp, window)

            @block.tensor
            def _(pe):
                def window(i, k):
                    if new(i):
                        pe.wait_ge(*ring[k](48 * (i // RING + 1)))
                        if old(i, 2):
                            pe.wait_ge(*xt_made(i - 1))
                        for j in range(G):
                            mm = pe.transpose(t_ps[:, k % 2, j * P:(j + 1) * P], xb[:, k, j, :], core.ident[:])
                        mm.then_inc(xb_turned.sem, 1)
                    if old(i, 1) and (not isinstance(i, int) or i - 1 < NW):
                        kk = (k - 1) % RING
                        pe.wait_ge(*xt_made(i))
                        if old(i, 3):
                            pe.wait_ge(*hh_made(i - 2))
                        for j in range(G):
                            at = slice(j * P, (j + 1) * P)
                            mm = pe.matmul(gu_ps[:, kk % 2, at], w13_s[:, kk, j, :], xt[:, kk % 2, at], start=True,
                                           stop=True)
                        mm.then_inc(gu_full.sem, 1)
                    if old(i, 2):
                        kk = (k - 2) % RING
                        pe.wait_ge(*hh_made(i - 1))
                        if old(i, 4):
                            pe.wait_ge(*yb_copied(i - 3))
                        for j in range(G):
                            at = slice(j * P, (j + 1) * P)
                            mm = pe.matmul(y_ps[:, kk % 2, at], hh[:, kk % 2, at], w2_s[:, kk, j // 2, :], start=True,
                                           stop=True)
                        mm.then_inc(yb_full.sem, 1)

                run(pe, window)

            @block.scalar
            def _(act):
                def window(i, k):
                    if new(i):
                        act.wait_ge(*xb_turned(i + 1))
                        if old(i, 2):
                            act.wait_ge(*gu_full(i - 1))
                        act.activation(xt[:, k % 2, :], t_ps[:, k % 2, :], ACT.Copy, scale=rw[:, 0:1])\
                           .then_inc(xt_made.sem, 1)
                    if old(i, 1) and (not isinstance(i, int) or i - 1 < NW):
                        kk = (k - 1) % RING
                        act.wait_ge(*gu_full(i))
                        act.activation(sg[H:P, kk % 2, :], gu_ps[0:H, kk % 2, :], ACT.Silu).then_inc(silu_made.sem, 1)

                act.wait_ge(*loaded(16))
                run(act, window)

            @block.vector
            def _(dve):
                def window(i, k):
                    if old(i, 1) and (not isinstance(i, int) or i - 1 < NW):
                        kk = (k - 1) % RING
                        dve.wait_ge(*silu_made(i))
                        if old(i, 3):
                            dve.wait_ge(*yb_full(i - 2))
                        for t in range(2):
                            mine = lambda a, rows: a[rows, kk % 2, :].rearrange("p (a t c) -> p a t c", t=2,
                                                                                c=P)[:, :, t, :]
                            up = slice(H, P)
                            last = dve.tensor_tensor(mine(hh, slice(t * H, t * H + H)), mine(sg, up),
                                                     mine(gu_ps, up), ALU.mult)
                        last.then_inc(hh_made.sem, 1)
                    if old(i, 2):
                        kk = (k - 2) % RING
                        dve.wait_ge(*yb_full(i - 1))
                        if old(i, 4):
                            dve.wait_ge(*stored[kk % 2](16 * ((i - 2) // 2)))
                        dve.tensor_copy(y[:, kk % 2], y_ps[:, kk % 2, :].rearrange("p (j d) -> p j d", j=G))\
                           .then_inc(yb_copied.sem, 1)

                dve.memset(y_next[:], 0.0).then_inc(y_cleared.sem, 1)
                dve.wait_ge(*hh_cleared(1))
                run(dve, window)

            @block.gpsimd
            def _(pool):
                pool.memset(hh[:], 0.0).then_inc(hh_cleared.sem, 1)

                def window(i, k):
                    if old(i, 2):
                        kk = (k - 2) % RING
                        pool.wait_ge(*yb_copied(i - 1))
                        pool.dma_start(dst[i - 2], y[:, kk % 2]).then_inc(stored[kk % 2].sem, 16)

                run(pool, window)
                for s in stored:
                    pool.wait_ge(*s(16 * NW // 2))
    stage_ends(core, loaded=16, hh_cleared=1, y_cleared=1,
             xb_turned=NW, xt_made=NW, gu_full=NW, silu_made=NW, hh_made=NW, yb_full=NW, yb_copied=NW,
             ring_slot0=12 * NW, ring_slot1=12 * NW, ring_slot2=12 * NW, ring_slot3=12 * NW,
             stored_even=8 * NW, stored_odd=8 * NW)


def combine(core, xn, ws, slot, y, w_gate, w_up, w_down):
    nc = core.nc
    H = 64
    names = ("loaded", "gu_full", "silu_made", "hh_made", "shared_full", "mix_step")
    (loaded, gu_full, silu_made, hh_made, shared_full, step) = (signal(core, n) for n in names)
    gathered = [signal(core, f"gathered{b}") for b in range(B)]
    with ExitStack() as ctx:
        tmp = lambda name, shape, dt=F32: ctx.enter_context(nc.sbuf_tensor(f"cm_{name}", shape, dt))
        wg, wu = tmp("w_gate", [P, H]), tmp("w_up", [P, H])
        wd = tmp("w_down", [H, P])
        sg, hh = tmp("sg", [H, 2, S]), tmp("hh", [H, 2, S])
        acc = tmp("acc", [P, NT, P])
        gu = ctx.enter_context(nc.psum_tensor("cm_gu", [H, 2, 2, S], F32))
        sh = ctx.enter_context(nc.psum_tensor("cm_sh", [P, B, S], F32))
        with nc.Block() as block:

            @block.sync
            def _(sp):
                for dst, src in ((wg, w_gate), (wu, w_up), (wd, w_down)):
                    sp.dma_start(dst[:], src).then_inc(loaded.sem, 16)

            @block.gpsimd
            def _(pool):
                for t in range(NT):
                    for k in range(2):
                        pool.indirect_dma_start(out=y[:, k, t, :], out_offset=None, in_=core.slots_out,
                                                in_offset=bass.IndirectOffsetOnAxis(ap=slot[:, k, t:t + 1], axis=0),
                                                bounds_check=L3_SLOTS - 1, oob_is_err=False)\
                            .then_inc(gathered[t // Q].sem, 16)

            @block.tensor
            def _(pe):
                def up(b):
                    if b >= 2:
                        pe.wait_ge(*hh_made(b - 1))
                    pe.matmul(gu[:, b % 2, 0, :], wg[:], xn[:, b * S:(b + 1) * S], start=True, stop=True)
                    pe.matmul(gu[:, b % 2, 1, :], wu[:], xn[:, b * S:(b + 1) * S], start=True, stop=True)\
                      .then_inc(gu_full.sem, 1)

                pe.wait_ge(*loaded(48))
                up(0)
                for b in range(B):
                    if b + 1 < B:
                        up(b + 1)
                    pe.wait_ge(*hh_made(b + 1))
                    for q in range(Q):
                        mm = pe.matmul(sh[:, b, q * P:(q + 1) * P], hh[:, b % 2, q * P:(q + 1) * P], wd[:], start=True,
                                       stop=True)
                    mm.then_inc(shared_full.sem, 1)

            @block.scalar
            def _(act):
                for b in range(B):
                    act.wait_ge(*gu_full(b + 1))
                    act.activation(sg[:, b % 2, :], gu[:, b % 2, 0, :], ACT.Silu).then_inc(silu_made.sem, 1)

            @block.vector
            def _(dve):
                for b in range(B):
                    dve.wait_ge(*silu_made(b + 1))
                    if b >= 2:
                        dve.wait_ge(*shared_full(b - 1))
                    dve.tensor_tensor(hh[:, b % 2, :], sg[:, b % 2, :], gu[:, b % 2, 1, :], ALU.mult)\
                       .then_inc(hh_made.sem, 1)
                n = 0
                for b in range(B):
                    dve.wait_ge(*shared_full(b + 1))
                    dve.wait_ge(*gathered[b](16 * 2 * Q))
                    for k in range(2):
                        for q in range(Q):
                            t = b * Q + q
                            base = sh[:, b, q * P:(q + 1) * P] if k == 0 else acc[:, t, :]
                            last = dve.scalar_tensor_tensor(acc[:, t, :], y[:, k, t, :], ws[:, k, t:t + 1], base, ALU.mult,
                                                            ALU.add)
                        last.then_inc(step.sem, 1)
                        n += 1
                        dve.wait_ge(*step(n))
                    ab, xb = acc[:, b * Q:b * Q + Q, :], core.x[:, b * Q:b * Q + Q, :]
                    dve.tensor_tensor(ab, ab, core.gate[:, 3, 1, b, :].unsqueeze(1).broadcast_to([P, Q, P]), ALU.mult)\
                       .then_inc(step.sem, 1)
                    n += 1
                    dve.wait_ge(*step(n))
                    dve.tensor_tensor(xb, xb, ab, ALU.add)
    stage_ends(core, loaded=48, gu_full=B, silu_made=B, hh_made=B, shared_full=B, mix_step=3 * B,
             **{f"gathered{b}": 32 * Q for b in range(B)})


INS = {
    "x": lambda a: a["L0_attn_x"],
    "ct": lambda a: np.concatenate([a[f"L{l}_c"] for l in range(LAYERS)], 0).T,
    "wmod": lambda a: np.stack([a[f"L{l}_wmod"].reshape(P, 6, P) for l in range(LAYERS)], 1),
    "l0_wq": lambda a: by_groups(a["L0_attn_Wq"], 8),
    "l0_wk": lambda a: by_groups(a["L0_attn_Wk"], 8),
    "l0_wv": lambda a: a["L0_attn_Wv"],
    "l0_wo": lambda a: a["L0_attn_Wo"].reshape(8, P, P),
    "l0_bo": lambda a: a["L0_attn_bo"].reshape(1, P),
    "l0_gw": lambda a: a["L0_ffn_gate_w"],
    "l0_gb": lambda a: a["L0_ffn_gate_b"].reshape(1, 8),
    "l0_w1": lambda a: a["L0_ffn_W1"],
    "l0_b1": lambda a: a["L0_ffn_b1"].reshape(8, 4, P).transpose(0, 2, 1),
    "l0_w2": lambda a: by_rows(a["L0_ffn_W2"], 4),
    "l0_b2": lambda a: a["L0_ffn_b2"],
    "l1_wq": lambda a: spread_heads(a["L1_attn_Wq"]),
    "l1_bq": lambda a: spread_heads(a["L1_attn_bq"].reshape(1, P))[:, 0, :].T,
    "l1_wkd": lambda a: a["L1_attn_Wkd"].reshape(P, 2, 32).transpose(1, 0, 2),
    "l1_bkd": lambda a: a["L1_attn_bkd"].reshape(2, 32).T,
    "l1_wku": lambda a: spread_heads(a["L1_attn_Wku"][:, :P]),
    "l1_minus": lambda a: low_blocks(),
    "l1_bku": lambda a: spread_heads(a["L1_attn_bku"][:P].reshape(1, P))[:, 0, :].T,
    "l1_wv": lambda a: a["L1_attn_Wku"][:, P:],
    "l1_bv": lambda a: a["L1_attn_bku"][P:].reshape(1, P),
    "l1_wo": lambda a: a["L1_attn_Wo"].reshape(4, 32, P),
    "l1_bo": lambda a: a["L1_attn_bo"].reshape(1, P),
    "l1_gw": lambda a: a["L1_ffn_gate_w"].T,
    "l1_w1": lambda a: two_parts(a["L1_ffn_w1"], a["L1_ffn_w3"], 4),
    "l1_w2": lambda a: by_rows(a["L1_ffn_w2"].transpose(0, 2, 1), 4),
    "l2_nw": lambda a: a["L2_attn_norm_w"].reshape(P, 1),
    "l2_win": lambda a: a["L2_attn_W_in"],
    "l2_buz": lambda a: a["L2_attn_b_in"][:P].reshape(P, 1),
    "l2_bg": lambda a: a["L2_attn_b_in"][P:].reshape(64, 1),
    "l2_wx": lambda a: a["L2_attn_W_x"],
    "l2_wdt": lambda a: a["L2_attn_W_dt"],
    "l2_bxdt": lambda a: np.concatenate([a["L2_attn_b_x"], a["L2_attn_b_dt"]])[:, None],
    "l2_wout": lambda a: a["L2_attn_W_out"],
    "l2_bout": lambda a: a["L2_attn_b_out"].reshape(1, P),
    "l2_gw": lambda a: a["L2_ffn_gate_w"].T,
    "l2_w1": lambda a: two_parts(
        np.concatenate([a["L2_ffn_fc1_w"][:, P:], a["L2_ffn_s_fc1_w"][2 * P:].reshape(2, P, P)]),
        np.concatenate([a["L2_ffn_fc1_w"][:, :P], a["L2_ffn_s_fc1_w"][:2 * P].reshape(2, P, P)]), 1),
    "l2_b1": lambda a: np.stack([
        np.concatenate([a["L2_ffn_fc1_b"][:, P:], a["L2_ffn_s_fc1_b"][2 * P:].reshape(2, P)]),
        np.concatenate([a["L2_ffn_fc1_b"][:, :P], a["L2_ffn_s_fc1_b"][:2 * P].reshape(2, P)])], 2),
    "l2_mult": lambda a: np.concatenate([a["L2_ffn_geglu_mult"], a["L2_ffn_s_geglu_mult"].reshape(2, P)])[:, :, None],
    "l2_w2": lambda a: np.concatenate([a["L2_ffn_fc2_w"].transpose(0, 2, 1),
                                       a["L2_ffn_s_fc2_w"].T.reshape(2, P, P)]),
    "l2_b2": lambda a: np.concatenate([a["L2_ffn_fc2_b"], a["L2_ffn_s_fc2_b"].reshape(1, P),
                                       np.zeros((1, P), np.float32)]),
    "l3_wq": lambda a: by_groups(a["L3_attn_Wq"], 8),
    "l3_wk": lambda a: by_groups(a["L3_attn_Wk"], 8),
    "l3_wv": lambda a: a["L3_attn_Wv"],
    "l3_wo": lambda a: a["L3_attn_Wo"].reshape(8, P, P),
    "l3_bo": lambda a: a["L3_attn_bo"].reshape(1, P),
    "l3_rw": lambda a: a["L3_ffn_rms_w"].reshape(P, 1),
    "l3_gw": lambda a: a["L3_ffn_gate_w"].T,
    "l3_w13": lambda a: a["L3_ffn_w13"],
    "l3_w2": lambda a: a["L3_ffn_w2"],
    "l3_sg": lambda a: a["L3_ffn_sw_gate"],
    "l3_su": lambda a: a["L3_ffn_sw_up"],
    "l3_sd": lambda a: a["L3_ffn_sw_down"],
}


def by_groups(w, groups):
    return w.reshape(w.shape[0], groups, -1).transpose(1, 0, 2)


def by_rows(w, blocks):
    e, f, n = w.shape
    return w.reshape(e, blocks, f // blocks, n).transpose(0, 2, 1, 3).reshape(e, f // blocks, blocks * n)


def two_parts(first, second, blocks):
    e, f, k = first.shape
    both = np.stack([w.reshape(e, blocks, f // blocks, k) for w in (first, second)], 2)
    return both.transpose(0, 4, 1, 2, 3).reshape(e, k, 2 * f)


def spread_heads(w):
    k = w.shape[0]
    out = np.repeat(w.reshape(k, 4, 4, 1, 8), 4, 3)
    return out.transpose(1, 0, 2, 3, 4).reshape(4, k, P)


def low_blocks():
    block = np.arange(P) // 8 % 4
    return np.stack([-(block % 2), -(block // 2)], 1).astype(np.float32)


@contextmanager
def moe_tensors(core, layer, E, w1, w2, mult=None):
    nc = core.nc
    with nc.sbuf_tensor(f"g{layer}", [P, E, NT], F32) as core.g, \
         nc.sbuf_tensor(f"g_t{layer}", [P, T], F32) as core.g_t, \
         nc.sbuf_tensor(f"b2_{layer}", [P, P], F32) as core.b2, \
         ExitStack() as ctx:
        yield ExpertWeights(core, ctx, layer, w1, w2, mult)


def build(nc, d, out, stages=None):
    on = lambda s: stages is None or s in stages
    with ExitStack() as ctx:
        core = Core(nc, ctx)
        setup(core, d["x"], d["ct"], d["wmod"])
        if on("a0"):
            layer_norm(core, 0, 0)
            with nc.sbuf_tensor("v0", [P, NT, v_width(64)], F32) as core.v, \
                 nc.sbuf_tensor("h_high0", [P, T], F32R) as core.h_hi, \
                 nc.sbuf_tensor("h_low0", [P, T], F32R) as core.h_lo:
                values_by_parts(core, "l0", d["l0_wv"], HEADS * 64)
                attention(core, 0, 8, 64, False, core.h, d["l0_wq"], d["l0_wk"], d["l0_wo"], d["l0_bo"],
                          q_scale=64 ** -0.5)
        if on("f0"):
            layer_norm(core, 0, 1)
            with moe_tensors(core, 0, 8, d["l0_w1"], d["l0_w2"]) as weights:
                route(core, 0, 8, d["l0_gw"], d["l0_gb"], "softmax", weights=weights)
                gate_rows(core, 0, 8, d["l0_b2"])
                experts(core, 0, 8, P, 4, ACT.Silu, weights, b1=d["l0_b1"])
        if on("a1"):
            layer_norm(core, 1, 0)
            with nc.sbuf_tensor("v1", [P, NT, v_width(8)], F32) as core.v, nc.sbuf_tensor("lat", [P, T], F32) as lat:
                latents(core, d["l1_wkd"], d["l1_bkd"], lat)
                values(core, "l1", lat, d["l1_wv"], d["l1_bv"], P)
                attention(core, 1, 4, 8, True, lat, d["l1_wq"], d["l1_wku"], d["l1_wo"], d["l1_bo"],
                          q_bias=d["l1_bq"], k_bias=d["l1_bku"], k_scale=8 ** -0.5, minus=d["l1_minus"])
        if on("f1"):
            layer_norm(core, 1, 1)
            with moe_tensors(core, 1, 8, d["l1_w1"], d["l1_w2"]) as weights:
                route(core, 1, 8, d["l1_gw"], None, "jitter", weights=weights)
                gate_rows(core, 1, 8, None)
                experts(core, 1, 8, 112, 4, ACT.Silu, weights, biased=False)
        if on("a2"):
            layer_norm(core, 2, 0)
            with nc.sbuf_tensor("xn2", [P, T], F32) as xn, nc.sbuf_tensor("xnt2", [P, NT, P], F32) as xn_tok:
                rms_norm(core, "l2", 2, 0, 1e-8, d["l2_nw"], xn_tok, xn)
                gated_scan(core, 2, xn, d["l2_win"], d["l2_buz"], d["l2_bg"], d["l2_wx"], d["l2_wdt"], d["l2_bxdt"], d["l2_wout"],
                           d["l2_bout"])
        if on("f2"):
            layer_norm(core, 2, 1)
            with moe_tensors(core, 2, 17, d["l2_w1"], d["l2_w2"], d["l2_mult"]) as weights:
                route(core, 2, 15, d["l2_gw"], None, "renormed", weights=weights)
                gate_rows(core, 2, 17, d["l2_b2"])
                experts(core, 2, 17, P, 1, ACT.Gelu, weights, b1=d["l2_b1"])
        if on("a3"):
            layer_norm(core, 3, 0)
            with nc.sbuf_tensor("v3", [P, NT, v_width(64)], F32) as core.v, \
                 nc.sbuf_tensor("h_high3", [P, T], F32R) as core.h_hi, \
                 nc.sbuf_tensor("h_low3", [P, T], F32R) as core.h_lo:
                values_by_parts(core, "l3", d["l3_wv"], HEADS * 64)
                attention(core, 3, 8, 64, True, core.h, d["l3_wq"], d["l3_wk"], d["l3_wo"], d["l3_bo"],
                          q_scale=64 ** -0.5)
        if on("f3"):
            layer_norm(core, 3, 1)
            with ExitStack() as half:
                sb = lambda name, shape, dt=F32: half.enter_context(nc.sbuf_tensor(name, shape, dt))
                xn, xn_tok = sb("xn3", [P, T]), sb("xnt3", [P, NT, P])
                hot, ws, idx_f = sb("hot3", [P, 2, NT, L3_E]), sb("ws3", [P, 2, NT]), sb("idx3", [P, NT, 8])
                slot = sb("slot3", [P, 2, NT], U32)
                y = sb("slot_results", [P, 2, NT, P])
                rms_norm(core, "l3", 3, 1, 1e-6, d["l3_rw"], xn_tok, xn)
                route(core, 3, L3_E, d["l3_gw"], None, "softmax", source=xn, chosen=(hot, ws, idx_f))
                dispatch(core, hot, ws, idx_f, slot, xn_tok)
                slot_experts(core, d["l3_rw"], d["l3_w13"], d["l3_w2"], y)
                combine(core, xn, ws, slot, y, d["l3_sg"], d["l3_su"], d["l3_sd"])
        store(core, out)


def store(core, out):
    nc = core.nc
    stored = signal(core, "stored")
    with nc.Block() as block:

        @block.sync
        def _(sp):
            sp.dma_start(out.rearrange("b (q p) d -> p (b q) d", p=P), core.x[:]).then_inc(stored.sem, 16)
            sp.wait_ge(*stored(16))


def kernel(**inputs):
    import concourse.bacc as bacc
    from concourse.bass_utils import run_bass_kernel_spmd

    nc = bacc.Bacc("TRN2", target_bir_lowering=False, num_devices=1)
    arrays, d = {}, {}
    for name, layout in INS.items():
        arrays[name] = np.ascontiguousarray(layout(inputs))
        d[name] = nc.dram_tensor(name, arrays[name].shape, F32, kind="ExternalInput").ap()
    out = nc.dram_tensor("out", (B, S, P), F32, kind="ExternalOutput").ap()
    build(nc, d, out)
    r = run_bass_kernel_spmd(nc, [arrays], core_ids=[0])
    return r.results[0]["out"]
```
